# Optimizing a Trainium2 kernel written in Bass

```python
import numpy as np
import jax
import jax.numpy as jnp

def _softmax(x, axis=-1):
    return jax.nn.softmax(x, axis=axis)

def _gelu(x):
    return jax.nn.gelu(x, approximate=True)

def _silu(x):
    return jax.nn.silu(x)

def _sigmoid(x):
    return jax.nn.sigmoid(x)

def _layernorm(x, axis=-1, eps=1e-05):
    m = jnp.mean(x, axis=axis, keepdims=True)
    v = jnp.var(x, axis=axis, keepdims=True)
    return (x - m) / jnp.sqrt(v + eps)

def _scatter_add(tgt, idx, src, axis=0):
    return tgt.at[idx].add(src)

def _segment_sum(src, seg, n):
    return jax.ops.segment_sum(src, seg, n)
kernel_name = 'mk_seq_postln_d2_jaxref_r4_0d5f97'

def setup_inputs(seed: int=0):
    np.random.seed(seed)
    _w = jnp.asarray

    def _L0_attn_setup():
        import jax, jax.numpy as jnp
        import numpy as np
        B, S, D, H = (2, 512, 256, 16)
        HD = D // H
        key = jax.random.key(seed)
        ks = jax.random.split(key, 5)
        return {'x': jax.random.normal(ks[0], (B, S, D), dtype=jnp.float32), 'qkv_w': jax.random.normal(ks[1], (3 * D, D), dtype=jnp.float32) * (1.0 / np.sqrt(D)), 'qkv_b': jax.random.normal(ks[2], (3 * D,), dtype=jnp.float32) * 0.02, 'proj_w': jax.random.normal(ks[3], (D, D), dtype=jnp.float32) * (1.0 / np.sqrt(D)), 'proj_b': jax.random.normal(ks[4], (D,), dtype=jnp.float32) * 0.02}
    _L0_attn_in = _L0_attn_setup()

    def _L0_ffn_setup():
        import jax, jax.numpy as jnp
        import numpy as np
        DIM = 256
        DEPTH = 2
        HEADS = 8
        DIM_HEAD = 64
        WINDOW = 128
        INNER = HEADS * DIM_HEAD
        HID = int(DIM * 4 * 2 / 3)
        B, N = (2, 2048)
        QK_SCALE = 8.0

        def shift_token(t):
            t1, t2 = jnp.split(t, 2, axis=-1)
            t2 = jnp.pad(t2, ((0, 0), (1, 0), (0, 0)))[:, :-1]
            return jnp.concatenate([t1, t2], axis=-1)

        def l2norm(t):
            return t / jnp.clip(jnp.linalg.norm(t, axis=-1, keepdims=True), 1e-12)

        def rotate_half(x):
            x1, x2 = jnp.split(x, 2, axis=-1)
            return jnp.concatenate([-x2, x1], axis=-1)

        def rotary_xpos(q, k):
            n = q.shape[-2]
            half_idx = jnp.arange(0, DIM_HEAD, 2, dtype=jnp.float32)
            inv_freq = 1.0 / 10000.0 ** (half_idx / DIM_HEAD)
            t = jnp.arange(n, dtype=jnp.float32)
            freqs = t[:, None] * inv_freq[None, :]
            freqs = jnp.concatenate([freqs, freqs], axis=-1)
            base = (half_idx + 0.4 * DIM_HEAD) / (1.4 * DIM_HEAD)
            power = (t - n // 2) / float(WINDOW // 2)
            scale = base[None, :] ** power[:, None]
            scale = jnp.concatenate([scale, scale], axis=-1)
            cos, sin = (jnp.cos(freqs), jnp.sin(freqs))
            q = q * cos * scale + rotate_half(q) * sin * scale
            k = k * cos / scale + rotate_half(k) * sin / scale
            return (q, k)

        def local_attention(q, k, v):
            b, h, n, d = q.shape
            w = n // WINDOW
            bq = q.reshape(b, h, w, WINDOW, d) * QK_SCALE
            bk = k.reshape(b, h, w, WINDOW, d)
            bv = v.reshape(b, h, w, WINDOW, d)

            def look_around(t):
                p = jnp.pad(t, ((0, 0), (0, 0), (1, 0), (0, 0), (0, 0)))
                return jnp.concatenate([p[:, :, :w], p[:, :, 1:]], axis=3)
            bk, bv = (look_around(bk), look_around(bv))
            bt = jnp.arange(n).reshape(w, WINDOW)
            btp = jnp.pad(bt, ((1, 0), (0, 0)), constant_values=-1)
            btk = jnp.concatenate([btp[:w], btp[1:]], axis=1)
            sim = jnp.einsum('bhwid,bhwjd->bhwij', bq, bk)
            i = bt[:, :, None]
            j = btk[:, None, :]
            mask = (i < j) | (i > j + WINDOW) | (j == -1)
            sim = jnp.where(mask, -jnp.finfo(sim.dtype).max, sim)
            attn = jax.nn.softmax(sim, axis=-1)
            out = jnp.einsum('bhwij,bhwjd->bhwid', attn, bv)
            return out.reshape(b, h, n, d)

        def _layer(x, wqkv, qs, ksc, wo, lg, lb, w1, b1, w2, b2):
            b, n, _ = x.shape
            h = shift_token(x)
            qkv = h @ wqkv
            q, k, v = jnp.split(qkv, 3, axis=-1)
            to_heads = lambda t: t.reshape(b, n, HEADS, DIM_HEAD).transpose(0, 2, 1, 3)
            q, k, v = (to_heads(q), to_heads(k), to_heads(v))
            q = l2norm(q) * qs
            k = l2norm(k) * ksc
            q, k = rotary_xpos(q, k)
            o = local_attention(q, k, v)
            o = o.transpose(0, 2, 1, 3).reshape(b, n, INNER)
            x = x + o @ wo
            h = shift_token(x)
            mu = h.mean(-1, keepdims=True)
            var = h.var(-1, keepdims=True)
            h = (h - mu) / jnp.sqrt(var + 1e-05) * lg + lb
            h = h @ w1 + b1
            a, g = jnp.split(h, 2, axis=-1)
            h = a * jax.nn.gelu(g, approximate=False)
            x = x + h @ w2 + b2
            return x
        key = jax.random.key(seed)
        ks = jax.random.split(key, 6)
        return {'x': jax.random.normal(ks[0], (B, N, DIM), jnp.float32), 'wqkv': jax.random.normal(ks[1], (DEPTH, DIM, 3 * INNER), jnp.float32) * 0.02, 'q_scale': jnp.ones((DEPTH, DIM_HEAD), jnp.float32), 'k_scale': jnp.ones((DEPTH, DIM_HEAD), jnp.float32), 'wo': jax.random.normal(ks[2], (DEPTH, INNER, DIM), jnp.float32) * 0.02, 'ln_g': jnp.ones((DEPTH, DIM), jnp.float32), 'ln_b': jnp.zeros((DEPTH, DIM), jnp.float32), 'w1': jax.random.normal(ks[3], (DEPTH, DIM, 2 * HID), jnp.float32) * 0.02, 'b1': jnp.zeros((DEPTH, 2 * HID), jnp.float32), 'w2': jax.random.normal(ks[4], (DEPTH, HID, DIM), jnp.float32) * 0.02, 'b2': jnp.zeros((DEPTH, DIM), jnp.float32)}
    _L0_ffn_in = _L0_ffn_setup()

    def _L1_attn_setup():
        import jax, jax.numpy as jnp
        import numpy as np
        B, L, D = (8, 1024, 256)
        H, f, K = (2, 128, 16)
        d = H * f
        TTT_BASE_LR = 1.0

        def _ln(x, g, b, eps=1e-06):
            mu = x.mean(-1, keepdims=True)
            var = ((x - mu) ** 2).mean(-1, keepdims=True)
            return g * (x - mu) * jax.lax.rsqrt(var + eps) + b

        def _ln_fused_l2_bwd(x, target, g, b, eps=1e-06):
            Dh = x.shape[-1]
            mu = x.mean(-1, keepdims=True)
            var = ((x - mu) ** 2).mean(-1, keepdims=True)
            std = jnp.sqrt(var + eps)
            xh = (x - mu) / std
            gy = (g * xh + b - target) * g
            return (Dh * gy - gy.sum(-1, keepdims=True) - xh * (gy * xh).sum(-1, keepdims=True)) / (Dh * std)

        def _ttt_linear(h, wq, wk, wv, wo, W1, b1, ttt_ln_w, ttt_ln_b, lr_w, lr_b, tok_idx, post_w, post_b):
            Bb, Ll, dm = h.shape
            nm = Ll // K

            def heads(w):
                return (h @ w).reshape(Bb, nm, K, H, f).transpose(0, 3, 1, 2, 4)
            XQ, XK, XV = (heads(wq), heads(wk), heads(wv))
            Xm = h.reshape(Bb, nm, K, dm)
            ttt_lr = jax.nn.sigmoid(jnp.einsum('bnkc,hoc->bhnko', Xm, lr_w) + lr_b[None, :, None, None, None])
            ttt_lr_eta = TTT_BASE_LR * ttt_lr.transpose(0, 1, 2, 4, 3) / f
            token_idx = jnp.maximum(1.0 / jnp.arange(1, K + 1, dtype=jnp.float32) + tok_idx, 0.0)
            eta = token_idx[None, None, None, :, None] * ttt_lr_eta
            gw = ttt_ln_w[:, None, :]
            gb = ttt_ln_b[:, None, :]

            def step(carry, inp):
                W1c, b1c = carry
                xq, xk, xv, et = inp
                Z1 = xk @ W1c + b1c
                grad = _ln_fused_l2_bwd(Z1, xv - xk, gw, gb)
                Attn = jnp.tril(xq @ jnp.swapaxes(xk, -1, -2))
                b1_bar = b1c - jnp.tril(et) @ grad
                Z1_bar = xq @ W1c - et * Attn @ grad + b1_bar
                last_eta = et[:, :, -1, :, None]
                W1n = W1c - jnp.swapaxes(last_eta * xk, -1, -2) @ grad
                b1n = b1c - (last_eta * grad).sum(-2, keepdims=True)
                return ((W1n, b1n), xq + _ln(Z1_bar, gw, gb))
            carry0 = (jnp.broadcast_to(W1[None], (Bb, H, f, f)), jnp.broadcast_to(b1[None], (Bb, H, 1, f)))
            xs = tuple((a.transpose(2, 0, 1, 3, 4) for a in (XQ, XK, XV, eta)))
            _, outs = jax.lax.scan(step, carry0, xs)
            out = outs.transpose(1, 0, 3, 2, 4).reshape(Bb, Ll, dm)
            out = _ln(out, post_w, post_b, eps=1e-05)
            return out @ wo
        key = jax.random.key(seed)
        ks = jax.random.split(key, 16)
        s = 0.02
        return {'x': jax.random.normal(ks[0], (B, L, D), jnp.float32), 'down_w': jax.random.normal(ks[1], (D, d), jnp.float32) * s, 'down_b': jnp.zeros((d,), jnp.float32), 'up_w': jax.random.normal(ks[2], (d, D), jnp.float32) * s, 'up_b': jnp.zeros((D,), jnp.float32), 'wq': jax.random.normal(ks[3], (d, d), jnp.float32) * s, 'wk': jax.random.normal(ks[4], (d, d), jnp.float32) * s, 'wv': jax.random.normal(ks[5], (d, d), jnp.float32) * s, 'wo': jax.random.normal(ks[6], (d, d), jnp.float32) * s, 'W1': jax.random.normal(ks[7], (H, f, f), jnp.float32) * s, 'b1': jnp.zeros((H, 1, f), jnp.float32), 'ttt_ln_w': jnp.ones((H, f), jnp.float32), 'ttt_ln_b': jnp.zeros((H, f), jnp.float32), 'lr_w': jax.random.normal(ks[8], (H, 1, d), jnp.float32) * s, 'lr_b': jnp.zeros((H,), jnp.float32), 'tok_idx': jnp.zeros((K,), jnp.float32), 'post_w': jnp.ones((d,), jnp.float32), 'post_b': jnp.zeros((d,), jnp.float32), 'ln_w': jnp.ones((d,), jnp.float32), 'ln_b': jnp.zeros((d,), jnp.float32)}
    _L1_attn_in = _L1_attn_setup()

    def _L1_ffn_setup():
        import jax, jax.numpy as jnp
        import numpy as np
        key = jax.random.key(seed)
        k1, k2, k3, k4, k5 = jax.random.split(key, 5)
        d_in, d_out, r = (256, 256, 32)
        x = jax.random.normal(k1, (8, 2048, d_in), dtype=jnp.float32)
        W = jax.random.normal(k2, (d_out, d_in), dtype=jnp.float32) * (1.0 / np.sqrt(d_in))
        b = jax.random.normal(k3, (d_out,), dtype=jnp.float32) * 0.01
        V_r = jax.random.normal(k4, (d_in, r), dtype=jnp.float32) * (1.0 / np.sqrt(d_in))
        C = jax.random.normal(k5, (d_out, r), dtype=jnp.float32) * (1.0 / np.sqrt(r))
        return {'x': x, 'W': W, 'b': b, 'V_r': V_r, 'C': C}
    _L1_ffn_in = _L1_ffn_setup()
    _d = {'L0_attn_x': _L0_attn_in['x'], 'L0_attn_qkv_w': _L0_attn_in['qkv_w'], 'L0_attn_qkv_b': _L0_attn_in['qkv_b'], 'L0_attn_proj_w': _L0_attn_in['proj_w'], 'L0_attn_proj_b': _L0_attn_in['proj_b'], 'L0_ffn_wqkv': _L0_ffn_in['wqkv'], 'L0_ffn_q_scale': _L0_ffn_in['q_scale'], 'L0_ffn_k_scale': _L0_ffn_in['k_scale'], 'L0_ffn_wo': _L0_ffn_in['wo'], 'L0_ffn_ln_g': _L0_ffn_in['ln_g'], 'L0_ffn_ln_b': _L0_ffn_in['ln_b'], 'L0_ffn_w1': _L0_ffn_in['w1'], 'L0_ffn_b1': _L0_ffn_in['b1'], 'L0_ffn_w2': _L0_ffn_in['w2'], 'L0_ffn_b2': _L0_ffn_in['b2'], 'L1_attn_down_w': _L1_attn_in['down_w'], 'L1_attn_down_b': _L1_attn_in['down_b'], 'L1_attn_up_w': _L1_attn_in['up_w'], 'L1_attn_up_b': _L1_attn_in['up_b'], 'L1_attn_wq': _L1_attn_in['wq'], 'L1_attn_wk': _L1_attn_in['wk'], 'L1_attn_wv': _L1_attn_in['wv'], 'L1_attn_wo': _L1_attn_in['wo'], 'L1_attn_W1': _L1_attn_in['W1'], 'L1_attn_b1': _L1_attn_in['b1'], 'L1_attn_ttt_ln_w': _L1_attn_in['ttt_ln_w'], 'L1_attn_ttt_ln_b': _L1_attn_in['ttt_ln_b'], 'L1_attn_lr_w': _L1_attn_in['lr_w'], 'L1_attn_lr_b': _L1_attn_in['lr_b'], 'L1_attn_tok_idx': _L1_attn_in['tok_idx'], 'L1_attn_post_w': _L1_attn_in['post_w'], 'L1_attn_post_b': _L1_attn_in['post_b'], 'L1_attn_ln_w': _L1_attn_in['ln_w'], 'L1_attn_ln_b': _L1_attn_in['ln_b'], 'L1_ffn_W': _L1_ffn_in['W'], 'L1_ffn_b': _L1_ffn_in['b'], 'L1_ffn_V_r': _L1_ffn_in['V_r'], 'L1_ffn_C': _L1_ffn_in['C']}
    _x0 = _d['L0_attn_x']
    _d['L0_attn_x'] = jax.random.normal(jax.random.fold_in(jax.random.key(seed), 1), (8, 1024, 256), dtype=_x0.dtype)
    del _x0
    return _d

def reference(L0_attn_x, L0_attn_qkv_w, L0_attn_qkv_b, L0_attn_proj_w, L0_attn_proj_b, L0_ffn_wqkv, L0_ffn_q_scale, L0_ffn_k_scale, L0_ffn_wo, L0_ffn_ln_g, L0_ffn_ln_b, L0_ffn_w1, L0_ffn_b1, L0_ffn_w2, L0_ffn_b2, L1_attn_down_w, L1_attn_down_b, L1_attn_up_w, L1_attn_up_b, L1_attn_wq, L1_attn_wk, L1_attn_wv, L1_attn_wo, L1_attn_W1, L1_attn_b1, L1_attn_ttt_ln_w, L1_attn_ttt_ln_b, L1_attn_lr_w, L1_attn_lr_b, L1_attn_tok_idx, L1_attn_post_w, L1_attn_post_b, L1_attn_ln_w, L1_attn_ln_b, L1_ffn_W, L1_ffn_b, L1_ffn_V_r, L1_ffn_C):

    def _L0_attn_ref(x, qkv_w, qkv_b, proj_w, proj_b):
        import jax, jax.numpy as jnp
        import numpy as np
        B, S, D, H = (2, 512, 256, 16)
        HD = D // H
        b, s, d = x.shape
        qkv = jnp.einsum('bsd,ed->bse', x, qkv_w) + qkv_b
        qkv = qkv.reshape(b, s, 3, H, HD)
        q = jnp.transpose(qkv[:, :, 0], (0, 2, 1, 3))
        k = jnp.transpose(qkv[:, :, 1], (0, 2, 1, 3))
        v = jnp.transpose(qkv[:, :, 2], (0, 2, 1, 3))
        scale = 1.0 / jnp.sqrt(jnp.asarray(HD, dtype=x.dtype))
        scores = jnp.einsum('bhqe,bhke->bhqk', q, k) * scale
        attn = jax.nn.softmax(scores, axis=-1)
        out = jnp.einsum('bhqk,bhke->bhqe', attn, v)
        out = jnp.transpose(out, (0, 2, 1, 3)).reshape(b, s, d)
        out = jnp.einsum('bsd,ed->bse', out, proj_w) + proj_b
        return out

    def _L0_ffn_ref(x, wqkv, q_scale, k_scale, wo, ln_g, ln_b, w1, b1, w2, b2):
        import jax, jax.numpy as jnp
        import numpy as np
        DIM = 256
        DEPTH = 2
        HEADS = 8
        DIM_HEAD = 64
        WINDOW = 128
        INNER = HEADS * DIM_HEAD
        HID = int(DIM * 4 * 2 / 3)
        B, N = (2, 2048)
        QK_SCALE = 8.0

        def shift_token(t):
            t1, t2 = jnp.split(t, 2, axis=-1)
            t2 = jnp.pad(t2, ((0, 0), (1, 0), (0, 0)))[:, :-1]
            return jnp.concatenate([t1, t2], axis=-1)

        def l2norm(t):
            return t / jnp.clip(jnp.linalg.norm(t, axis=-1, keepdims=True), 1e-12)

        def rotate_half(x):
            x1, x2 = jnp.split(x, 2, axis=-1)
            return jnp.concatenate([-x2, x1], axis=-1)

        def rotary_xpos(q, k):
            n = q.shape[-2]
            half_idx = jnp.arange(0, DIM_HEAD, 2, dtype=jnp.float32)
            inv_freq = 1.0 / 10000.0 ** (half_idx / DIM_HEAD)
            t = jnp.arange(n, dtype=jnp.float32)
            freqs = t[:, None] * inv_freq[None, :]
            freqs = jnp.concatenate([freqs, freqs], axis=-1)
            base = (half_idx + 0.4 * DIM_HEAD) / (1.4 * DIM_HEAD)
            power = (t - n // 2) / float(WINDOW // 2)
            scale = base[None, :] ** power[:, None]
            scale = jnp.concatenate([scale, scale], axis=-1)
            cos, sin = (jnp.cos(freqs), jnp.sin(freqs))
            q = q * cos * scale + rotate_half(q) * sin * scale
            k = k * cos / scale + rotate_half(k) * sin / scale
            return (q, k)

        def local_attention(q, k, v):
            b, h, n, d = q.shape
            w = n // WINDOW
            bq = q.reshape(b, h, w, WINDOW, d) * QK_SCALE
            bk = k.reshape(b, h, w, WINDOW, d)
            bv = v.reshape(b, h, w, WINDOW, d)

            def look_around(t):
                p = jnp.pad(t, ((0, 0), (0, 0), (1, 0), (0, 0), (0, 0)))
                return jnp.concatenate([p[:, :, :w], p[:, :, 1:]], axis=3)
            bk, bv = (look_around(bk), look_around(bv))
            bt = jnp.arange(n).reshape(w, WINDOW)
            btp = jnp.pad(bt, ((1, 0), (0, 0)), constant_values=-1)
            btk = jnp.concatenate([btp[:w], btp[1:]], axis=1)
            sim = jnp.einsum('bhwid,bhwjd->bhwij', bq, bk)
            i = bt[:, :, None]
            j = btk[:, None, :]
            mask = (i < j) | (i > j + WINDOW) | (j == -1)
            sim = jnp.where(mask, -jnp.finfo(sim.dtype).max, sim)
            attn = jax.nn.softmax(sim, axis=-1)
            out = jnp.einsum('bhwij,bhwjd->bhwid', attn, bv)
            return out.reshape(b, h, n, d)

        def _layer(x, wqkv, qs, ksc, wo, lg, lb, w1, b1, w2, b2):
            b, n, _ = x.shape
            h = shift_token(x)
            qkv = h @ wqkv
            q, k, v = jnp.split(qkv, 3, axis=-1)
            to_heads = lambda t: t.reshape(b, n, HEADS, DIM_HEAD).transpose(0, 2, 1, 3)
            q, k, v = (to_heads(q), to_heads(k), to_heads(v))
            q = l2norm(q) * qs
            k = l2norm(k) * ksc
            q, k = rotary_xpos(q, k)
            o = local_attention(q, k, v)
            o = o.transpose(0, 2, 1, 3).reshape(b, n, INNER)
            x = x + o @ wo
            h = shift_token(x)
            mu = h.mean(-1, keepdims=True)
            var = h.var(-1, keepdims=True)
            h = (h - mu) / jnp.sqrt(var + 1e-05) * lg + lb
            h = h @ w1 + b1
            a, g = jnp.split(h, 2, axis=-1)
            h = a * jax.nn.gelu(g, approximate=False)
            x = x + h @ w2 + b2
            return x
        for l in range(DEPTH):
            x = _layer(x, wqkv[l], q_scale[l], k_scale[l], wo[l], ln_g[l], ln_b[l], w1[l], b1[l], w2[l], b2[l])
        return x

    def _L1_attn_ref(x, down_w, down_b, up_w, up_b, wq, wk, wv, wo, W1, b1, ttt_ln_w, ttt_ln_b, lr_w, lr_b, tok_idx, post_w, post_b, ln_w, ln_b):
        import jax, jax.numpy as jnp
        import numpy as np
        B, L, D = (8, 1024, 256)
        H, f, K = (2, 128, 16)
        d = H * f
        TTT_BASE_LR = 1.0

        def _ln(x, g, b, eps=1e-06):
            mu = x.mean(-1, keepdims=True)
            var = ((x - mu) ** 2).mean(-1, keepdims=True)
            return g * (x - mu) * jax.lax.rsqrt(var + eps) + b

        def _ln_fused_l2_bwd(x, target, g, b, eps=1e-06):
            Dh = x.shape[-1]
            mu = x.mean(-1, keepdims=True)
            var = ((x - mu) ** 2).mean(-1, keepdims=True)
            std = jnp.sqrt(var + eps)
            xh = (x - mu) / std
            gy = (g * xh + b - target) * g
            return (Dh * gy - gy.sum(-1, keepdims=True) - xh * (gy * xh).sum(-1, keepdims=True)) / (Dh * std)

        def _ttt_linear(h, wq, wk, wv, wo, W1, b1, ttt_ln_w, ttt_ln_b, lr_w, lr_b, tok_idx, post_w, post_b):
            Bb, Ll, dm = h.shape
            nm = Ll // K

            def heads(w):
                return (h @ w).reshape(Bb, nm, K, H, f).transpose(0, 3, 1, 2, 4)
            XQ, XK, XV = (heads(wq), heads(wk), heads(wv))
            Xm = h.reshape(Bb, nm, K, dm)
            ttt_lr = jax.nn.sigmoid(jnp.einsum('bnkc,hoc->bhnko', Xm, lr_w) + lr_b[None, :, None, None, None])
            ttt_lr_eta = TTT_BASE_LR * ttt_lr.transpose(0, 1, 2, 4, 3) / f
            token_idx = jnp.maximum(1.0 / jnp.arange(1, K + 1, dtype=jnp.float32) + tok_idx, 0.0)
            eta = token_idx[None, None, None, :, None] * ttt_lr_eta
            gw = ttt_ln_w[:, None, :]
            gb = ttt_ln_b[:, None, :]

            def step(carry, inp):
                W1c, b1c = carry
                xq, xk, xv, et = inp
                Z1 = xk @ W1c + b1c
                grad = _ln_fused_l2_bwd(Z1, xv - xk, gw, gb)
                Attn = jnp.tril(xq @ jnp.swapaxes(xk, -1, -2))
                b1_bar = b1c - jnp.tril(et) @ grad
                Z1_bar = xq @ W1c - et * Attn @ grad + b1_bar
                last_eta = et[:, :, -1, :, None]
                W1n = W1c - jnp.swapaxes(last_eta * xk, -1, -2) @ grad
                b1n = b1c - (last_eta * grad).sum(-2, keepdims=True)
                return ((W1n, b1n), xq + _ln(Z1_bar, gw, gb))
            carry0 = (jnp.broadcast_to(W1[None], (Bb, H, f, f)), jnp.broadcast_to(b1[None], (Bb, H, 1, f)))
            xs = tuple((a.transpose(2, 0, 1, 3, 4) for a in (XQ, XK, XV, eta)))
            _, outs = jax.lax.scan(step, carry0, xs)
            out = outs.transpose(1, 0, 3, 2, 4).reshape(Bb, Ll, dm)
            out = _ln(out, post_w, post_b, eps=1e-05)
            return out @ wo
        h = jax.nn.silu(x @ down_w + down_b)
        h = _ttt_linear(h, wq, wk, wv, wo, W1, b1, ttt_ln_w, ttt_ln_b, lr_w, lr_b, tok_idx, post_w, post_b)
        h = _ln(h, ln_w, ln_b, eps=1e-05)
        return h @ up_w + up_b

    def _L1_ffn_ref(x, W, b, V_r, C):
        import jax, jax.numpy as jnp
        import numpy as np
        base = jnp.einsum('bsd,od->bso', x, W) + b
        correction = jnp.einsum('bsr,or->bso', jnp.einsum('bsd,dr->bsr', x, V_r), C)
        return base + correction
    x = L0_attn_x
    x = _layernorm(x + _L0_attn_ref(x, L0_attn_qkv_w, L0_attn_qkv_b, L0_attn_proj_w, L0_attn_proj_b), axis=-1)
    x = _layernorm(x + _L0_ffn_ref(x, L0_ffn_wqkv, L0_ffn_q_scale, L0_ffn_k_scale, L0_ffn_wo, L0_ffn_ln_g, L0_ffn_ln_b, L0_ffn_w1, L0_ffn_b1, L0_ffn_w2, L0_ffn_b2), axis=-1)
    x = _layernorm(x + _L1_attn_ref(x, L1_attn_down_w, L1_attn_down_b, L1_attn_up_w, L1_attn_up_b, L1_attn_wq, L1_attn_wk, L1_attn_wv, L1_attn_wo, L1_attn_W1, L1_attn_b1, L1_attn_ttt_ln_w, L1_attn_ttt_ln_b, L1_attn_lr_w, L1_attn_lr_b, L1_attn_tok_idx, L1_attn_post_w, L1_attn_post_b, L1_attn_ln_w, L1_attn_ln_b), axis=-1)
    x = _layernorm(x + _L1_ffn_ref(x, L1_ffn_W, L1_ffn_b, L1_ffn_V_r, L1_ffn_C), axis=-1)
    return x

_drawn_inputs = setup_inputs


def setup_inputs(seed=0):
    import zlib

    import numpy as np

    out = dict(_drawn_inputs(seed))
    spreads = {'L0_ffn_q_scale': (1.0, 0.6),
     'L0_ffn_k_scale': (1.0, 0.6),
     'L0_ffn_ln_g': (1.0, 0.6),
     'L0_ffn_ln_b': (0.0, 0.8),
     'L0_ffn_b1': (0.0, 0.8),
     'L0_ffn_b2': (0.0, 0.1),
     'L1_attn_down_b': (0.0, 0.1),
     'L1_attn_up_b': (0.0, 0.1),
     'L1_attn_b1': (0.0, 0.1),
     'L1_attn_ttt_ln_w': (1.0, 0.2),
     'L1_attn_ttt_ln_b': (0.0, 0.1),
     'L1_attn_lr_b': (0.0, 2.0),
     'L1_attn_tok_idx': (0.0, 0.364),
     'L1_attn_post_w': (1.0, 0.2),
     'L1_attn_post_b': (0.0, 0.1),
     'L1_attn_ln_w': (1.0, 0.2),
     'L1_attn_ln_b': (0.0, 0.28)}
    factors = {'L0_attn_qkv_b': 2.706,
     'L0_attn_proj_b': 3.23,
     'L0_ffn_wqkv': 3.386,
     'L0_ffn_wo': 3.338,
     'L1_attn_lr_w': 47.881,
     'L1_ffn_b': 8.0}
    for name, (base, spread) in spreads.items():
        noise = np.random.default_rng([zlib.crc32(name.encode()), seed]).standard_normal(out[name].shape)
        drawn = base * np.exp(spread * noise) if base else spread * noise
        out[name] = jnp.asarray(drawn.astype(out[name].dtype))
    for name, factor in factors.items():
        out[name] = (out[name] * factor).astype(out[name].dtype)
    return out
```

```python
from contextlib import ExitStack

import numpy as np

import concourse.bass as bass
from concourse import mybir

F32 = mybir.dt.float32
BF16 = mybir.dt.bfloat16
ALU = mybir.AluOpType
ACT = mybir.ActivationFunctionType
AXX = mybir.AxisListType.X

P = 128
B, L, D = 8, 1024, 256
NT = B * L // P
CH = 512
NC = B * L // CH
TPC = CH // P
DC = D // P


class Stage:

    def __init__(self, nc, name):
        self.nc, self.name, self.stack, self.sems = nc, name, ExitStack(), []

    def __enter__(self):
        self.stack.__enter__()
        return self

    def __exit__(self, *what):
        left = self.stack.__exit__(*what)
        self.nc.clear_and_free_semaphores(self.sems)
        self.nc.all_engine_barrier()
        return left

    def sb(self, name, shape, dt=F32):
        return self.stack.enter_context(self.nc.sbuf_tensor(f"{self.name}_{name}", list(shape), dt))

    def ps(self, name, shape, dt=F32):
        return self.stack.enter_context(self.nc.psum_tensor(f"{self.name}_{name}", list(shape), dt))

    def sem(self, name):
        self.sems.append(self.nc.alloc_semaphore(f"{self.name}_{name}"))
        return self.sems[-1]

    def block(self):
        return self.stack.enter_context(self.nc.Block())


def pipelined(eng, n, steps, peel=0):
    deepest = max(lag for _, lag in steps)
    first = max(deepest + deepest % 2, 2)
    last = n - peel

    def peeled(s):
        for fn, lag in steps:
            t = s - lag
            if 0 <= t < n:
                fn(t, t // 2, t % 2)

    for s in range(min(first, last)):
        peeled(s)
    if last > first:
        with eng.Fori(0, (last - first) // 2) as i:
            for u in range(2):
                for fn, lag in steps:
                    off = first + u - lag
                    fn(i * 2 + off, i + off // 2, off % 2)
    for s in range(last, n + deepest):
        peeled(s)
HA, EA = 16, 16
QUADS = HA // 4
NI = B * QUADS
KT = L // P
Q_PART = [0, 0, 0, 1, 1, 2]
K_PART = [0, 1, 2, 0, 1, 0]
ROWS = EA * len(Q_PART)
SHIFT_ROWS = 3


def attn_project(nc, xT, wqkvT, qkv_b_col, vb_row, parts, values):
    with Stage(nc, "pj") as st:
        w = st.sb("w", [P, DC, 3 * D])
        bcol = st.sb("bcol", [P, 4])
        vb = st.sb("vb", [P, D])
        x = [st.sb(f"x{i}", [P, DC, CH]) for i in range(2)]
        full = st.sb("full", [P, 4, CH])
        rest = st.sb("rest", [P, 4, CH])
        split = [st.sb(f"split{i}", [P, 3, 4, CH], BF16) for i in range(2)]
        v = [st.sb(f"v{i}", [P, TPC, HA, 2 * EA]) for i in range(2)]
        pqk = [st.ps(f"pqk{m}", [P, CH]) for m in range(4)]
        pv = [st.ps(f"pv{j}", [P, 2, D]) for j in range(2)]
        w_in = st.sem("w_in")
        x_in = [st.sem(f"x_in{i}") for i in range(2)]
        x_free = st.sem("x_free")
        qk_mm = st.sem("qk_mm")
        v_mm = st.sem("v_mm")
        biased = st.sem("biased")
        part1 = st.sem("part1")
        dve = st.sem("dve")
        v_done = st.sem("v_done")
        ones_set = st.sem("ones_set")
        passed = st.sem("passed")
        stored = [st.sem(f"stored{i}") for i in range(2)]
        blk = st.block()

        @blk.sync
        def _(sp):
            sp.dma_start(w[:], wqkvT.rearrange("(c p) n -> p c n", p=P)).then_inc(w_in, 16)
            sp.dma_start(bcol[:], qkv_b_col).then_inc(w_in, 16)
            sp.dma_start(vb[:], vb_row.to_broadcast([P, D])).then_inc(w_in, 16)

            def load(t, k, p):
                sp.wait_ge(x_free, t + 1)
                sp.sem_inc(passed, 1)
                sp.dma_start(x[p][:], xT.rearrange("(c p) n -> p c n", p=P)[:, :, bass.ds(t * CH, CH)]
                             ).then_inc(x_in[p], 16)

            def store(t, k, p):
                sp.wait_ge(dve, t * 12 + 24)
                sp.wait_ge(part1, t * 4 + 8)
                sp.sem_inc(passed, 1)
                for j in range(3):
                    for which in range(2):
                        sp.dma_start(parts[j, which, k].rearrange("m r n -> r m n")[:, :, p * CH:(p + 1) * CH],
                                     split[p][:, j, 2 * which:2 * which + 2]).then_inc(stored[p], 16)
                sp.wait_ge(v_done, t * 2 + 4)
                sp.sem_inc(passed, 1)
                for g in range(QUADS):
                    sp.dma_start(values[k, g].rearrange("(j r) n -> r j n", r=P)[:, p * TPC:(p + 1) * TPC],
                                 v[p][:, :, 4 * g:4 * g + 4].rearrange("r j h e -> r j (h e)")
                                 ).then_inc(stored[p], 16)

            pipelined(sp, NC, [(load, 0), (store, 1)])
            for p in range(2):
                sp.wait_ge(stored[p], 160 * NC // 2 + 16)

        @blk.tensor
        def _(pe):
            pe.sem_inc(x_free, 2)
            pe.wait_ge(w_in, 48)

            def project(t, k, p):
                pe.wait_ge(x_in[p], k * 16 + 16)
                for m in range(4):
                    pe.wait_ge(biased, t * 4 + m + 1)
                    for c in range(DC):
                        mm = pe.matmul(pqk[m][:], w[:, c, m * P:(m + 1) * P], x[p][:, c],
                                       start=(c == 0), stop=(c == DC - 1))
                    mm.then_inc(qk_mm, 1)
                for j in range(2):
                    pe.wait_ge(v_done, t * 2 + j + 1)
                    for h in range(2):
                        for c in range(DC):
                            mm = pe.matmul(pv[j][:, h], x[p][:, c, (2 * j + h) * P:(2 * j + h + 1) * P],
                                           w[:, c, 2 * D:], start=(c == 0), stop=(c == DC - 1))
                    mm.then_inc(v_mm, 1)
                pe.wait_ge(v_mm, t * 2 + 2)
                pe.sem_inc(x_free, 1)

            pipelined(pe, NC, [(project, 0)])

        @blk.scalar
        def _(act):
            act.sem_inc(biased, 4)
            act.wait_ge(w_in, 48)

            def bias(t, k, p):
                for m in range(4):
                    act.wait_ge(qk_mm, t * 4 + m + 1)
                    act.wait_ge(dve, t * 12 + m * 3 + 1)
                    act.wait_ge(part1, t * 4 + m + 1)
                    act.activation(full[:, m], pqk[m][:], ACT.Identity, bias=bcol[:, m:m + 1]).then_inc(biased, 1)

            pipelined(act, NC, [(bias, 0)])

        @blk.gpsimd
        def _(pool):
            for p in range(2):
                pool.memset(v[p][:, :, :, EA:], 1.0).then_inc(ones_set, 1)
            pool.sem_inc(part1, 4)
            for p in range(2):
                pool.sem_inc(stored[p], 16)

            def first(t, k, p):
                pool.wait_ge(stored[p], k * 160 + 16)
                for m in range(4):
                    pool.wait_ge(biased, t * 4 + m + 5)
                    pool.sem_inc(passed, 1)
                    pool.tensor_copy(split[p][:, 0, m], full[:, m]).then_inc(part1, 1)

            pipelined(pool, NC, [(first, 0)])

        @blk.vector
        def _(dve_):
            dve_.sem_inc(dve, 12)
            dve_.sem_inc(v_done, 2)
            dve_.wait_ge(ones_set, 2)
            dve_.wait_ge(w_in, 48)

            def rest_parts(t, k, p):
                dve_.wait_ge(stored[p], k * 160 + 16)
                for m in range(4):
                    dve_.wait_ge(part1, t * 4 + m + 5)
                    dve_.tensor_tensor(rest[:, m], full[:, m], split[p][:, 0, m], ALU.subtract).then_inc(dve, 1)
                    dve_.wait_ge(dve, t * 12 + m * 3 + 13)
                    dve_.tensor_copy(split[p][:, 1, m], rest[:, m]).then_inc(dve, 1)
                    dve_.wait_ge(dve, t * 12 + m * 3 + 14)
                    dve_.tensor_tensor(split[p][:, 2, m], rest[:, m], split[p][:, 1, m], ALU.subtract
                                       ).then_inc(dve, 1)

            def value(t, k, p):
                for j in range(2):
                    dve_.wait_ge(v_mm, t * 2 + j + 1)
                    dve_.tensor_tensor(
                        v[p][:, 2 * j:2 * j + 2, :, 0:EA],
                        pv[j][:].rearrange("r a (h e) -> r a h e", h=HA),
                        vb[:].rearrange("r (a h e) -> r a h e", a=1, h=HA).to_broadcast([P, 2, HA, EA]),
                        ALU.add).then_inc(v_done, 1)

            pipelined(dve_, NC, [(rest_parts, 0), (value, 0)])


def attn_core(nc, parts, values, ident, heads_out):
    UNITS = 4 * KT * 2
    STEPS = 2 * KT * 2
    TURNS = STEPS // 2
    LAST_1 = 28
    TURN_AT = (3, 20)
    V_CREDIT = 2 * TURNS + 4
    K2 = ROWS + SHIFT_ROWS
    with Stage(nc, "co") as st:
        q1 = [st.sb(f"q1_{i}", [P, 4, L], BF16) for i in range(2)]
        k1 = [st.sb(f"k1_{i}", [P, 4, L], BF16) for i in range(2)]
        q2 = [st.sb(f"q2_{i}", [P, 4, L], BF16) for i in range(2)]
        k2 = [st.sb(f"k2_{i}", [P, 4, L], BF16) for i in range(2)]
        v = [st.sb(f"v{i}", [P, KT, P]) for i in range(2)]
        probs = [st.sb(f"probs{i}", [P, 4, CH]) for i in range(4)]
        half_max = st.sb("half_max", [P, 4 * KT, 2])
        neg_max = st.sb("neg_max", [P, 4 * KT])
        left = st.sb("left", [P, 4 * KT])
        shift = st.sb("shift", [P, SHIFT_ROWS, 4 * KT], BF16)
        shift_t = [st.sb(f"shift_t{i}", [SHIFT_ROWS * 4 * KT, P], BF16) for i in range(2)]
        idb = st.sb("idb", [P, P], BF16)
        idf = st.sb("idf", [P, P])
        o_sb = [st.sb(f"o_sb{i}", [P, CH]) for i in range(2)]
        recip = [st.sb(f"recip{i}", [P, TPC * 4]) for i in range(2)]
        o_n = [st.sb(f"o_n{i}", [P, TPC, 4 * EA]) for i in range(2)]
        row_ps = [st.ps(f"row_ps{i}", [P, CH]) for i in range(2)]
        col_ps = [st.ps(f"col_ps{i}", [P, 2, CH]) for i in range(2)]
        o_ps = st.ps("o_ps", [P, CH])
        misc = st.ps("misc", [P, CH])
        misc_bf = misc[0:SHIFT_ROWS * 4 * KT, 0:P // 2].bitcast(BF16)

        const_in = st.sem("const_in")
        idb_done = st.sem("idb_done")
        ones_set = st.sem("ones_set")
        in1 = [st.sem(f"in1_{i}") for i in range(2)]
        in2 = [st.sem(f"in2_{i}") for i in range(2)]
        shift_in = [st.sem(f"shift_in{i}") for i in range(2)]
        row_mm = st.sem("row_mm")
        maxed = st.sem("maxed")
        dve = st.sem("dve")
        shift_mm = st.sem("shift_mm")
        shift_ev = st.sem("shift_ev")
        col_mm = st.sem("col_mm")
        exped = st.sem("exped")
        v_mm = st.sem("v_mm")
        o_read = st.sem("o_read")
        turned = st.sem("turned")
        recip_done = st.sem("recip_done")
        normed = st.sem("normed")
        stored = [st.sem(f"stored{i}") for i in range(2)]
        passed = st.sem("passed")
        blk = st.block()

        @blk.sync
        def _(sp):
            sp.dma_start(idf[:], ident).then_inc(const_in, 16)

            def load_stack(dst, which, part_of, t, sem):
                for g, part in enumerate(part_of):
                    src = parts[part, which].rearrange("b m r n -> (b m r) n")[bass.ds(t * 4 * EA, 4 * EA), :]
                    sp.dma_start(dst[EA * g:EA * (g + 1)], src.rearrange("(h e) n -> e h n", e=EA)).then_inc(sem, 16)

            def load1(t, k, p):
                sp.wait_ge(row_mm, t * UNITS + UNITS)
                sp.sem_inc(passed, 1)
                load_stack(q1[p], 0, Q_PART, t, in1[p])
                load_stack(k1[p], 1, K_PART, t, in1[p])

            def load2(t, k, p):
                sp.wait_ge(v_mm, t * TURNS + V_CREDIT - TURNS)
                sp.sem_inc(passed, 1)
                load_stack(q2[p], 0, Q_PART, t, in2[p])
                load_stack(k2[p], 1, K_PART, t, in2[p])
                sp.dma_start(v[p][:], values.rearrange("b g n c -> (b g n) c")[bass.ds(t * L, L), :].rearrange("(a r) n -> r a n", r=P)
                             ).then_inc(in2[p], 16)

            def shift_rows(t, k, p):
                sp.wait_ge(v_mm, t * TURNS + V_CREDIT - TURNS)
                sp.wait_ge(shift_ev, t + 1)
                for j in range(SHIFT_ROWS):
                    sp.dma_start(q2[p][ROWS + j:ROWS + j + 1].rearrange("j h (q c) -> j (h q) c", c=P),
                                 shift_t[p][4 * KT * j:4 * KT * (j + 1)]).then_inc(shift_in[p], 16)

            def store(t, k, qc):
                sp.wait_ge(normed, t * 2 + qc + 3)
                sp.sem_inc(passed, 1)
                dst = heads_out.rearrange("b g n c -> (b g n) c")[bass.ds(t * L + qc * CH, CH), :]
                sp.dma_start(dst.rearrange("(a r) c -> r a c", r=P), o_n[qc][:]).then_inc(stored[qc], 16)

            def body(t, k, p):
                static = isinstance(t, int)
                if not (static and t + 2 >= NI):
                    load1(t + 2, k + 1, p)
                if not (static and t + 1 >= NI):
                    load2(t + 1, k + p, 1 - p)
                if not (static and t == 0):
                    store(t - 1, k, 1)
                store(t, k, 0)
                if not (static and t + 1 >= NI):
                    shift_rows(t + 1, k + p, 1 - p)

            load1(0, 0, 0)
            load1(1, 0, 1)
            load2(0, 0, 0)
            shift_rows(0, 0, 0)
            pipelined(sp, NI, [(body, 1)], peel=2)
            store(NI - 1, 0, 1)
            for qc in range(2):
                sp.wait_ge(stored[qc], 16 * NI + 16)

        @blk.tensor
        def _(pe):
            pe.sem_inc(row_mm, 2 * UNITS)
            pe.sem_inc(v_mm, V_CREDIT)
            pe.sem_inc(turned, 2)
            pe.wait_ge(const_in, 16)
            pe.wait_ge(idb_done, 1)
            pe.wait_ge(ones_set, 2)

            def row_scores(t, k, p, u):
                h, qt, half = u // (2 * KT), u // 2 % KT, u % 2
                if u == 0:
                    pe.wait_ge(in1[p], k * 192 + 192)
                pe.wait_ge(maxed, t * UNITS + u + 1)
                pe.matmul(row_ps[u % 2][:], q1[p][0:ROWS, h, qt * P:(qt + 1) * P],
                          k1[p][0:ROWS, h, half * CH:(half + 1) * CH], start=True, stop=True).then_inc(row_mm, 1)

            def turn_shift(t, k, p):
                pe.wait_ge(dve, t * 6 + 6)
                if not (isinstance(t, int) and t == 0):
                    pe.wait_ge(normed, t * 2 + 1)
                pe.transpose(misc_bf, shift[:].rearrange("r j x -> r (j x)"), idb[:]).then_inc(shift_mm, 1)

            def col_scores(t, k, p, s):
                qc, kt, pair = s // (2 * KT), s // 2 % KT, s % 2
                if s == 0:
                    pe.wait_ge(in2[p], k * 208 + 208)
                    pe.wait_ge(shift_in[p], k * 48 + 48)
                pe.wait_ge(exped, t * STEPS + s + 1)
                for j in range(2):
                    h = 2 * pair + j
                    mm = pe.matmul(col_ps[s % 2][:, j], k2[p][0:K2, h, kt * P:(kt + 1) * P],
                                   q2[p][0:K2, h, qc * CH:(qc + 1) * CH], start=True, stop=True)
                mm.then_inc(col_mm, 1)

            def times_v(t, k, p, m):
                qc, kt = m // KT, m % KT
                if kt == 0:
                    pe.wait_ge(o_read, t * 2 + qc + 1)
                pe.wait_ge(exped, t * STEPS + 2 * m + 4)
                for h in range(4):
                    mm = pe.matmul(o_ps[32 * h:32 * h + 32, :], v[p][:, kt, 32 * h:32 * h + 32],
                                   probs[m % 4][:, h], start=(kt == 0), stop=(kt == KT - 1))
                mm.then_inc(v_mm, 1)

            def turn_back(t, qc):
                pe.wait_ge(o_read, t * 2 + qc + 2)
                pe.wait_ge(normed, t * 2 + qc + 2)
                if qc == 1 and not (isinstance(t, int) and t == NI - 1):
                    pe.wait_ge(shift_ev, t + 2)
                elif qc == 0:
                    pe.wait_ge(shift_ev, t + 1)
                for a in range(TPC):
                    mm = pe.transpose(misc[:, a * P:(a + 1) * P], o_sb[qc][:, a * P:(a + 1) * P], idf[:])
                mm.then_inc(turned, 1)

            def body(t, k, p):
                first = isinstance(t, int) and t == 0
                last = isinstance(t, int) and t == NI - 1
                for s in range(STEPS):
                    col_scores(t, k, p, s)
                    if s < LAST_1 and not last:
                        for u in range(UNITS * s // LAST_1, UNITS * (s + 1) // LAST_1):
                            row_scores(t + 1, k + p, 1 - p, u)
                    if s == 1 and not first:
                        times_v(t - 1, k + p - 1, 1 - p, TURNS - 1)
                    if s % 2 and s >= 3:
                        times_v(t, k, p, (s - 3) // 2)
                    if s == TURN_AT[0] and not first:
                        turn_back(t - 1, 1)
                    if s == TURN_AT[1]:
                        turn_back(t, 0)
                    if s == 30 and not last:
                        turn_shift(t + 1, k + p, 1 - p)

            for u in range(UNITS):
                row_scores(0, 0, 0, u)
            turn_shift(0, 0, 0)
            pipelined(pe, NI, [(body, 1)], peel=2)
            times_v(NI - 1, 0, (NI - 1) % 2, TURNS - 1)
            turn_back(NI - 1, 1)

        @blk.scalar
        def _(act):
            act.sem_inc(exped, 2)
            act.sem_inc(o_read, 1)

            def copy_shift(t, k, p):
                act.wait_ge(shift_mm, t + 1)
                if not (isinstance(t, int) and t < 2):
                    act.wait_ge(shift_in[p], k * 48)
                act.copy(shift_t[p][:], misc_bf).then_inc(shift_ev, 1)

            def exp(t, k, p, s):
                act.wait_ge(col_mm, t * STEPS + s + 1)
                act.wait_ge(v_mm, t * TURNS + s // 2 - 3 + V_CREDIT)
                act.activation(probs[s // 2 % 4][:, 2 * (s % 2):2 * (s % 2) + 2], col_ps[s % 2][:], ACT.Exp,
                               scale=float(EA) ** -0.5).then_inc(exped, 1)

            def copy_o(t, qc):
                act.wait_ge(v_mm, t * TURNS + (qc + 1) * KT + V_CREDIT)
                act.wait_ge(turned, t * 2 + qc + 1)
                act.copy(o_sb[qc][:], o_ps[:]).then_inc(o_read, 1)

            def body(t, k, p):
                first = isinstance(t, int) and t == 0
                last = isinstance(t, int) and t == NI - 1
                for s in range(STEPS):
                    exp(t, k, p, s)
                    if s == 2 and not first:
                        copy_o(t - 1, 1)
                    if s == 18:
                        copy_o(t, 0)
                    if s == 30 and not last:
                        copy_shift(t + 1, k + p, 1 - p)

            copy_shift(0, 0, 0)
            pipelined(act, NI, [(body, 1)], peel=2)
            copy_o(NI - 1, 1)

        @blk.gpsimd
        def _(pool):
            for p in range(2):
                pool.memset(k2[p][ROWS:K2], 1.0).then_inc(ones_set, 1)
                pool.sem_inc(stored[p], 16)

        @blk.vector
        def _(ve):
            ve.sem_inc(maxed, 2)
            ve.sem_inc(normed, 2)
            ve.wait_ge(const_in, 16)
            ve.tensor_copy(idb[:], idf[:]).then_inc(idb_done, 1)

            def row_max(t, u):
                ve.wait_ge(row_mm, t * UNITS + u + 1 + 2 * UNITS)
                ve.tensor_reduce(half_max[:, u // 2, u % 2:u % 2 + 1], row_ps[u % 2][:], AXX, ALU.max
                                 ).then_inc(maxed, 1)

            def split_max(t):
                ve.wait_ge(maxed, t * UNITS + UNITS + 2)
                if not (isinstance(t, int) and t == 0):
                    ve.wait_ge(shift_mm, t)
                ve.tensor_reduce(neg_max[:], half_max[:], AXX, ALU.max, negate=True).then_inc(dve, 1)
                ve.wait_ge(dve, t * 6 + 1)
                ve.tensor_copy(shift[:, 0], neg_max[:]).then_inc(dve, 1)
                ve.wait_ge(dve, t * 6 + 2)
                ve.tensor_tensor(left[:], neg_max[:], shift[:, 0], ALU.subtract).then_inc(dve, 1)
                ve.wait_ge(dve, t * 6 + 3)
                ve.tensor_copy(shift[:, 1], left[:]).then_inc(dve, 1)
                ve.wait_ge(dve, t * 6 + 4)
                ve.tensor_tensor(neg_max[:], left[:], shift[:, 1], ALU.subtract).then_inc(dve, 1)
                ve.wait_ge(dve, t * 6 + 5)
                ve.tensor_copy(shift[:, 2], neg_max[:]).then_inc(dve, 1)

            def norm(t, qc):
                heads = misc[:].rearrange("r (x e) -> r x e", e=2 * EA)
                ve.wait_ge(turned, t * 2 + qc + 3)
                ve.reciprocal(recip[qc][:], heads[:, :, EA]).then_inc(recip_done, 1)
                ve.wait_ge(recip_done, t * 2 + qc + 1)
                ve.wait_ge(stored[qc], t * 16 + 16)
                ve.tensor_tensor(o_n[qc][:].rearrange("r a (h e) -> r (a h) e", e=EA), heads[:, :, 0:EA],
                                 recip[qc][:].rearrange("r (x e) -> r x e", e=1).to_broadcast([P, TPC * 4, EA]),
                                 ALU.mult).then_inc(normed, 1)

            def body(t, k, p):
                first = isinstance(t, int) and t == 0
                last = isinstance(t, int) and t == NI - 1
                after = [UNITS * (s + 1) // LAST_1 for s in TURN_AT]
                for u in range(UNITS):
                    if u == after[0] and not first:
                        norm(t - 1, 1)
                    if u == after[1]:
                        norm(t, 0)
                    if not last:
                        row_max(t + 1, u)
                if not last:
                    split_max(t + 1)

            for u in range(UNITS):
                row_max(0, u)
            split_max(0)
            pipelined(ve, NI, [(body, 1)], peel=2)
            norm(NI - 1, 1)


EPS = 1e-5


def attn_close(nc, x, heads, proj_wT, proj_b_row, ident, x1):
    with Stage(nc, "cl") as st:
        w = st.sb("w", [P, DC, D])
        bias = st.sb("bias", [P, D])
        idf = st.sb("idf", [P, P])
        zero = st.sb("zero", [B, D])
        power = st.sb("power", [P, TPC])
        h = [st.sb(f"h{i}", [P, TPC, D]) for i in range(2)]
        xr = [st.sb(f"xr{i}", [P, TPC, D]) for i in range(2)]
        xb = [st.sb(f"xb{i}", [P, TPC, D]) for i in range(2)]
        hT = [st.sb(f"hT{i}", [P, DC, CH]) for i in range(2)]
        res = [st.sb(f"res{i}", [P, TPC, D]) for i in range(2)]
        out = [st.sb(f"out{i}", [P, TPC, D]) for i in range(2)]
        stats = st.sb("stats", [P, TPC, 6])
        mv = [st.sb(f"mv{i}", [P, TPC, 2]) for i in range(2)]
        var = [st.sb(f"var{i}", [P, TPC]) for i in range(2)]
        rstd = [st.sb(f"rstd{i}", [P, TPC]) for i in range(2)]
        turn_ps = [[st.ps(f"turn{i}{c}", [P, CH]) for c in range(DC)] for i in range(2)]
        y_ps = [[st.ps(f"y{i}{j}", [P, 2, D]) for j in range(2)] for i in range(2)]

        const_in = st.sem("const_in")
        set_ = st.sem("set")
        h_in = [st.sem(f"h_in{i}") for i in range(2)]
        x_in = [st.sem(f"x_in{i}") for i in range(2)]
        turned = st.sem("turned")
        hT_done = st.sem("hT_done")
        y_mm = st.sem("y_mm")
        xb_done = st.sem("xb_done")
        added = st.sem("added")
        dve = st.sem("dve")
        rstd_done = st.sem("rstd_done")
        normed = st.sem("normed")
        stored = [st.sem(f"stored{i}") for i in range(2)]
        zeros_out = st.sem("zeros_out")
        passed = st.sem("passed")
        blk = st.block()
        xc = x.rearrange("(t a r) c -> t r a c", a=TPC, r=P)

        @blk.sync
        def _(sp):
            sp.dma_start(w[:], proj_wT.rearrange("(c p) n -> p c n", p=P)).then_inc(const_in, 16)
            sp.dma_start(bias[:], proj_b_row.to_broadcast([P, D])).then_inc(const_in, 16)
            sp.dma_start(idf[:], ident).then_inc(const_in, 16)
            sp.wait_ge(set_, 2)
            sp.dma_start(x1[:, 0], zero[:]).then_inc(zeros_out, 16)

            def load(t, k, p):
                sp.wait_ge(turned, t * DC + DC)
                sp.sem_inc(passed, 1)
                for g in range(QUADS):
                    src = heads[k, g].rearrange("(t a r) c -> t r a c", a=TPC, r=P)[p]
                    sp.dma_start(h[p][:, :, 4 * EA * g:4 * EA * (g + 1)], src).then_inc(h_in[p], 16)
                sp.wait_ge(xb_done, t + 1)
                sp.sem_inc(passed, 1)
                sp.dma_start(xr[p][:], xc[t]).then_inc(x_in[p], 16)

            def store(t, k, p):
                sp.wait_ge(normed, t * TPC + 3 * TPC)
                sp.sem_inc(passed, 1)
                sp.dma_start(x1[k, 1 + p * CH:1 + (p + 1) * CH].rearrange("(a r) c -> r a c", r=P), out[p][:]
                             ).then_inc(stored[p], 16)

            pipelined(sp, NC, [(load, 0), (store, 3)])
            sp.wait_ge(zeros_out, 16)
            for p in range(2):
                sp.wait_ge(stored[p], 16 * NC // 2 + 16)

        @blk.tensor
        def _(pe):
            pe.sem_inc(turned, 2 * DC)
            pe.sem_inc(y_mm, 4)
            pe.wait_ge(const_in, 48)

            def turn(t, k, p):
                pe.wait_ge(h_in[p], k * 64 + 64)
                for c in range(DC):
                    pe.wait_ge(hT_done, t * DC + c + 1)
                    for a in range(TPC):
                        mm = pe.transpose(turn_ps[p][c][:, a * P:(a + 1) * P], h[p][:, a, c * P:(c + 1) * P], idf[:])
                    mm.then_inc(turned, 1)

            def project(t, k, p):
                pe.wait_ge(hT_done, t * DC + 3 * DC)
                for j in range(2):
                    pe.wait_ge(added, t * 2 + j + 1)
                    for a in range(2):
                        for c in range(DC):
                            mm = pe.matmul(y_ps[p][j][:, a], hT[p][:, c, (2 * j + a) * P:(2 * j + a + 1) * P],
                                           w[:, c], start=(c == 0), stop=(c == DC - 1))
                    mm.then_inc(y_mm, 1)

            pipelined(pe, NC, [(turn, 0), (project, 1)])

        @blk.scalar
        def _(act):
            act.sem_inc(hT_done, 2 * DC)

            def copy_h(t, k, p):
                for c in range(DC):
                    act.wait_ge(turned, t * DC + c + 1 + 2 * DC)
                    act.wait_ge(y_mm, t * 2 + 2)
                    act.copy(hT[p][:, c], turn_ps[p][c][:]).then_inc(hT_done, 1)

            pipelined(act, NC, [(copy_h, 0)])

        @blk.gpsimd
        def _(pool):
            pool.sem_inc(xb_done, 2)
            for p in range(2):
                pool.sem_inc(stored[p], 16)
            pool.memset(zero[:], 0.0).then_inc(set_, 1)
            pool.memset(power[:], -0.5).then_inc(set_, 1)
            pool.wait_ge(set_, 2)
            pool.wait_ge(const_in, 48)

            def add_bias(t, k, p):
                pool.wait_ge(x_in[p], k * 16 + 16)
                pool.wait_ge(added, t * 2 + 2)
                pool.tensor_tensor(xb[p][:], xr[p][:], bias[:].rearrange("r (a c) -> r a c", a=1
                                   ).to_broadcast([P, TPC, D]), ALU.add).then_inc(xb_done, 1)

            def root(t, k, p):
                pool.wait_ge(dve, t * (2 * TPC + 1) + 2 * TPC + 1)
                pool.tensor_tensor(rstd[p][:], var[p][:], power[:], ALU.pow).then_inc(rstd_done, 1)

            pipelined(pool, NC, [(add_bias, 0), (root, 1)])

        @blk.vector
        def _(ve):
            ve.sem_inc(added, 4)
            ve.sem_inc(normed, 2 * TPC)

            def add(t, k, p):
                ve.wait_ge(normed, t * TPC + TPC)
                for j in range(2):
                    ve.wait_ge(y_mm, t * 2 + j + 5)
                    ve.wait_ge(xb_done, t + 3)
                    ve.tensor_tensor(res[p][:, 2 * j:2 * j + 2], y_ps[p][j][:], xb[p][:, 2 * j:2 * j + 2], ALU.add
                                     ).then_inc(added, 1)

            def moments(t, k, p):
                n = t * (2 * TPC + 1)
                for a in range(TPC):
                    ve.wait_ge(added, t * 2 + a // 2 + 5)
                    ve.bn_stats(stats[:, a], res[p][:, a]).then_inc(dve, 1)
                ve.wait_ge(dve, n + TPC)
                ve.sem_inc(passed, 1)
                for a in range(TPC):
                    ve.bn_aggr(mv[p][:, a], stats[:, a]).then_inc(dve, 1)
                ve.wait_ge(dve, n + 2 * TPC)
                ve.tensor_scalar(var[p][:], mv[p][:, :, 1], EPS, None, ALU.add).then_inc(dve, 1)

            def norm(t, k, p):
                ve.wait_ge(rstd_done, t + 1)
                ve.wait_ge(stored[p], k * 16 + 16)
                for a in range(TPC):
                    ve.tensor_scalar(out[p][:, a], res[p][:, a], mv[p][:, a, 0:1], rstd[p][:, a:a + 1],
                                     ALU.subtract, ALU.mult).then_inc(normed, 1)

            pipelined(ve, NC, [(add, 0), (moments, 0), (norm, 1)])


HB, EB = 8, 64
INNER = HB * EB
WIN = P
NW = L // WIN
PAIRS = HB // 2
QK_SCALE = 8.0
MASKED = -1e37
ROWS_B = 1 + L


def window_attn(nc, name, src, dst, wqkv, wo, q_scale, k_scale, rope, masks, masks0, ident):
    src_rows, dst_rows = src.rearrange("b n c -> (b n) c"), dst.rearrange("b n c -> (b n) c")
    with Stage(nc, name) as st:
        w = st.sb("w", [P, DC, 3 * INNER])
        w_out = st.sb("w_out", [P, PAIRS, D])
        idf = st.sb("idf", [P, P])
        tab = st.sb("tab", [P, NW, 4, EB])
        scales = st.sb("scales", [P, 4, EB])
        mask = [st.sb(f"mask{i}", [P, 2 * WIN]) for i in range(2)]
        zero = st.sb("zero", [B, D])
        power = st.sb("power", [P, HB])
        xf = [st.sb(f"xf{i}", [P, P]) for i in range(2)]
        xs = [st.sb(f"xs{i}", [P, P]) for i in range(2)]
        xr = [st.sb(f"xr{i}", [P, D]) for i in range(2)]
        hT = st.sb("hT", [P, DC, P])
        sq = st.sb("sq", [P, 2, INNER])
        ssq = st.sb("ssq", [P, 2, HB])
        inv = st.sb("inv", [P, 2, HB])
        by_cos = st.sb("by_cos", [P, 2, INNER])
        by_sin = st.sb("by_sin", [P, 2, INNER])
        turned = st.sb("turned", [P, 2, INNER])
        unit = st.sb("unit", [P, 2, INNER])
        qT = st.sb("qT", [P, HB, P])
        kT = [st.sb(f"kT{i}", [P, PAIRS, WIN]) for i in range(2)]
        v = [st.sb(f"v{i}", [P, INNER]) for i in range(2)]
        sim = st.sb("sim", [P, HB, 2 * WIN])
        top = st.sb("top", [P, HB])
        shift = st.sb("shift", [P, HB])
        probs = st.sb("probs", [P, HB, 2 * WIN])
        total = st.sb("total", [P, HB])
        recip = st.sb("recip", [P, HB])
        pn = st.sb("pn", [P, HB, 2 * WIN])
        pT = st.sb("pT", [P, PAIRS, CH])
        oT = st.sb("oT", [P, PAIRS, P])
        out = [st.sb(f"out{i}", [P, D]) for i in range(2)]
        t_ps = st.ps("t_ps", [P, DC, P])
        y_ps = t_ps
        qkv_ps = [st.ps(f"qkv_ps{i}", [P, INNER]) for i in range(3)]
        s_ps = [st.ps(f"s_ps{g}", [P, CH]) for g in range(PAIRS)]
        o_ps = s_ps[0]

        const_in, set_, tab_done = st.sem("const_in"), st.sem("set"), st.sem("tab_done")
        a_in = [st.sem(f"a_in{i}") for i in range(2)]
        r_in = [st.sem(f"r_in{i}") for i in range(2)]
        m_in = st.sem("m_in")
        xT_mm = st.sem("xT_mm")
        hT_done = st.sem("hT_done")
        qkv_mm = st.sem("qkv_mm")
        squared = st.sem("squared")
        summed = st.sem("summed")
        bounded = st.sem("bounded")
        inv_done = st.sem("inv_done")
        rope_mul = st.sem("rope_mul")
        rope_add = st.sem("rope_add")
        unit_done = st.sem("unit_done")
        qkT_mm = st.sem("qkT_mm")
        qT_done = st.sem("qT_done")
        kT_done = st.sem("kT_done")
        v_done = st.sem("v_done")
        s_mm = st.sem("s_mm")
        top_done = st.sem("top_done")
        shift_done = st.sem("shift_done")
        exped = st.sem("exped")
        recip_done = st.sem("recip_done")
        pn_done = st.sem("pn_done")
        pT_mm = st.sem("pT_mm")
        pT_act = st.sem("pT_act")
        pT_dve = st.sem("pT_dve")
        o_mm = st.sem("o_mm")
        oT_done = st.sem("oT_done")
        y_mm = st.sem("y_mm")
        y_done = st.sem("y_done")
        stored = [st.sem(f"stored{i}") for i in range(2)]
        zeros_out = st.sem("zeros_out")
        passed = st.sem("passed")
        blk = st.block()

        def static(t):
            return isinstance(t, int)

        @blk.sync
        def _(sp):
            for c in range(DC):
                sp.dma_start(w[:, c], wqkv[c * P:(c + 1) * P]).then_inc(const_in, 16)
            sp.dma_start(w_out[:], wo.rearrange("(g p) n -> p g n", p=P)).then_inc(const_in, 16)
            sp.dma_start(idf[:], ident).then_inc(const_in, 16)
            for f in range(4):
                sp.dma_start(tab[:, :, f], rope[f].rearrange("(w r) e -> r w e", r=P)).then_inc(const_in, 16)
            sp.dma_start(mask[0][:, WIN:], masks[:, WIN:]).then_inc(const_in, 16)
            sp.dma_start(mask[1][:], masks).then_inc(const_in, 16)
            for f, scale in enumerate((q_scale, k_scale)):
                sp.dma_start(scales[:, 2 * f], scale.to_broadcast([P, EB])).then_inc(const_in, 16)
                for h in range(2):
                    sp.dma_start(scales[:, 2 * f + 1, h * EB // 2:(h + 1) * EB // 2],
                                 scale[:, (1 - h) * EB // 2:(2 - h) * EB // 2].to_broadcast([P, EB // 2])
                                 ).then_inc(const_in, 16)
            sp.wait_ge(set_, 5)
            sp.dma_start(dst[:, 0], zero[:]).then_inc(zeros_out, 16)

            def load(t, k, p):
                sp.wait_ge(xT_mm, t + 1)
                sp.sem_inc(passed, 1)
                sp.dma_start(xf[p][:], src_rows[bass.ds(t * P + k // 4 + 1, P), 0:P]).then_inc(a_in[p], 16)
                sp.dma_start(xs[p][:], src_rows[bass.ds(t * P + k // 4, P), P:D]).then_inc(a_in[p], 16)

            def load_rest(t, k, p):
                sp.wait_ge(y_done, t + 1)
                sp.sem_inc(passed, 1)
                sp.dma_start(xr[p][:], src_rows[bass.ds(t * P + k // 4 + 1, P), :]).then_inc(r_in[p], 16)
                if p == 0:
                    sp.wait_ge(top_done, t * HB + HB)
                    sp.sem_inc(passed, 1)
                    sp.dma_start(mask[0][:, 0:WIN], masks0[k % 4]).then_inc(m_in, 16)

            def store(t, k, p):
                sp.wait_ge(y_done, t + 3)
                sp.sem_inc(passed, 1)
                sp.dma_start(dst_rows[bass.ds(t * P + k // 4 + 1, P), :], out[p][:]).then_inc(stored[p], 16)

            pipelined(sp, NT, [(load, 0), (load_rest, 0), (store, 3)])
            sp.wait_ge(zeros_out, 16)
            for p in range(2):
                sp.wait_ge(stored[p], 16 * NT // 2 + 16)

        @blk.tensor
        def _(pe):
            pe.sem_inc(xT_mm, 2)
            pe.wait_ge(const_in, 16 * 16)
            pe.wait_ge(set_, 5)

            def turn_x(t, k, p):
                pe.wait_ge(a_in[p], k * 32 + 32)
                pe.wait_ge(y_done, t + 1)
                for c, x in enumerate((xf[p], xs[p])):
                    mm = pe.transpose(t_ps[:, c], x[:], idf[:])
                mm.then_inc(xT_mm, 1)

            def qkv(t, k, p):
                pe.wait_ge(hT_done, t + 1)
                for i in range(3):
                    if not (static(t) and t == 0):
                        if i == 0:
                            pe.wait_ge(qT_done, t * 2)
                        elif i == 1:
                            pe.wait_ge(kT_done, t)
                        else:
                            pe.wait_ge(v_done, t)
                    for c in range(DC):
                        mm = pe.matmul(qkv_ps[i][:], hT[:, c], w[:, c, i * INNER:(i + 1) * INNER],
                                       start=(c == 0), stop=(c == DC - 1))
                    mm.then_inc(qkv_mm, 1)

            def turn_qk(t, k, p):
                for i in range(2):
                    pe.wait_ge(unit_done, t * 2 + i + 1)
                    for g in range(PAIRS):
                        mm = pe.transpose(qkv_ps[i][:, g * P:(g + 1) * P], unit[:, i, g * P:(g + 1) * P], idf[:])
                    mm.then_inc(qkT_mm, 1)

            def scores(t, k, p):
                pe.wait_ge(qT_done, t * 2 + 2)
                pe.wait_ge(kT_done, t + 1)
                for g in range(PAIRS):
                    if not (static(t) and t == 0):
                        if g == 0:
                            pe.wait_ge(oT_done, t)
                        elif g == 1:
                            pe.wait_ge(pT_act, t * 2)
                        else:
                            pe.wait_ge(pT_dve, t * 2)
                    for j in range(2):
                        for c, keys in enumerate((kT[1 - p], kT[p])):
                            mm = pe.matmul(s_ps[g][:, (2 * j + c) * P:(2 * j + c + 1) * P], qT[:, 2 * g + j],
                                           keys[:, g], start=True, stop=True)
                    mm.then_inc(s_mm, 1)

            def turn_p(t, k, p):
                for g in range(PAIRS):
                    pe.wait_ge(pn_done, t * HB + 2 * g + 2)
                    for j in range(2):
                        for c in range(2):
                            mm = pe.transpose(s_ps[g][:, (2 * j + c) * P:(2 * j + c + 1) * P],
                                              pn[:, 2 * g + j, c * WIN:(c + 1) * WIN], idf[:])
                    mm.then_inc(pT_mm, 1)

            def times_v(t, k, p):
                pe.wait_ge(pT_act, t * 2 + 2)
                pe.wait_ge(pT_dve, t * 2 + 2)
                pe.wait_ge(v_done, t + 1)
                for g in range(PAIRS):
                    for c, values in enumerate((v[1 - p], v[p])):
                        for j in range(2):
                            h = 2 * g + j
                            mm = pe.matmul(o_ps[EB * j:EB * (j + 1), g * P:(g + 1) * P],
                                           values[:, h * EB:(h + 1) * EB],
                                           pT[:, g, (2 * j + c) * P:(2 * j + c + 1) * P],
                                           start=(c == 0), stop=(c == 1))
                mm.then_inc(o_mm, 1)

            def out_proj(t, k, p):
                pe.wait_ge(oT_done, t + 1)
                if not (static(t) and t == NT - 1):
                    pe.wait_ge(hT_done, t + 2)
                for g in range(PAIRS):
                    mm = pe.matmul(y_ps[:].rearrange("r c n -> r (c n)"), oT[:, g], w_out[:, g],
                                   start=(g == 0), stop=(g == PAIRS - 1))
                mm.then_inc(y_mm, 1)

            pipelined(pe, NT, [(turn_x, 0), (scores, 1), (qkv, 0), (turn_p, 1), (times_v, 1), (turn_qk, 0),
                               (out_proj, 1)])

        @blk.scalar
        def _(act):
            def copy_x(t, k, p):
                act.wait_ge(xT_mm, t + 3)
                if not (static(t) and t == 0):
                    act.wait_ge(qkv_mm, t * 3)
                act.copy(hT[:], t_ps[:]).then_inc(hT_done, 1)

            def exps(t, k, p):
                if not (static(t) and t == 0):
                    act.wait_ge(pn_done, t * HB)
                for h in range(HB):
                    if h % 2 == 0:
                        act.wait_ge(shift_done, t * PAIRS + h // 2 + 1)
                    act.activation(probs[:, h], sim[:, h], ACT.Exp, bias=shift[:, h:h + 1], scale=QK_SCALE,
                                   accum_out=total[:, h:h + 1]).then_inc(exped, 1)

            def squares(t, k, p):
                for i in range(2):
                    act.wait_ge(qkv_mm, t * 3 + i + 1)
                    if not (static(t) and t == 0):
                        act.wait_ge(summed, t * 2 + i - 1)
                    act.activation(sq[:, i], qkv_ps[i][:], ACT.Square).then_inc(squared, 1)

            def copy_p(t, k, p):
                for g in range(2):
                    act.wait_ge(pT_mm, t * PAIRS + g + 1)
                    if not (static(t) and t == 0):
                        act.wait_ge(o_mm, t)
                    act.copy(pT[:, g], s_ps[g][:]).then_inc(pT_act, 1)

            def copy_o(t, k, p):
                act.wait_ge(o_mm, t + 1)
                if not (static(t) and t == 0):
                    act.wait_ge(y_mm, t)
                act.copy(oT[:].rearrange("r g n -> r (g n)"), o_ps[:]).then_inc(oT_done, 1)

            def copy_v(t, k, p):
                act.wait_ge(qkv_mm, t * 3 + 3)
                if not (static(t) and t == 0):
                    act.wait_ge(o_mm, t)
                act.copy(v[p][:], qkv_ps[2][:]).then_inc(v_done, 1)

            def copy_q(t, k, p):
                act.wait_ge(qkT_mm, t * 2 + 1)
                if not (static(t) and t == 0):
                    act.wait_ge(s_mm, t * PAIRS)
                for j in range(2):
                    rows = slice(EB * j, EB * (j + 1))
                    act.copy(qT[rows, j:HB:2], qkv_ps[0][rows, :].rearrange("r (g n) -> r g n", g=PAIRS)
                             ).then_inc(qT_done, 1)

            act.wait_ge(set_, 5)
            pipelined(act, NT, [(copy_x, 0), (exps, 1), (squares, 0), (copy_p, 1), (copy_o, 1), (copy_v, 0),
                                (copy_q, 0)])

        @blk.gpsimd
        def _(pool):
            pool.memset(zero[:], 0.0).then_inc(set_, 1)
            pool.memset(power[:], -0.5).then_inc(set_, 1)
            pool.memset(kT[1][:], 0.0).then_inc(set_, 1)
            pool.memset(v[1][:], 0.0).then_inc(set_, 1)
            pool.memset(qT[:], 0.0).then_inc(set_, 1)
            for p in range(2):
                pool.sem_inc(stored[p], 16)
            pool.wait_ge(set_, 5)

            def unit_rows(t, k, p):
                for i in range(2):
                    pool.wait_ge(bounded, t * 2 + i + 1)
                    pool.tensor_tensor(inv[:, i], ssq[:, i], power[:], ALU.pow).then_inc(inv_done, 1)
                for i in range(2):
                    pool.wait_ge(inv_done, t * 2 + i + 1)
                    pool.wait_ge(rope_add, t * 2 + i + 1)
                    if not (static(t) and t == 0):
                        pool.wait_ge(qkT_mm, t * 2 + i - 1)
                    pool.tensor_tensor(unit[:, i].rearrange("r (h e) -> r h e", h=HB),
                                       turned[:, i].rearrange("r (h e) -> r h e", h=HB),
                                       inv[:, i].rearrange("r (h e) -> r h e", e=1).to_broadcast([P, HB, EB]),
                                       ALU.mult).then_inc(unit_done, 1)

            pipelined(pool, NT, [(unit_rows, 0)])

        @blk.vector
        def _(ve):
            ve.sem_inc(top_done, 2 * HB)
            ve.sem_inc(y_done, 2)
            ve.wait_ge(const_in, 16 * 16)
            for i in range(2):
                for j in range(2):
                    f = 2 * i + j
                    ve.tensor_tensor(tab[:, :, f], tab[:, :, f], scales[:, f].rearrange("r (w e) -> r w e", w=1
                                     ).to_broadcast([P, NW, EB]), ALU.mult).then_inc(tab_done, 1)
            ve.wait_ge(tab_done, 4)

            def soften(t, k, p):
                if p == 0:
                    ve.wait_ge(m_in, k * 16 + 16)
                if not (static(t) and t == 0):
                    ve.wait_ge(exped, t * HB)
                for g in range(PAIRS):
                    ve.wait_ge(s_mm, t * PAIRS + g + 1)
                    ve.sem_inc(passed, 1)
                    for j in range(2):
                        h = 2 * g + j
                        ve.tensor_tensor_reduce(out=sim[:, h], in0=s_ps[g][:, j * 2 * WIN:(j + 1) * 2 * WIN],
                                                in1=mask[p][:], scale=1.0, scalar=-3e38, op0=ALU.add, op1=ALU.max,
                                                accum_out=top[:, h:h + 1]).then_inc(top_done, 1)
                    ve.wait_ge(top_done, t * HB + 2 * g + 2 + 2 * HB)
                    ve.tensor_scalar(shift[:, 2 * g:2 * g + 2], top[:, 2 * g:2 * g + 2], -QK_SCALE, None, ALU.mult
                                     ).then_inc(shift_done, 1)
                for g in range(PAIRS):
                    ve.wait_ge(exped, t * HB + 2 * g + 2)
                    ve.reciprocal(recip[:, 2 * g:2 * g + 2], total[:, 2 * g:2 * g + 2]).then_inc(recip_done, 1)
                    ve.wait_ge(recip_done, t * PAIRS + g + 1)
                    if not (static(t) and t == 0):
                        ve.wait_ge(pT_mm, t * PAIRS + g + 1 - PAIRS)
                    for h in range(2 * g, 2 * g + 2):
                        ve.tensor_scalar(pn[:, h], probs[:, h], recip[:, h:h + 1], None, ALU.mult).then_inc(pn_done, 1)

            def norms(t, k, p):
                for i in range(2):
                    ve.wait_ge(squared, t * 2 + i + 1)
                    if not (static(t) and t == 0):
                        ve.wait_ge(inv_done, t * 2 + i - 1)
                    ve.tensor_reduce(ssq[:, i], sq[:, i].rearrange("r (h e) -> r h e", h=HB), AXX, ALU.add
                                     ).then_inc(summed, 1)
                for i in range(2):
                    ve.wait_ge(summed, t * 2 + i + 1)
                    ve.tensor_scalar(ssq[:, i], ssq[:, i], 1e-24, None, ALU.max).then_inc(bounded, 1)

            def rotate(t, k, p):
                w_ = k % 4 * 2 + p
                for i in range(2):
                    halves = qkv_ps[i][:].rearrange("r (h a e) -> r h a e", h=HB, a=2)
                    ve.wait_ge(qkv_mm, t * 3 + i + 1)
                    if not (static(t) and t == 0):
                        ve.wait_ge(rope_add, t * 2 + i - 1)
                    for j, x, dst_ in ((0, halves, by_cos), (1, halves[:, :, ::-1, :], by_sin)):
                        table = tab[:, bass.ds(w_, 1), 2 * i + j].rearrange("r w (a e) -> r w a e", a=2)
                        ve.tensor_tensor(dst_[:, i].rearrange("r (h a e) -> r h a e", h=HB, a=2), x,
                                         table.to_broadcast([P, HB, 2, EB // 2]), ALU.mult).then_inc(rope_mul, 1)
                for i in range(2):
                    ve.wait_ge(rope_mul, t * 4 + 2 * i + 2)
                    if not (static(t) and t == 0):
                        ve.wait_ge(unit_done, t * 2 + i - 1)
                    ve.tensor_tensor(turned[:, i], by_cos[:, i], by_sin[:, i], ALU.add).then_inc(rope_add, 1)

            def copy_p(t, k, p):
                for g in range(2, PAIRS):
                    ve.wait_ge(pT_mm, t * PAIRS + g + 1)
                    if not (static(t) and t == 0):
                        ve.wait_ge(o_mm, t)
                    ve.tensor_copy(pT[:, g], s_ps[g][:]).then_inc(pT_dve, 1)

            def copy_k(t, k, p):
                ve.wait_ge(qkT_mm, t * 2 + 2)
                if not (static(t) and t == 0):
                    ve.wait_ge(s_mm, t * PAIRS)
                ve.tensor_copy(kT[p][:].rearrange("r g n -> r (g n)"), qkv_ps[1][:]).then_inc(kT_done, 1)

            def add(t, k, p):
                ve.wait_ge(y_mm, t + 1)
                ve.wait_ge(r_in[p], k * 16 + 16)
                ve.wait_ge(stored[p], k * 16 + 16)
                ve.tensor_tensor(out[p][:], y_ps[:].rearrange("r c n -> r (c n)"), xr[p][:], ALU.add).then_inc(y_done, 1)

            pipelined(ve, NT, [(soften, 1), (norms, 0), (rotate, 0), (copy_p, 1), (copy_k, 0), (add, 1)])


HID = int(D * 4 * 2 / 3)
MT = -(-HID // P)
M_ROWS = [min(P, HID - m * P) for m in range(MT)]
AG = 2 * MT


def gated_ffn(nc, name, src, dst, w1, b1_col, w2, b2_row, ln_g_col, ln_b_col, ident, base=None):
    with Stage(nc, name) as st:
        w = st.sb("w", [P, DC, 2 * HID])
        wg = st.sb("wg", [P, DC, 2 * HID])
        v = st.sb("v", [P, MT, D])
        b1 = st.sb("b1", [P, AG])
        bias = st.sb("bias", [P, AG])
        b2 = st.sb("b2", [P, D])
        lg = st.sb("lg", [P, DC])
        lb = st.sb("lb", [P, DC])
        lb_wide = st.sb("lb_wide", [P, DC, 64])
        idf = st.sb("idf", [P, P])
        zero = st.sb("zero", [B, D])
        power = st.sb("power", [P, TPC])
        x = [st.sb(f"x{i}", [P, TPC, D]) for i in range(2)]
        xr = [st.sb(f"xr{i}", [P, TPC, D]) for i in range(2)]
        xb = [st.sb(f"xb{i}", [P, TPC, D]) for i in range(2)]
        xn = [st.sb(f"xn{i}", [P, TPC, D]) for i in range(2)]
        hT = [st.sb(f"hT{i}", [P, DC, CH]) for i in range(2)]
        ge = [st.sb(f"ge{i}", [P, CH]) for i in range(2)]
        hg = st.sb("hg", [P, MT, CH])
        out = [st.sb(f"out{i}", [P, TPC, D]) for i in range(2)]
        stats = st.sb("stats", [P, TPC, 6])
        mv = st.sb("mv", [P, TPC, 2])
        var = st.sb("var", [P, TPC])
        rstd = st.sb("rstd", [P, TPC])
        if base is not None:
            xbase = [st.sb(f"xbase{i}", [P, TPC, D]) for i in range(2)]
            xsum = st.sb("xsum", [P, TPC, D])
            res = [st.sb(f"res{i}", [P, TPC, D]) for i in range(2)]
            stats2 = st.sb("stats2", [P, TPC, 6])
            mv2 = [st.sb(f"mv2{i}", [P, TPC, 2]) for i in range(2)]
            var2 = [st.sb(f"var2{i}", [P, TPC]) for i in range(2)]
            rstd2 = [st.sb(f"rstd2{i}", [P, TPC]) for i in range(2)]
        turn_ps = [st.ps(f"turn{c}", [P, CH]) for c in range(DC)]
        a_ps = [st.ps(f"a_ps{i}", [P, CH]) for i in range(2)]
        g_ps = [st.ps(f"g_ps{i}", [P, CH]) for i in range(2)]
        y_ps = [st.ps(f"y_ps{j}", [P, 2, D]) for j in range(2)]

        const_in, set_, wg_done, lb_done = (st.sem(s) for s in ("const_in", "set", "wg_done", "lb_done"))
        bias_mm, bias_done = st.sem("bias_mm"), st.sem("bias_done")
        h_in = [st.sem(f"h_in{i}") for i in range(2)]
        x_in = [st.sem(f"x_in{i}") for i in range(2)]
        moments = st.sem("moments")
        rstd_done = st.sem("rstd_done")
        xn_done = st.sem("xn_done")
        turned = st.sem("turned")
        hT_done = st.sem("hT_done")
        ag_mm = st.sem("ag_mm")
        gelu_done = st.sem("gelu_done")
        gated = st.sem("gated")
        y_mm = st.sem("y_mm")
        xb_done = st.sem("xb_done")
        summed = st.sem("summed")
        added = st.sem("added")
        moments2 = st.sem("moments2")
        rstd2_done = st.sem("rstd2_done")
        normed = st.sem("normed")
        stored = [st.sem(f"stored{i}") for i in range(2)]
        zeros_out = st.sem("zeros_out")
        passed = st.sem("passed")
        blk = st.block()
        X_LOADS = 1 if base is None else 2

        @blk.sync
        def _(sp):
            sp.dma_start(w[:], w1.rearrange("(c p) n -> p c n", p=P)).then_inc(const_in, 16)
            sp.dma_start(b1[:], b1_col).then_inc(const_in, 16)
            sp.dma_start(b2[:], b2_row.to_broadcast([P, D])).then_inc(const_in, 16)
            sp.dma_start(lg[:], ln_g_col).then_inc(const_in, 16)
            sp.dma_start(lb[:], ln_b_col).then_inc(const_in, 16)
            sp.dma_start(idf[:], ident).then_inc(const_in, 16)
            sp.wait_ge(set_, 4)
            sp.dma_start(v[:, 0:MT - 1], w2[0:(MT - 1) * P].rearrange("(m p) n -> p m n", p=P)).then_inc(const_in, 16)
            sp.dma_start(v[0:M_ROWS[-1], MT - 1], w2[(MT - 1) * P:HID]).then_inc(const_in, 16)
            if base is None:
                sp.dma_start(dst[:, 0], zero[:]).then_inc(zeros_out, 16)

            def load(t, k, p):
                sp.wait_ge(xn_done, t * TPC + TPC)
                sp.sem_inc(passed, 1)
                for half in range(DC):
                    lo = 1 - half + p * CH
                    sp.dma_start(x[p][:, :, half * P:(half + 1) * P],
                                 src[k, lo:lo + CH, half * P:(half + 1) * P].rearrange("(a r) c -> r a c", r=P)
                                 ).then_inc(h_in[p], 16)
                sp.wait_ge(xb_done, t + 1)
                sp.sem_inc(passed, 1)
                rows = slice(1 + p * CH, 1 + (p + 1) * CH)
                sp.dma_start(xr[p][:], src[k, rows].rearrange("(a r) c -> r a c", r=P)).then_inc(x_in[p], 16)
                if base is not None:
                    sp.dma_start(xbase[p][:], base[k, rows].rearrange("(a r) c -> r a c", r=P)).then_inc(x_in[p], 16)

            def store(t, k, p):
                if base is None:
                    sp.wait_ge(added, t * 2 + 6)
                    place = dst[k, 1 + p * CH:1 + (p + 1) * CH]
                else:
                    sp.wait_ge(normed, t * TPC + 3 * TPC)
                    place = dst[k, p * CH:(p + 1) * CH]
                sp.sem_inc(passed, 1)
                sp.dma_start(place.rearrange("(a r) c -> r a c", r=P), out[p][:]).then_inc(stored[p], 16)

            pipelined(sp, NC, [(load, 0), (store, 3)])
            if base is None:
                sp.wait_ge(zeros_out, 16)
            for p in range(2):
                sp.wait_ge(stored[p], 16 * NC // 2 + 16)

        @blk.tensor
        def _(pe):
            pe.sem_inc(turned, 2 * DC)
            pe.sem_inc(ag_mm, 2 * AG)
            pe.sem_inc(y_mm, 2)
            pe.wait_ge(const_in, 16 * 8)
            pe.wait_ge(lb_done, 1)
            for i in range(AG):
                m, lo = i % MT, i // MT * HID + i % MT * P
                bank = a_ps[i % 2]
                if i > 1:
                    pe.wait_ge(bias_done, i - 1)
                for c in range(DC):
                    mm = pe.matmul(bank[0:M_ROWS[m], 0:64], w[:, c, lo:lo + M_ROWS[m]], lb_wide[:, c],
                                   start=(c == 0), stop=(c == DC - 1))
                mm.then_inc(bias_mm, 1)
            pe.wait_ge(bias_done, AG)
            pe.wait_ge(wg_done, DC)

            def turn(t, k, p):
                pe.wait_ge(xn_done, t * TPC + 3 * TPC)
                for c in range(DC):
                    pe.wait_ge(hT_done, t * DC + c + 1)
                    for a in range(TPC):
                        mm = pe.transpose(turn_ps[c][:, a * P:(a + 1) * P], xn[p][:, a, c * P:(c + 1) * P], idf[:])
                    mm.then_inc(turned, 1)

            def hidden(t, k, p):
                pe.wait_ge(hT_done, t * DC + 2 * DC)
                for m in range(MT):
                    pe.wait_ge(gated, t * MT + m + 1)
                    for bank, lo in ((g_ps[m % 2], HID + m * P), (a_ps[m % 2], m * P)):
                        for c in range(DC):
                            mm = pe.matmul(bank[0:M_ROWS[m], :], wg[:, c, lo:lo + M_ROWS[m]], hT[p][:, c],
                                           start=(c == 0), stop=(c == DC - 1))
                        mm.then_inc(ag_mm, 1)

            def project(t, k, p):
                pe.wait_ge(gated, t * MT + MT + 2)
                for j in range(2):
                    pe.wait_ge(added, t * 2 + j + 3)
                    for a in range(2):
                        for m in range(MT):
                            lo = (2 * j + a) * P
                            mm = pe.matmul(y_ps[j][:, a], hg[:, m, lo:lo + P], v[:, m],
                                           start=(m == 0), stop=(m == MT - 1))
                    mm.then_inc(y_mm, 1)

            pipelined(pe, NC, [(hidden, 1), (turn, 0), (project, 1)])

        @blk.scalar
        def _(act):
            act.sem_inc(hT_done, DC)
            act.wait_ge(bias_done, AG)

            def gelus(t, k, p):
                for m in range(MT):
                    act.wait_ge(ag_mm, t * AG + 2 * AG + 2 * m + 1)
                    act.wait_ge(gated, t * MT + m + 1)
                    act.activation(ge[m % 2][0:M_ROWS[m], :], g_ps[m % 2][0:M_ROWS[m], :], ACT.Gelu,
                                   bias=bias[0:M_ROWS[m], MT + m:MT + m + 1]).then_inc(gelu_done, 1)

            def copy_h(t, k, p):
                for c in range(DC):
                    act.wait_ge(turned, t * DC + c + 1 + 2 * DC)
                    act.wait_ge(ag_mm, t * AG + AG)
                    act.copy(hT[p][:, c], turn_ps[c][:]).then_inc(hT_done, 1)

            pipelined(act, NC, [(gelus, 1), (copy_h, 0)])

        @blk.gpsimd
        def _(pool):
            pool.sem_inc(xb_done, 2)
            for p in range(2):
                pool.sem_inc(stored[p], 16)
            pool.memset(zero[:], 0.0).then_inc(set_, 1)
            pool.memset(power[:], -0.5).then_inc(set_, 1)
            pool.memset(v[:, MT - 1], 0.0).then_inc(set_, 1)
            pool.memset(hg[:, MT - 1], 0.0).then_inc(set_, 1)
            pool.wait_ge(set_, 4)
            pool.wait_ge(const_in, 16 * 8)
            wide_b2 = b2[:].rearrange("r (a c) -> r a c", a=1).to_broadcast([P, TPC, D])

            def root(t, k, p):
                pool.wait_ge(moments, t * (2 * TPC + 1) + 2 * TPC + 1)
                if not (isinstance(t, int) and t == 0):
                    pool.wait_ge(xn_done, t * TPC + 2 * TPC)
                pool.tensor_tensor(rstd[:], var[:], power[:], ALU.pow).then_inc(rstd_done, 1)

            def add_bias(t, k, p):
                pool.wait_ge(x_in[p], k * 16 * X_LOADS + 16 * X_LOADS)
                pool.wait_ge(added, t * 2 + 2)
                if base is None:
                    pool.tensor_tensor(xb[p][:], xr[p][:], wide_b2, ALU.add).then_inc(xb_done, 1)
                else:
                    if not (isinstance(t, int) and t == 0):
                        pool.wait_ge(xb_done, t + 2)
                    pool.tensor_tensor(xsum[:], xr[p][:], wide_b2, ALU.add).then_inc(summed, 1)
                    pool.wait_ge(summed, t + 1)
                    pool.tensor_tensor(xb[p][:], xsum[:], xbase[p][:], ALU.add).then_inc(xb_done, 1)

            def root2(t, k, p):
                pool.wait_ge(moments2, t * (2 * TPC + 1) + 2 * TPC + 1)
                pool.tensor_tensor(rstd2[p][:], var2[p][:], power[:], ALU.pow).then_inc(rstd2_done, 1)

            pipelined(pool, NC, [(root, 0), (add_bias, 0)] + ([] if base is None else [(root2, 1)]))

        @blk.vector
        def _(ve):
            ve.sem_inc(xn_done, 2 * TPC)
            ve.sem_inc(gated, 2)
            ve.sem_inc(added, 4)
            ve.sem_inc(normed, 2 * TPC)
            ve.wait_ge(set_, 4)
            ve.wait_ge(const_in, 16 * 8)
            ve.tensor_copy(lb_wide[:], lb[:].rearrange("r (c o) -> r c o", o=1).to_broadcast([P, DC, 64])
                           ).then_inc(lb_done, 1)
            for c in range(DC):
                ve.tensor_scalar(wg[:, c], w[:, c], lg[:, c:c + 1], None, ALU.mult).then_inc(wg_done, 1)
            for i in range(AG):
                rows = slice(0, M_ROWS[i % MT])
                ve.wait_ge(bias_mm, i + 1)
                ve.tensor_tensor(bias[rows, i:i + 1], a_ps[i % 2][rows, 0:1], b1[rows, i:i + 1], ALU.add
                                 ).then_inc(bias_done, 1)
            ve.wait_ge(bias_done, AG)

            def measure(t, k, p):
                n = t * (2 * TPC + 1)
                ve.wait_ge(h_in[p], k * 32 + 32)
                for a in range(TPC):
                    ve.bn_stats(stats[:, a], x[p][:, a]).then_inc(moments, 1)
                ve.wait_ge(moments, n + TPC)
                ve.wait_ge(xn_done, t * TPC + 2 * TPC)
                ve.sem_inc(passed, 1)
                for a in range(TPC):
                    ve.bn_aggr(mv[:, a], stats[:, a]).then_inc(moments, 1)
                ve.wait_ge(moments, n + 2 * TPC)
                ve.tensor_scalar(var[:], mv[:, :, 1], EPS, None, ALU.add).then_inc(moments, 1)

            def normalise(t, k, p):
                ve.wait_ge(rstd_done, t + 1)
                ve.wait_ge(turned, t * DC + DC)
                for a in range(TPC):
                    ve.tensor_scalar(xn[p][:, a], x[p][:, a], mv[:, a, 0:1], rstd[:, a:a + 1],
                                     ALU.subtract, ALU.mult).then_inc(xn_done, 1)

            def gate(tiles):
                def fn(t, k, p):
                    ve.wait_ge(y_mm, t * 2 + 2)
                    for m in tiles:
                        rows = slice(0, M_ROWS[m])
                        ve.wait_ge(ag_mm, t * AG + 2 * AG + 2 * m + 2)
                        ve.wait_ge(gelu_done, t * MT + m + 1)
                        ve.scalar_tensor_tensor(out=hg[rows, m], in0=a_ps[m % 2][rows, :], scalar=bias[rows, m:m + 1],
                                                in1=ge[m % 2][rows, :], op0=ALU.add, op1=ALU.mult).then_inc(gated, 1)
                return fn

            def add(t, k, p):
                if base is None:
                    ve.wait_ge(stored[p], k * 16 + 16)
                else:
                    ve.wait_ge(normed, t * TPC + TPC)
                place = out[p] if base is None else res[p]
                for j in range(2):
                    ve.wait_ge(y_mm, t * 2 + j + 3)
                    ve.wait_ge(xb_done, t + 3)
                    ve.tensor_tensor(place[:, 2 * j:2 * j + 2], y_ps[j][:], xb[p][:, 2 * j:2 * j + 2], ALU.add
                                     ).then_inc(added, 1)

            def measure2(t, k, p):
                n = t * (2 * TPC + 1)
                for a in range(TPC):
                    ve.wait_ge(added, t * 2 + a // 2 + 5)
                    ve.bn_stats(stats2[:, a], res[p][:, a]).then_inc(moments2, 1)
                ve.wait_ge(moments2, n + TPC)
                ve.sem_inc(passed, 1)
                for a in range(TPC):
                    ve.bn_aggr(mv2[p][:, a], stats2[:, a]).then_inc(moments2, 1)
                ve.wait_ge(moments2, n + 2 * TPC)
                ve.tensor_scalar(var2[p][:], mv2[p][:, :, 1], EPS, None, ALU.add).then_inc(moments2, 1)

            def norm(t, k, p):
                ve.wait_ge(rstd2_done, t + 1)
                ve.wait_ge(stored[p], k * 16 + 16)
                for a in range(TPC):
                    ve.tensor_scalar(out[p][:, a], res[p][:, a], mv2[p][:, a, 0:1], rstd2[p][:, a:a + 1],
                                     ALU.subtract, ALU.mult).then_inc(normed, 1)

            steps = [(measure, 0), (gate(range(0, 3)), 1), (normalise, 0), (gate(range(3, MT)), 1), (add, 1)]
            if base is not None:
                steps = [(norm, 2)] + steps + [(measure2, 1)]
            pipelined(ve, NC, steps)


HC, EC = 2, D // 2
TM = 16
NS = L // TM
SQ = B // 4
REC = D + HC + HC * P


def step_rows(x, n):
    return x.rearrange("b (n t) c -> n b t c", t=TM)[n]


def ttt_project(nc, xs, down_w, down_b_col, wq, wk, wv, gain_row, shift_row, lr_wT, lr_b_row, tok_idx_row,
                inv_pos_row, causal, ident, kq, rec, xk, xq):
    with Stage(nc, "tp") as st:
        wd = st.sb("wd", [P, DC, D])
        wkq = st.sb("wkq", [P, DC, 2 * D])
        wvs = st.sb("wvs", [P, DC, D])
        wu = st.sb("wu", [P, DC, D + HC])
        db = st.sb("db", [P, DC])
        gain = st.sb("gain", [P, D])
        shift = st.sb("shift", [P, D])
        bias = st.sb("bias", [P, D + HC])
        idx = st.sb("idx", [P, TM])
        inv_pos = st.sb("inv_pos", [P, TM])
        last = st.sb("last", [P, 1])
        mask = st.sb("mask", [P, P])
        coef = st.sb("coef", [P, HC * P])
        idf = st.sb("idf", [P, P])
        x = [st.sb(f"x{i}", [P, TPC, D]) for i in range(2)]
        xT = st.sb("xT", [P, DC, CH])
        sg = st.sb("sg", [P, DC, CH])
        hT = [st.sb(f"hT{i}", [P, DC, CH]) for i in range(2)]
        kqT = [st.sb(f"kqT{i}", [P, 2 * HC, CH]) for i in range(2)]
        recs = [st.sb(f"recs{i}", [P, TPC, REC]) for i in range(2)]
        tk = [st.sb(f"tk{i}", [P, TPC, D]) for i in range(2)]
        tq = [st.sb(f"tq{i}", [P, TPC, D]) for i in range(2)]
        lr_raw = st.sb("lr_raw", [P, TPC, HC])
        lr_sg = st.sb("lr_sg", [P, TPC, HC])
        x_ps = [st.ps(f"x_ps{c}", [P, CH]) for c in range(DC)]
        m_ps = [st.ps(f"m_ps{i}", [P, CH]) for i in range(4)]
        g_ps = [st.ps(f"g_ps{i}", [P, 2, HC, P]) for i in range(2)]

        const_in, prep, wu_done = st.sem("const_in"), st.sem("prep"), st.sem("wu_done")
        x_in = [st.sem(f"x_in{i}") for i in range(2)]
        turned = st.sem("turned")
        xT_done = st.sem("xT_done")
        down_mm = st.sem("down_mm")
        sg_done = st.sem("sg_done")
        h_done = st.sem("h_done")
        kq_mm = st.sem("kq_mm")
        kq_done = st.sem("kq_done")
        gram_mm = st.sem("gram_mm")
        ct_done = st.sem("ct_done")
        u_mm = st.sem("u_mm")
        u_done = st.sem("u_done")
        lr_done = st.sem("lr_done")
        lr_sig = st.sem("lr_sig")
        lr_out = st.sem("lr_out")
        tok_mm = st.sem("tok_mm")
        tk_done = st.sem("tk_done")
        tq_done = st.sem("tq_done")
        stored = [st.sem(f"stored{i}") for i in range(2)]
        passed = st.sem("passed")
        blk = st.block()
        STORES = 4

        @blk.sync
        def _(sp):
            def halves(dst, w):
                return sp.dma_start(dst, w.rearrange("(c p) n -> p c n", p=P)).then_inc(const_in, 16)
            halves(wd[:], down_w)
            halves(wkq[:, :, 0:D], wk)
            halves(wkq[:, :, D:], wq)
            halves(wvs[:], wv)
            halves(wu[:, :, D:], lr_wT)
            for dst, row in ((gain[:], gain_row), (shift[:], shift_row), (bias[:, D:], lr_b_row),
                             (idx[:], tok_idx_row), (inv_pos[:], inv_pos_row)):
                sp.dma_start(dst, row.to_broadcast([P, row.shape[1]])).then_inc(const_in, 16)
            for dst, table in ((db, down_b_col), (mask, causal), (idf, ident)):
                sp.dma_start(dst[:], table).then_inc(const_in, 16)

            def load(t, k, p):
                sp.wait_ge(turned, t * DC + DC)
                sp.sem_inc(passed, 1)
                for a in range(TPC):
                    sp.dma_start(x[p][:, a], step_rows(xs, t * TPC + a)).then_inc(x_in[p], 16)

            def store(t, k, p):
                for done, count in ((kq_done, t * 4 + 4), (u_done, t * 4 + 4), (ct_done, t * 2 + 4),
                                    (lr_out, t + 2), (tk_done, t * 2 + 4), (tq_done, t * 2 + 4)):
                    sp.wait_ge(done, count)
                    sp.sem_inc(passed, 1)
                sp.dma_start(kq[t], kqT[p][:]).then_inc(stored[p], 16)
                for place, src in ((rec, recs), (xk, tk), (xq, tq)):
                    sp.dma_start(place.rearrange("(t a) r c -> t r a c", a=TPC)[t], src[p][:]).then_inc(stored[p], 16)

            pipelined(sp, NC, [(load, 0), (store, 3)])
            for p in range(2):
                sp.wait_ge(stored[p], 16 * STORES * (NC // 2 + 1))

        @blk.tensor
        def _(pe):
            pe.sem_inc(turned, 2 * DC)
            pe.sem_inc(down_mm, DC)
            pe.sem_inc(u_mm, 8)
            pe.sem_inc(tok_mm, 8)
            pe.wait_ge(const_in, 16 * 13)
            pe.wait_ge(wu_done, 2 * DC)

            def turn(t, k, p):
                pe.wait_ge(x_in[p], k * 64 + 64)
                for c in range(DC):
                    pe.wait_ge(h_done, t * DC + c + 1)
                    for a in range(TPC):
                        mm = pe.transpose(x_ps[c][:, a * P:(a + 1) * P], x[p][:, a, c * P:(c + 1) * P], idf[:])
                    mm.then_inc(turned, 1)

            def down(t, k, p):
                pe.wait_ge(xT_done, t * DC + DC)
                for m in range(DC):
                    for c in range(DC):
                        mm = pe.matmul(x_ps[m][:], wd[:, c, m * P:(m + 1) * P], xT[:, c],
                                       start=(c == 0), stop=(c == DC - 1))
                    mm.then_inc(down_mm, 1)

            def keys_queries(t, k, p):
                pe.wait_ge(h_done, t * DC + 2 * DC)
                for i in range(4):
                    if i < 2:
                        pe.wait_ge(tk_done, t * 2 + i + 1)
                    else:
                        pe.wait_ge(tq_done, t * 2 + i - 1)
                    for c in range(DC):
                        mm = pe.matmul(m_ps[i][:], wkq[:, c, i * P:(i + 1) * P], hT[p][:, c],
                                       start=(c == 0), stop=(c == DC - 1))
                    mm.then_inc(kq_mm, 1)

            def token_rows(t, k, p):
                for a in range(TPC):
                    pe.wait_ge(kq_done, t * 4 + a + 1)
                    for c in range(DC):
                        mm = pe.matmul(m_ps[a][:, 0:D + HC], hT[p][:, c, a * P:(a + 1) * P], wu[:, c],
                                       start=(c == 0), stop=(c == DC - 1))
                    mm.then_inc(u_mm, 1)

            def grams(t, k, p):
                for i in range(2):
                    pe.wait_ge(ct_done, t * 2 + i + 1)
                    for j in range(2):
                        for h in range(HC):
                            lo = (2 * i + j) * P
                            mm = pe.matmul(g_ps[i][:, j, h], kqT[p][:, h, lo:lo + P], kqT[p][:, HC + h, lo:lo + P],
                                           start=True, stop=True)
                    mm.then_inc(gram_mm, 1)

            def turn_back(t, k, p):
                for i in range(4):
                    which = i // 2
                    pe.wait_ge(u_done, t * 4 + i + 1)
                    pe.wait_ge(lr_done, t * 4 + i + 1)
                    for j in range(2):
                        for h in range(HC):
                            lo = (2 * (i % 2) + j) * P
                            mm = pe.transpose(m_ps[i][:, j * D + h * P:j * D + (h + 1) * P],
                                              kqT[p][:, HC * which + h, lo:lo + P], idf[:])
                    mm.then_inc(tok_mm, 1)

            pipelined(pe, NC, [(turn, 0), (keys_queries, 1), (down, 0), (token_rows, 1), (grams, 1), (turn_back, 1)])

        @blk.scalar
        def _(act):
            act.wait_ge(const_in, 16 * 13)

            def copy_x(t, k, p):
                for c in range(DC):
                    act.wait_ge(turned, t * DC + c + 1 + 2 * DC)
                    act.wait_ge(down_mm, t * DC + DC)
                    act.copy(xT[:, c], x_ps[c][:]).then_inc(xT_done, 1)

            def sigmoid(t, k, p):
                for m in range(DC):
                    act.wait_ge(down_mm, t * DC + DC + m + 1)
                    act.wait_ge(h_done, t * DC + m + 1)
                    act.activation(sg[:, m], x_ps[m][:], ACT.Sigmoid, bias=db[:, m:m + 1]).then_inc(sg_done, 1)

            def copy_kq(t, k, p):
                act.wait_ge(stored[p], (k + 1) * 16 * STORES)
                act.wait_ge(tok_mm, t * 4 + 4)
                for i in range(4):
                    act.wait_ge(kq_mm, t * 4 + i + 1)
                    act.copy(kqT[p][:, i], m_ps[i][:]).then_inc(kq_done, 1)

            def rates(t, k, p):
                act.wait_ge(lr_done, t * 4 + 4)
                act.wait_ge(lr_out, t + 1)
                act.activation(lr_sg[:], lr_raw[:], ACT.Sigmoid).then_inc(lr_sig, 1)

            pipelined(act, NC, [(copy_x, 0), (copy_kq, 1), (sigmoid, 0), (rates, 1)])

        @blk.vector
        def _(ve):
            ve.sem_inc(h_done, DC)
            ve.sem_inc(ct_done, 2)
            ve.sem_inc(lr_out, 1)
            ve.sem_inc(tk_done, 2)
            ve.sem_inc(tq_done, 2)
            for p in range(2):
                ve.sem_inc(stored[p], 16 * STORES)
            ve.wait_ge(const_in, 16 * 13)
            for c in range(DC):
                ve.tensor_tensor(wvs[:, c], wkq[:, c, 0:D], wvs[:, c], ALU.subtract).then_inc(wu_done, 1)
            ve.wait_ge(wu_done, DC)
            for c in range(DC):
                ve.tensor_tensor(wu[:, c, 0:D], wvs[:, c], gain[:], ALU.mult).then_inc(wu_done, 1)
            ve.tensor_tensor(bias[:, 0:D], shift[:], gain[:], ALU.mult).then_inc(prep, 1)
            ve.tensor_tensor(idx[:], idx[:], inv_pos[:], ALU.add).then_inc(prep, 1)
            ve.wait_ge(prep, 2)
            ve.tensor_scalar(idx[:], idx[:], 0.0, -1.0, ALU.max, ALU.mult).then_inc(prep, 1)
            ve.wait_ge(prep, 3)
            for h in range(HC):
                ve.tensor_tensor(coef[:, h * P:(h + 1) * P].rearrange("r (b i) -> r b i", b=B),
                                 mask[:].rearrange("r (b i) -> r b i", b=B),
                                 idx[:].rearrange("r (b i) -> r b i", b=1).to_broadcast([P, B, TM]), ALU.mult
                                 ).then_inc(prep, 1)
            ve.tensor_copy(last[:], idx[:, TM - 1:TM]).then_inc(prep, 1)
            ve.wait_ge(prep, 4 + HC)
            wide_coef = coef[:].rearrange("r (a n) -> r a n", a=1).to_broadcast([P, 2, HC * P])

            def gate(t, k, p):
                ve.wait_ge(u_mm, t * 4 + 4)
                for m in range(DC):
                    ve.wait_ge(sg_done, t * DC + m + 1)
                    ve.scalar_tensor_tensor(out=hT[p][:, m], in0=x_ps[m][:], scalar=db[:, m:m + 1], in1=sg[:, m],
                                            op0=ALU.add, op1=ALU.mult).then_inc(h_done, 1)

            def copy_u(t, k, p):
                ve.wait_ge(stored[p], (k + 1) * 16 * STORES)
                ve.wait_ge(lr_out, t + 1)
                for a in range(TPC):
                    ve.wait_ge(u_mm, t * 4 + a + 9)
                    ve.tensor_tensor(recs[p][:, a, 0:D], m_ps[a][:, 0:D], bias[:, 0:D], ALU.add).then_inc(u_done, 1)
                    ve.tensor_tensor(lr_raw[:, a], m_ps[a][:, D:D + HC], bias[:, D:], ALU.add).then_inc(lr_done, 1)

            def coefs(t, k, p):
                for i in range(2):
                    ve.wait_ge(gram_mm, t * 2 + i + 1)
                    ve.scalar_tensor_tensor(
                        out=recs[p][:, 2 * i:2 * i + 2, D + HC:],
                        in0=g_ps[i][:].rearrange("r a h n -> r a (h n)"), scalar=1.0, in1=wide_coef,
                        op0=ALU.add, op1=ALU.mult).then_inc(ct_done, 1)

            def copy_k(t, k, p):
                ve.wait_ge(lr_sig, t + 1)
                ve.tensor_scalar(recs[p][:, :, D:D + HC], lr_sg[:], 1.0 / EC, None, ALU.mult).then_inc(lr_out, 1)
                for i in range(2):
                    ve.wait_ge(tok_mm, t * 4 + i + 9)
                    ve.sem_inc(passed, 1)
                    ve.tensor_scalar(tk[p][:, 2 * i:2 * i + 2].rearrange("r a c -> r (a c)"), m_ps[i][:],
                                     last[:], None, ALU.mult).then_inc(tk_done, 1)

            def copy_q(t, k, p):
                for i in range(2):
                    ve.wait_ge(tok_mm, t * 4 + i + 11)
                    ve.tensor_tensor(tq[p][:, 2 * i:2 * i + 2], m_ps[2 + i][:].rearrange("r (a c) -> r a c", a=2),
                                     shift[:].rearrange("r (a c) -> r a c", a=1).to_broadcast([P, 2, D]), ALU.add
                                     ).then_inc(tq_done, 1)

            pipelined(ve, NC, [(gate, 0), (copy_u, 1), (coefs, 1), (copy_k, 1), (copy_q, 1)])


TTT_EPS = 1e-6
OPS = 11


def ttt_scan(nc, kq, rec, xk, w_first, b_first_row, gain_row, tok_idx_row, inv_pos_row, same_seq, ident, z1):
    with Stage(nc, "ts") as st:
        gain2 = st.sb("gain2", [P, HC, P])
        idx = st.sb("idx", [P, TM])
        inv_pos = st.sb("inv_pos", [P, TM])
        spread = st.sb("spread", [P, P])
        idf = st.sb("idf", [P, P])
        power = st.sb("power", [P, 1])
        kqc = [st.sb(f"kqc{i}", [P, 2 * HC, P]) for i in range(2)]
        kqp = [st.sb(f"kqp{i}", [P, 2 * HC * 4, 2 * 32]) for i in range(2)]
        rc = [st.sb(f"rc{i}", [P, REC]) for i in range(2)]
        xkm = [st.sb(f"xkm{i}", [P, B, D]) for i in range(2)]
        ws = [st.sb(f"ws{h}", [P, B, P]) for h in range(HC)]
        bs = [[st.sb(f"bs{i}{h}", [P, P]) for h in range(HC)] for i in range(2)]
        z, zc, g2, gy, junk, gw, grad = ([st.sb(f"{s}{h}", [P, P]) for h in range(HC)]
                                         for s in ("z", "zc", "g2", "gy", "junk", "gw", "grad"))
        stats = [st.sb(f"stats{h}", [P, 6]) for h in range(HC)]
        mv = [st.sb(f"mv{h}", [P, 2]) for h in range(HC)]
        var, rstd, s1, s2, rr, rate, mean1, q2 = (
            [st.sb(f"{s}{h}", [P, 1]) for h in range(HC)]
            for s in ("var", "rstd", "s1", "s2", "rr", "rate", "mean1", "q2"))
        out = [st.sb(f"out{i}", [P, HC, P]) for i in range(2)]
        w_ps = [[st.ps(f"w_ps{h}{i}", [P, CH]) for i in range(2)] for h in range(HC)]
        k_ps = [st.ps(f"k_ps{h}", [P, P]) for h in range(HC)]
        q_ps = [st.ps(f"q_ps{h}", [P, 2, P]) for h in range(HC)]

        const_in, set_, prep = st.sem("const_in"), st.sem("set"), st.sem("prep")
        kq_in = [st.sem(f"kq_in{i}") for i in range(2)]
        rec_in = [st.sem(f"rec_in{i}") for i in range(2)]
        xk_in = [st.sem(f"xk_in{i}") for i in range(2)]
        kq_spread = st.sem("kq_spread")
        z_mm = [st.sem(f"z_mm{h}") for h in range(HC)]
        d = [st.sem(f"d{h}") for h in range(HC)]
        rstd_done = [st.sem(f"rstd_done{h}") for h in range(HC)]
        w_mm = [st.sem(f"w_mm{h}") for h in range(HC)]
        w_done = [st.sem(f"w_done{h}") for h in range(HC)]
        zc_done = [st.sem(f"zc_done{h}") for h in range(HC)]
        rates_done = [st.sem(f"rates_done{h}") for h in range(HC)]
        b_done = [st.sem(f"b_done{h}") for h in range(HC)]
        c_mm = [st.sem(f"c_mm{h}") for h in range(HC)]
        z1_done = [st.sem(f"z1_done{h}") for h in range(HC)]
        stored = [st.sem(f"stored{i}") for i in range(2)]
        passed = st.sem("passed")
        blk = st.block()
        CONSTS = 16 * (HC * B + 7)

        @blk.sync
        def _(sp):
            for h in range(HC):
                for s in range(B):
                    sp.dma_start(ws[h][:, s], w_first[h]).then_inc(const_in, 16)
            sp.dma_start(gain2[:].rearrange("r h g -> r (h g)"), gain_row.to_broadcast([P, D])).then_inc(const_in, 16)
            for h in range(HC):
                sp.dma_start(bs[0][h][:], b_first_row[:, h * P:(h + 1) * P].to_broadcast([P, P])
                             ).then_inc(const_in, 16)
            for dst, r in ((idx[:], tok_idx_row), (inv_pos[:], inv_pos_row)):
                sp.dma_start(dst, r.to_broadcast([P, TM])).then_inc(const_in, 16)
            for dst, table in ((spread, same_seq), (idf, ident)):
                sp.dma_start(dst[:], table).then_inc(const_in, 16)
            sp.wait_ge(set_, 5)

            def load_kq(t, k, p):
                sp.wait_ge(kq_spread, t + 1)
                sp.sem_inc(passed, 1)
                sp.dma_start(kqc[p][:], kq[k // 2][:, :, bass.ds((k % 2) * 2 * P + p * P, P)]).then_inc(kq_in[p], 16)

            def load_rest(t, k, p):
                for h in range(HC):
                    sp.wait_ge(c_mm[h], t + 1)
                    sp.sem_inc(passed, 1)
                sp.dma_start(rc[p][:], rec[t]).then_inc(rec_in[p], 16)
                for s in range(B):
                    rows = slice(s * TM, (s + 1) * TM)
                    sp.dma_start(xkm[p][rows, s], xk[t, rows]).then_inc(xk_in[p], 16)

            def store(t, k, p):
                for h in range(HC):
                    sp.wait_ge(z1_done[h], t + 2)
                    sp.sem_inc(passed, 1)
                sp.dma_start(z1[t], out[p][:].rearrange("r h g -> r (h g)")).then_inc(stored[p], 16)

            pipelined(sp, NS, [(load_kq, 0), (load_rest, 0), (store, 3)])
            for p in range(2):
                sp.wait_ge(stored[p], 16 * NS // 2 + 16)

        @blk.tensor
        def _(pe):
            for h in range(HC):
                pe.sem_inc(c_mm[h], 2)
            pe.wait_ge(const_in, CONSTS)
            pe.wait_ge(prep, 5)

            def products(h):
                def fn(t, k, p):
                    pe.wait_ge(kq_spread, t + 3)
                    if not (isinstance(t, int) and t == 0):
                        pe.wait_ge(w_done[h], t * 2)
                    if not (isinstance(t, int) and t == 0):
                        pe.wait_ge(d[h], t * OPS)
                    for which, z_out in ((0, k_ps[h][:]), (1, q_ps[h][:, 0])):
                        if which == 1:
                            pe.wait_ge(z1_done[h], t + 1)
                            if not (isinstance(t, int) and t == 0):
                                pe.wait_ge(b_done[h], t)
                        for half in range(SQ):
                            for q in range(4):
                                mm = pe.matmul(z_out[32 * q:32 * q + 32, :],
                                               kqp[p][:, (which * HC + h) * 4 + q, half * 32:half * 32 + 32],
                                               ws[h][:, SQ * q + half],
                                               start=(half == 0), stop=(which == 0 and half == SQ - 1))
                        if which == 0:
                            mm.then_inc(z_mm[h], 1)
                return fn

            def updates(h):
                def fn(t, k, p):
                    pe.wait_ge(xk_in[p], k * 16 * B + 16 * B)
                    pe.wait_ge(d[h], t * OPS + OPS)
                    for i in range(2):
                        for s in range(4):
                            mm = pe.matmul(w_ps[h][i][:, s * P:(s + 1) * P], xkm[p][:, 4 * i + s, h * P:(h + 1) * P],
                                           grad[h][:], start=True, stop=True)
                        mm.then_inc(w_mm[h], 1)
                    pe.matmul(q_ps[h][:, 0], rc[p][:, D + HC + h * P:D + HC + (h + 1) * P], grad[h][:],
                              start=False, stop=False)
                    pe.matmul(q_ps[h][:, 0], idf[:], bs[p][h][:], start=False, stop=True)
                    pe.matmul(q_ps[h][:, 1], spread[:], grad[h][:], start=True, stop=True).then_inc(c_mm[h], 1)
                return fn

            pipelined(pe, NS, [(products(0), 1), (updates(1), 2), (products(1), 1), (updates(0), 1)])

        @blk.scalar
        def _(act):
            act.sem_inc(kq_spread, 2)
            for h in range(HC):
                act.sem_inc(z1_done[h], 1)
            act.wait_ge(set_, 5)

            def spread_kq(t, k, p):
                act.wait_ge(kq_in[p], k * 16 + 16)
                for h in range(HC):
                    if not (isinstance(t, int) and t < 2):
                        act.wait_ge(c_mm[h], t + 1)
                src = kqc[p][:].rearrange("r w (q a t) -> r (w q) a t", q=4, a=SQ)
                for a in range(SQ):
                    inst = act.copy(kqp[p][:, :, a * 48:a * 48 + TM], src[:, :, a])
                inst.then_inc(kq_spread, 1)

            def centre(h):
                def fn(t, k, p):
                    act.wait_ge(d[h], t * OPS + 3)
                    act.activation(zc[h][:], z[h][:], ACT.Identity, bias=mv[h][:, 0:1], scale=-1.0
                                   ).then_inc(zc_done[h], 1)
                return fn

            def result(h):
                def fn(t, k, p):
                    act.wait_ge(stored[p], k * 16 + 16)
                    act.wait_ge(c_mm[h], t + 3)
                    act.wait_ge(b_done[h], t + 1)
                    act.copy(out[p][:, h], q_ps[h][:, 0]).then_inc(z1_done[h], 1)
                return fn

            pipelined(act, NS, [(centre(0), 1), (result(1), 2), (spread_kq, 0), (centre(1), 1), (result(0), 1)])

        @blk.gpsimd
        def _(pool):
            for p in range(2):
                pool.sem_inc(stored[p], 16)
            pool.memset(power[:], -0.5).then_inc(set_, 1)
            for p in range(2):
                pool.memset(kqp[p][:], 0.0).then_inc(set_, 1)
                pool.memset(xkm[p][:], 0.0).then_inc(set_, 1)
            pool.wait_ge(set_, 5)

            def root(h):
                def fn(t, k, p):
                    pool.wait_ge(d[h], t * OPS + 4)
                    pool.tensor_tensor(rstd[h][:], var[h][:], power[:], ALU.pow).then_inc(rstd_done[h], 1)
                    pool.wait_ge(rec_in[p], k * 16 + 16)
                    pool.wait_ge(rstd_done[h], t + 1)
                    pool.tensor_tensor(rate[h][:], rstd[h][:], rc[p][:, D + h:D + h + 1], ALU.mult
                                       ).then_inc(rates_done[h], 1)
                    pool.tensor_tensor(rr[h][:], rstd[h][:], rstd[h][:], ALU.mult).then_inc(rates_done[h], 1)
                return fn

            pipelined(pool, NS, [(root(0), 1), (root(1), 1)])

        @blk.vector
        def _(ve):
            ve.wait_ge(const_in, CONSTS)
            ve.tensor_tensor(gain2[:], gain2[:], gain2[:], ALU.mult).then_inc(prep, 1)
            ve.tensor_tensor(idx[:], idx[:], inv_pos[:], ALU.add).then_inc(prep, 1)
            ve.wait_ge(prep, 2)
            ve.tensor_scalar(idx[:], idx[:], 0.0, -1.0, ALU.max, ALU.mult).then_inc(prep, 1)
            ve.wait_ge(prep, 3)
            ve.tensor_scalar(spread[:], spread[:], idx[:, TM - 1:TM], None, ALU.mult).then_inc(prep, 1)
            ve.sem_inc(prep, 1)

            def gradient(h):
                def fn(t, k, p):
                    def after(op):
                        ve.wait_ge(d[h], t * OPS + op)
                    u = rc[p][:, h * P:(h + 1) * P]
                    ve.wait_ge(z_mm[h], t + 1)
                    if not (isinstance(t, int) and t == 0):
                        ve.wait_ge(b_done[h], t)
                        after(0)
                    ve.tensor_tensor(z[h][:], k_ps[h][:], bs[p][h][:], ALU.add).then_inc(d[h], 1)
                    after(1)
                    ve.bn_stats(stats[h][:], z[h][:]).then_inc(d[h], 1)
                    after(2)
                    ve.sem_inc(passed, 1)
                    ve.bn_aggr(mv[h][:], stats[h][:]).then_inc(d[h], 1)
                    after(3)
                    ve.tensor_scalar(var[h][:], mv[h][:, 1:2], TTT_EPS, None, ALU.add).then_inc(d[h], 1)
                    ve.scalar_tensor_tensor(out=g2[h][:], in0=z[h][:], scalar=mv[h][:, 0:1], in1=gain2[:, h],
                                            op0=ALU.subtract, op1=ALU.mult).then_inc(d[h], 1)
                    ve.wait_ge(rstd_done[h], t + 1)
                    ve.wait_ge(rec_in[p], k * 16 + 16)
                    after(5)
                    ve.sem_inc(passed, 1)
                    ve.scalar_tensor_tensor(out=gy[h][:], in0=g2[h][:], scalar=rstd[h][:], in1=u, op0=ALU.mult,
                                            op1=ALU.add, accum_out=s1[h][:]).then_inc(d[h], 1)
                    ve.wait_ge(zc_done[h], t + 1)
                    after(6)
                    ve.sem_inc(passed, 1)
                    ve.tensor_tensor_reduce(out=junk[h][:], in0=gy[h][:], in1=zc[h][:], scale=-1.0 / EC, scalar=0.0,
                                            op0=ALU.mult, op1=ALU.add, accum_out=s2[h][:]).then_inc(d[h], 1)
                    ve.tensor_scalar(mean1[h][:], s1[h][:], 1.0 / EC, None, ALU.mult).then_inc(d[h], 1)
                    ve.wait_ge(rates_done[h], t * 2 + 2)
                    after(7)
                    ve.tensor_tensor(q2[h][:], s2[h][:], rr[h][:], ALU.mult).then_inc(d[h], 1)
                    after(9)
                    ve.scalar_tensor_tensor(out=gw[h][:], in0=zc[h][:], scalar=q2[h][:], in1=gy[h][:], op0=ALU.mult,
                                            op1=ALU.add).then_inc(d[h], 1)
                    after(10)
                    ve.tensor_scalar(grad[h][:], gw[h][:], mean1[h][:], rate[h][:], ALU.subtract, ALU.mult
                                     ).then_inc(d[h], 1)
                return fn

            def next_state(h):
                def fn(t, k, p):
                    for i in range(2):
                        ve.wait_ge(w_mm[h], t * 2 + i + 1)
                        part = ws[h][:, 4 * i:4 * i + 4].rearrange("r s g -> r (s g)")
                        ve.tensor_tensor(part, w_ps[h][i][:], part, ALU.add).then_inc(w_done[h], 1)
                    ve.wait_ge(c_mm[h], t + 3)
                    ve.tensor_tensor(bs[1 - p][h][:], q_ps[h][:, 1], bs[p][h][:], ALU.add).then_inc(b_done[h], 1)
                return fn

            ve.wait_ge(prep, 5)
            pipelined(ve, NS, [(gradient(0), 1), (next_state(1), 2), (gradient(1), 1), (next_state(0), 1)])


RANK = 32
GROUPS = [HC, 1, 1, 1, 1]
NORM_EPS = [TTT_EPS, EPS, EPS, EPS, EPS]
PROJ = (3, 2, 1)


def ttt_close(nc, z1, xq, xs, gain_row, post_w_col, post_b_col, wo, ln_w_col, ln_b_col, up_w, up_b_row,
              w_lastT, b_last_row, v_rT, c_T, ident, y):
    with Stage(nc, "tc") as st:
        w = [None] + [st.sb(f"w{i}", [P, DC, D]) for i in (1, 2, 3)]
        raw = [st.sb(f"raw{i}", [P, DC, D]) for i in range(2)]
        col = st.sb("col", [P, 4, DC])
        wide = st.sb("wide", [P, 2, DC, P])
        bias = [st.sb(f"bias{i}", [P, D]) for i in range(3)]
        gain = st.sb("gain", [P, D])
        vt = st.sb("vt", [P, D])
        ct = st.sb("ct", [P, D])
        idf = st.sb("idf", [P, P])
        power = st.sb("power", [P, TPC * HC])
        z_in_sb = [st.sb(f"z{i}", [P, TPC, D]) for i in range(2)]
        q_sb = [st.sb(f"q{i}", [P, TPC, D]) for i in range(2)]
        x_sb = [st.sb(f"x{i}", [P, TPC, D]) for i in range(2)]
        xb = st.sb("xb", [P, TPC, D])
        yb = st.sb("yb", [P, TPC, D])
        scaled = st.sb("scaled", [P, TPC, D])
        r = [None] + [st.sb(f"r{i}", [P, TPC, D]) for i in range(1, 5)]
        n = [st.sb(f"n{i}", [P, TPC, D]) for i in range(4)]
        out = [st.sb(f"out{i}", [P, TPC, D]) for i in range(2)]
        xT = [None] + [st.sb(f"xT{i}", [P, DC, CH]) for i in (1, 2, 3)]
        stats = [st.sb(f"stats{i}", [P, TPC * g, 6]) for i, g in enumerate(GROUPS)]
        mv = [st.sb(f"mv{i}", [P, TPC * g, 2]) for i, g in enumerate(GROUPS)]
        var, rstd, nb = ([st.sb(f"{s}{i}", [P, TPC * g]) for i, g in enumerate(GROUPS)] for s in ("var", "rstd", "nb"))
        turn_ps = [st.ps(f"turn{c}", [P, CH]) for c in range(DC)]
        y_ps = [None] + [[st.ps(f"y{i}{j}", [P, 2, D]) for j in range(2)] for i in (1, 2, 3)]

        const_in, set_, prep, bias_mm, bias_done = (
            st.sem(s) for s in ("const_in", "set", "prep", "bias_mm", "bias_done"))
        z_in, q_in, x_in, stored = ([st.sem(f"{s}{i}") for i in range(2)] for s in ("z_in", "q_in", "x_in", "stored"))
        G = [TPC * g for g in GROUPS]
        measured = [st.sem(f"measured{i}") for i in range(5)]
        rooted = [st.sem(f"rooted{i}") for i in range(5)]
        nb_done = [st.sem(f"nb_done{i}") for i in range(5)]
        normed = [st.sem(f"normed{i}") for i in range(5)]
        scaled_done = st.sem("scaled_done")
        summed = [None] + [st.sem(f"summed{i}") for i in range(1, 5)]
        xb_done = st.sem("xb_done")
        yb_done = st.sem("yb_done")
        turned = [None] + [st.sem(f"turned{i}") for i in (1, 2, 3)]
        copied = [None] + [st.sem(f"copied{i}") for i in (1, 2, 3)]
        y_mm = [None] + [st.sem(f"y_mm{i}") for i in (1, 2, 3)]
        passed = st.sem("passed")
        blk = st.block()
        CONSTS = 16 * 15

        def groups(tile_, i):
            return tile_[:].rearrange("r a (h c) -> r (a h) c", h=GROUPS[i])

        @blk.sync
        def _(sp):
            for dst, m in ((raw[0], wo), (raw[1], up_w), (w[3], w_lastT)):
                sp.dma_start(dst[:], m.rearrange("(c p) n -> p c n", p=P)).then_inc(const_in, 16)
            for i, c in enumerate((post_w_col, post_b_col, ln_w_col, ln_b_col)):
                sp.dma_start(col[:, i], c).then_inc(const_in, 16)
            for dst, row in ((bias[1], up_b_row), (bias[2], b_last_row), (gain, gain_row)):
                sp.dma_start(dst[:], row.to_broadcast([P, D])).then_inc(const_in, 16)
            sp.dma_start(idf[:], ident).then_inc(const_in, 16)
            sp.wait_ge(set_, 4)
            sp.dma_start(vt[0:RANK, :], v_rT).then_inc(const_in, 16)
            sp.dma_start(ct[0:RANK, :], c_T).then_inc(const_in, 16)
            sp.sem_inc(const_in, 2 * 16)

            def load_z(t, k, p):
                sp.wait_ge(normed[0], t * G[0] + G[0])
                sp.sem_inc(passed, 1)
                sp.dma_start(z_in_sb[p][:], z1.rearrange("(t a) r c -> t r a c", a=TPC)[t]).then_inc(z_in[p], 16)
                sp.wait_ge(summed[1], t * 2 + 2)
                sp.sem_inc(passed, 1)
                sp.dma_start(q_sb[p][:], xq.rearrange("(t a) r c -> t r a c", a=TPC)[t]).then_inc(q_in[p], 16)

            def load_x(t, k, p):
                sp.wait_ge(xb_done, t + 1)
                sp.sem_inc(passed, 1)
                for a in range(TPC):
                    sp.dma_start(x_sb[p][:, a], step_rows(xs, t * TPC + a)).then_inc(x_in[p], 16)

            def store(t, k, p):
                sp.wait_ge(normed[4], t * G[4] + 3 * G[4])
                sp.sem_inc(passed, 1)
                for a in range(TPC):
                    sp.dma_start(step_rows(y, t * TPC + a), out[p][:, a]).then_inc(stored[p], 16)

            pipelined(sp, NC, [(load_z, 0), (load_x, 2), (store, 5)])
            for p in range(2):
                sp.wait_ge(stored[p], 64 * NC // 2 + 64)

        @blk.tensor
        def _(pe):
            for i in PROJ:
                pe.sem_inc(turned[i], DC)
                pe.sem_inc(y_mm[i], 2)
            pe.wait_ge(const_in, CONSTS)
            pe.wait_ge(prep, 5)
            for i in range(2):
                for c in range(DC):
                    mm = pe.matmul(y_ps[1 + i][0][:, 0], wide[:, i, c], raw[i][:, c], start=(c == 0), stop=(c == DC - 1))
                mm.then_inc(bias_mm, 1)
            for c in range(DC):
                pe.matmul(y_ps[3][c][:, 0], vt[:, c * P:(c + 1) * P], ct[:], start=True, stop=True).then_inc(bias_mm, 1)
            pe.wait_ge(bias_done, 4)

            def turn(i):
                def fn(t, k, p):
                    s = t + i
                    if isinstance(t, int):
                        for j in PROJ:
                            chunk = min(s - j if j > i else s - 1 - j, NC - 1)
                            if chunk >= 0:
                                pe.wait_ge(copied[j], chunk * DC + DC)
                    else:
                        j = i + 1 if i < 3 else 1
                        pe.wait_ge(copied[j], t * DC + (i - j if j > i else i - 1 - j) * DC + DC)
                    pe.wait_ge(normed[i], t * G[i] + 3 * G[i])
                    for c in range(DC):
                        for a in range(TPC):
                            mm = pe.transpose(turn_ps[c][:, a * P:(a + 1) * P], n[i][:, a, c * P:(c + 1) * P], idf[:])
                        mm.then_inc(turned[i], 1)
                return fn

            def product(i):
                def fn(t, k, p):
                    pe.wait_ge(copied[i], t * DC + DC)
                    for j in range(2):
                        pe.wait_ge(summed[i + 1], t * 2 + j + 3)
                        for a in range(2):
                            for c in range(DC):
                                lo = (2 * j + a) * P
                                mm = pe.matmul(y_ps[i][j][:, a], xT[i][:, c, lo:lo + P], w[i][:, c],
                                               start=(c == 0), stop=(c == DC - 1))
                        mm.then_inc(y_mm[i], 1)
                return fn

            pipelined(pe, NC, [(turn(3), 3), (turn(2), 2), (product(3), 3), (turn(1), 1), (product(2), 2),
                               (product(1), 1)])

        @blk.scalar
        def _(act):
            for i in range(5):
                act.sem_inc(normed[i], 2 * G[i])

            def apply(i):
                def fn(t, k, p):
                    act.wait_ge(nb_done[i], t + 2)
                    if i == 0:
                        act.wait_ge(scaled_done, t + 1)
                    elif i == 4:
                        act.wait_ge(stored[p], k * 64 + 64)
                    else:
                        act.wait_ge(turned[i], t * DC + DC)
                    if i == 3:
                        act.wait_ge(yb_done, t + 1)
                    src, dst = (z_in_sb[p] if i == 0 else r[i]), (out[p] if i == 4 else n[i])
                    for g in range(G[i]):
                        act.activation(groups(dst, i)[:, g], groups(src, i)[:, g], ACT.Identity,
                                       bias=nb[i][:, g:g + 1], scale=rstd[i][:, g:g + 1]).then_inc(normed[i], 1)
                return fn

            def copy(i):
                def fn(t, k, p):
                    act.wait_ge(y_mm[i], t * 2 + 2)
                    for c in range(DC):
                        act.wait_ge(turned[i], t * DC + c + 1 + DC)
                        act.copy(xT[i][:, c], turn_ps[c][:]).then_inc(copied[i], 1)
                return fn

            pipelined(act, NC, [(apply(4), 4), (apply(3), 3), (apply(2), 2), (copy(3), 3), (apply(1), 1),
                                (copy(2), 2), (apply(0), 0), (copy(1), 1)])

        @blk.gpsimd
        def _(pool):
            pool.sem_inc(xb_done, 2)
            pool.sem_inc(yb_done, 1)
            for p in range(2):
                pool.sem_inc(stored[p], 64)
            pool.memset(power[:], -0.5).then_inc(set_, 1)
            pool.memset(vt[:], 0.0).then_inc(set_, 1)
            pool.memset(ct[:], 0.0).then_inc(set_, 1)
            pool.sem_inc(set_, 1)
            pool.wait_ge(set_, 4)
            pool.wait_ge(const_in, CONSTS)
            pool.wait_ge(bias_done, 4)

            def wide_row(tile_):
                return tile_[:].rearrange("r (a c) -> r a c", a=1).to_broadcast([P, TPC, D])

            def root(i):
                def fn(t, k, p):
                    pool.wait_ge(measured[i], t * (2 * G[i] + 1) + 2 * G[i] + 1)
                    pool.wait_ge(normed[i], t * G[i] + 2 * G[i])
                    pool.tensor_tensor(rstd[i][:], var[i][:], power[:, 0:G[i]], ALU.pow).then_inc(rooted[i], 1)
                return fn

            def residual(t, k, p):
                pool.wait_ge(x_in[p], k * 64 + 64)
                pool.wait_ge(summed[3], t * 2 + 4)
                pool.tensor_tensor(xb[:], x_sb[p][:], wide_row(bias[1]), ALU.add).then_inc(xb_done, 1)

            def residual_last(t, k, p):
                pool.wait_ge(normed[3], t * G[3] + 3 * G[3])
                pool.wait_ge(summed[4], t * 2 + 4)
                pool.tensor_tensor(yb[:], n[3][:], wide_row(bias[2]), ALU.add).then_inc(yb_done, 1)

            pipelined(pool, NC, [(root(4), 4), (root(3), 3), (root(2), 2), (root(1), 1), (root(0), 0),
                                 (residual, 2), (residual_last, 3)])

        @blk.vector
        def _(ve):
            for i in range(5):
                ve.sem_inc(nb_done[i], 1)
            for i in range(1, 5):
                ve.sem_inc(summed[i], 4)
            ve.sem_inc(scaled_done, 1)
            ve.wait_ge(const_in, CONSTS)
            for i in range(2):
                for c in range(DC):
                    ve.tensor_scalar(w[1 + i][:, c], raw[i][:, c], col[:, 2 * i, c:c + 1], None, ALU.mult
                                     ).then_inc(prep, 1)
            ve.tensor_copy(wide[:], col[:, 1:4:2].rearrange("r i (c o) -> r i c o", o=1).to_broadcast([P, 2, DC, P])
                           ).then_inc(prep, 1)
            ve.wait_ge(bias_mm, 4)
            ve.tensor_copy(bias[0][:], y_ps[1][0][:, 0]).then_inc(bias_done, 1)
            ve.tensor_tensor(bias[1][:], y_ps[2][0][:, 0], bias[1][:], ALU.add).then_inc(bias_done, 1)
            for c in range(DC):
                ve.tensor_tensor(w[3][:, c], y_ps[3][c][:, 0], w[3][:, c], ALU.add).then_inc(bias_done, 1)
            ve.wait_ge(bias_done, 4)
            wide_gain = gain[:].rearrange("r (a c) -> r a c", a=1).to_broadcast([P, TPC, D])
            wide_bias = bias[0][:].rearrange("r (a c) -> r a c", a=1).to_broadcast([P, 2, D])

            def measure(i):
                def fn(t, k, p):
                    base = t * (2 * G[i] + 1)
                    if i == 0:
                        ve.wait_ge(z_in[p], k * 16 + 16)
                    elif i == 1:
                        ve.wait_ge(normed[0], t * G[0] + 3 * G[0])
                        ve.wait_ge(summed[1], t * 2 + 4)
                        ve.tensor_tensor(scaled[:], n[0][:], wide_gain, ALU.mult).then_inc(scaled_done, 1)
                        ve.wait_ge(scaled_done, t + 2)
                        ve.wait_ge(q_in[p], k * 16 + 16)
                    if i > 0:
                        ve.wait_ge(normed[i], t * G[i] + 2 * G[i])
                    if i == 3:
                        ve.wait_ge(xb_done, t + 3)
                    if i == 4:
                        ve.wait_ge(yb_done, t + 2)
                    if i > 0:
                        for j in range(2):
                            part = slice(2 * j, 2 * j + 2)
                            if i > 1:
                                ve.wait_ge(y_mm[i - 1], t * 2 + j + 3)
                            a = scaled[:, part] if i == 1 else y_ps[i - 1][j][:]
                            b = (q_sb[p][:, part], wide_bias, xb[:, part], yb[:, part])[i - 1]
                            ve.tensor_tensor(r[i][:, part], a, b, ALU.add).then_inc(summed[i], 1)
                    ve.wait_ge(nb_done[i], t + 1)
                    src = groups(z_in_sb[p] if i == 0 else r[i], i)
                    for g in range(G[i]):
                        if i > 0 and g % 2 == 0:
                            ve.wait_ge(summed[i], t * 2 + g // 2 + 5)
                        ve.bn_stats(stats[i][:, g], src[:, g]).then_inc(measured[i], 1)
                    ve.wait_ge(measured[i], base + G[i])
                    ve.sem_inc(passed, 1)
                    for g in range(G[i]):
                        ve.bn_aggr(mv[i][:, g], stats[i][:, g]).then_inc(measured[i], 1)
                    ve.wait_ge(measured[i], base + 2 * G[i])
                    ve.tensor_scalar(var[i][:], mv[i][:, :, 1], NORM_EPS[i], None, ALU.add).then_inc(measured[i], 1)
                return fn

            def offset(i):
                def fn(t, k, p):
                    ve.wait_ge(rooted[i], t + 1)
                    ve.wait_ge(normed[i], t * G[i] + 2 * G[i])
                    ve.sem_inc(passed, 1)
                    ve.scalar_tensor_tensor(out=nb[i][:], in0=mv[i][:, :, 0], scalar=-1.0, in1=rstd[i][:],
                                            op0=ALU.mult, op1=ALU.mult).then_inc(nb_done[i], 1)
                return fn

            pipelined(ve, NC, [(measure(4), 4), (measure(3), 3), (offset(4), 4), (measure(2), 2), (offset(3), 3),
                               (measure(1), 1), (offset(2), 2), (measure(0), 0), (offset(1), 1), (offset(0), 0)])


def model(nc, d, y):
    def scratch(name, shape, dt=F32):
        return nc.dram_tensor(name, list(shape), dt).ap()

    parts = scratch("qk_parts", (3, 2, B, 2, P, L), BF16)
    values = scratch("values", (B, QUADS, L, P))
    heads = scratch("heads", (B, QUADS, L, 4 * EA))
    x = [scratch(f"x{i}", (B, ROWS_B, D)) for i in range(5)]
    xs = scratch("xs", (B, L, D))
    kq = scratch("kq", (NC, P, 2 * HC, CH))
    rec = scratch("rec", (NS, P, REC))
    xk, xq, z1 = (scratch(s, (NS, P, D)) for s in ("xk", "xq", "z1"))
    ident = d["ident"]

    attn_project(nc, d["xT"], d["qkv_wT"], d["qkv_b_col"], d["v_b_row"], parts, values)
    attn_core(nc, parts, values, ident, heads)
    attn_close(nc, d["x"], heads, d["proj_wT"], d["proj_b_row"], ident, x[0])

    for i in range(2):
        window_attn(nc, f"wa{i}", x[2 * i], x[2 * i + 1], d["wqkv"][i], d["wo"][i], d["q_scale"][i:i + 1],
                    d["k_scale"][i:i + 1], d["rope"], d["masks"], d["masks0"], ident)
        gated_ffn(nc, f"gf{i}", x[2 * i + 1], x[2 * i + 2] if i == 0 else xs, d["w1"][i], d["b1_col"][i],
                  d["w2"][i], d["b2"][i:i + 1], d["ln_g_col"][i], d["ln_b_col"][i], ident,
                  None if i == 0 else x[0])

    ttt_project(nc, xs, d["down_w"], d["down_b_col"], d["wq"], d["wk"], d["wv"], d["ttt_w_row"], d["ttt_b_row"],
                d["lr_wT"], d["lr_b_row"], d["tok_idx_row"], d["inv_pos"], d["causal"], ident, kq, rec, xk, xq)
    ttt_scan(nc, kq, rec, xk, d["w_first"], d["b_first_row"], d["ttt_w_row"], d["tok_idx_row"], d["inv_pos"],
             d["same_seq"], ident, z1)
    ttt_close(nc, z1, xq, xs, d["ttt_w_row"], d["post_w_col"], d["post_b_col"], d["ttt_wo"], d["ln_w_col"],
              d["ln_b_col2"], d["up_w"], d["up_b_row"], d["w_lastT"], d["b_last_row"], d["v_rT"], d["c_T"], ident, y)


def shape_constants():
    f = np.float32
    half = np.arange(0, EB, 2, dtype=f)
    freqs = np.arange(L, dtype=f)[:, None] * (1.0 / f(10000.0) ** (half / f(EB))).astype(f)[None, :]
    freqs = np.concatenate([freqs, freqs], -1)
    base = ((half + f(0.4 * EB)) / f(1.4 * EB)).astype(f)
    power = ((np.arange(L, dtype=f) - L // 2) / f(WIN // 2)).astype(f)
    scale = (base[None] ** power[:, None]).astype(f)
    scale = np.concatenate([scale, scale], -1)
    sign = np.concatenate([-np.ones(EB // 2), np.ones(EB // 2)]).astype(f)
    cos, sin = np.cos(freqs), np.sin(freqs)
    rope = np.stack([cos * scale, sin * scale * sign, cos / scale, sin / scale * sign]).astype(f)
    i, j = np.arange(WIN)[:, None], np.arange(WIN)[None]
    before = np.where(j >= i, 0, MASKED)
    masks = np.concatenate([before, np.where(j <= i, 0, MASKED)], 1).astype(f)
    masks0 = np.stack([np.full((WIN, WIN), MASKED)] + [before] * (NW // 2 - 1)).astype(f)
    r = np.arange(P)
    same = r[:, None] // TM == r[None] // TM
    return dict(rope=rope, masks=masks, masks0=masks0, ident=np.eye(P, dtype=f), same_seq=same.astype(f),
                causal=(same & (r[:, None] <= r[None])).astype(f),
                inv_pos=(1.0 / np.arange(1, TM + 1, dtype=f)).reshape(1, TM).astype(f))


def laid_out(a):
    def columns(v):
        n = -(-v.size // P)
        out = np.zeros(n * P, v.dtype)
        out[:v.size] = v
        return out.reshape(n, P).T

    t = "L1_attn_"
    qkv_b, b1 = a["L0_attn_qkv_b"], a["L0_ffn_b1"]
    return dict(
        x=a["L0_attn_x"].reshape(B * L, D), xT=a["L0_attn_x"].reshape(B * L, D).T, qkv_wT=a["L0_attn_qkv_w"].T,
        qkv_b_col=columns(qkv_b[:2 * D]), v_b_row=qkv_b[2 * D:].reshape(1, D), proj_wT=a["L0_attn_proj_w"].T,
        proj_b_row=a["L0_attn_proj_b"].reshape(1, D),
        wqkv=a["L0_ffn_wqkv"], wo=a["L0_ffn_wo"], q_scale=a["L0_ffn_q_scale"], k_scale=a["L0_ffn_k_scale"],
        w1=a["L0_ffn_w1"], w2=a["L0_ffn_w2"], b2=a["L0_ffn_b2"],
        b1_col=np.stack([np.concatenate([columns(b[:HID]), columns(b[HID:])], 1) for b in b1]),
        ln_g_col=np.stack([columns(v) for v in a["L0_ffn_ln_g"]]),
        ln_b_col=np.stack([columns(v) for v in a["L0_ffn_ln_b"]]),
        down_w=a[t + "down_w"], down_b_col=columns(a[t + "down_b"]), wq=a[t + "wq"], wk=a[t + "wk"], wv=a[t + "wv"],
        ttt_w_row=a[t + "ttt_ln_w"].reshape(1, D), ttt_b_row=a[t + "ttt_ln_b"].reshape(1, D),
        lr_wT=a[t + "lr_w"].reshape(HC, D).T, lr_b_row=a[t + "lr_b"].reshape(1, HC),
        tok_idx_row=a[t + "tok_idx"].reshape(1, TM), w_first=a[t + "W1"], b_first_row=a[t + "b1"].reshape(1, D),
        post_w_col=columns(a[t + "post_w"]), post_b_col=columns(a[t + "post_b"]), ttt_wo=a[t + "wo"],
        ln_w_col=columns(a[t + "ln_w"]), ln_b_col2=columns(a[t + "ln_b"]), up_w=a[t + "up_w"],
        up_b_row=a[t + "up_b"].reshape(1, D), w_lastT=a["L1_ffn_W"].T, b_last_row=a["L1_ffn_b"].reshape(1, D),
        v_rT=a["L1_ffn_V_r"].T, c_T=a["L1_ffn_C"].T)


def kernel(**inputs):
    import concourse.bacc as _bacc
    from concourse.bass_utils import run_bass_kernel_spmd as _run

    arrays = laid_out({name: np.asarray(a) for name, a in inputs.items()})
    arrays.update(shape_constants())
    arrays = {name: np.ascontiguousarray(a) for name, a in arrays.items()}

    nc = _bacc.Bacc("TRN2", target_bir_lowering=False, num_devices=1)
    dram = {name: nc.dram_tensor(name, a.shape, mybir.dt.from_np(a.dtype), kind="ExternalInput").ap()
            for name, a in arrays.items()}
    y = nc.dram_tensor("y", [B, L, D], F32, kind="ExternalOutput").ap()
    model(nc, dram, y)
    return _run(nc, [arrays], core_ids=[0]).results[0]["y"]
```

```python
from contextlib import ExitStack

import numpy as np

import concourse.bass as bass
from concourse import mybir

F32 = mybir.dt.float32
BF16 = mybir.dt.bfloat16
ALU = mybir.AluOpType
ACT = mybir.ActivationFunctionType
AXX = mybir.AxisListType.X

P = 128
B, L, D = 8, 1024, 256
NT = B * L // P
CH = 512
NC = B * L // CH
TPC = CH // P
DC = D // P


class Stage:

    def __init__(self, nc, name):
        self.nc, self.name, self.stack, self.sems = nc, name, ExitStack(), []

    def __enter__(self):
        self.stack.__enter__()
        return self

    def __exit__(self, *what):
        left = self.stack.__exit__(*what)
        self.nc.clear_and_free_semaphores(self.sems)
        self.nc.all_engine_barrier()
        return left

    def sb(self, name, shape, dt=F32):
        return self.stack.enter_context(self.nc.sbuf_tensor(f"{self.name}_{name}", list(shape), dt))

    def ps(self, name, shape, dt=F32):
        return self.stack.enter_context(self.nc.psum_tensor(f"{self.name}_{name}", list(shape), dt))

    def sem(self, name):
        self.sems.append(self.nc.alloc_semaphore(f"{self.name}_{name}"))
        return self.sems[-1]

    def block(self):
        return self.stack.enter_context(self.nc.Block())


def pipelined(eng, n, steps, peel=0):
    deepest = max(lag for _, lag in steps)
    first = max(deepest + deepest % 2, 2)
    last = n - peel

    def peeled(s):
        for fn, lag in steps:
            t = s - lag
            if 0 <= t < n:
                fn(t, t // 2, t % 2)

    for s in range(min(first, last)):
        peeled(s)
    if last > first:
        with eng.Fori(0, (last - first) // 2) as i:
            for u in range(2):
                for fn, lag in steps:
                    off = first + u - lag
                    fn(i * 2 + off, i + off // 2, off % 2)
    for s in range(last, n + deepest):
        peeled(s)
HA, EA = 16, 16
QUADS = HA // 4
NI = B * QUADS
KT = L // P
Q_PART = [0, 0, 0, 1, 1, 2]
K_PART = [0, 1, 2, 0, 1, 0]
ROWS = EA * len(Q_PART)
SHIFT_ROWS = 3


def attn_project(nc, xT, wqkvT, qkv_b_col, vb_row, parts, values):
    with Stage(nc, "pj") as st:
        w = st.sb("w", [P, DC, 3 * D])
        bcol = st.sb("bcol", [P, 4])
        vb = st.sb("vb", [P, D])
        x = [st.sb(f"x{i}", [P, DC, CH]) for i in range(2)]
        full = st.sb("full", [P, 4, CH])
        rest = st.sb("rest", [P, 4, CH])
        split = [st.sb(f"split{i}", [P, 3, 4, CH], BF16) for i in range(2)]
        v = [st.sb(f"v{i}", [P, TPC, HA, 2 * EA]) for i in range(2)]
        pqk = [st.ps(f"pqk{m}", [P, CH]) for m in range(4)]
        pv = [st.ps(f"pv{j}", [P, 2, D]) for j in range(2)]
        w_in = st.sem("w_in")
        x_in = [st.sem(f"x_in{i}") for i in range(2)]
        x_free = st.sem("x_free")
        qk_mm = st.sem("qk_mm")
        v_mm = st.sem("v_mm")
        biased = st.sem("biased")
        part1 = st.sem("part1")
        dve = st.sem("dve")
        v_done = st.sem("v_done")
        ones_set = st.sem("ones_set")
        passed = st.sem("passed")
        stored = [st.sem(f"stored{i}") for i in range(2)]
        blk = st.block()

        @blk.sync
        def _(sp):
            sp.dma_start(w[:], wqkvT.rearrange("(c p) n -> p c n", p=P)).then_inc(w_in, 16)
            sp.dma_start(bcol[:], qkv_b_col).then_inc(w_in, 16)
            sp.dma_start(vb[:], vb_row.to_broadcast([P, D])).then_inc(w_in, 16)

            def load(t, k, p):
                sp.wait_ge(x_free, t + 1)
                sp.sem_inc(passed, 1)
                sp.dma_start(x[p][:], xT.rearrange("(c p) n -> p c n", p=P)[:, :, bass.ds(t * CH, CH)]
                             ).then_inc(x_in[p], 16)

            def store(t, k, p):
                sp.wait_ge(dve, t * 12 + 24)
                sp.wait_ge(part1, t * 4 + 8)
                sp.sem_inc(passed, 1)
                for j in range(3):
                    for which in range(2):
                        sp.dma_start(parts[j, which, k].rearrange("m r n -> r m n")[:, :, p * CH:(p + 1) * CH],
                                     split[p][:, j, 2 * which:2 * which + 2]).then_inc(stored[p], 16)
                sp.wait_ge(v_done, t * 2 + 4)
                sp.sem_inc(passed, 1)
                for g in range(QUADS):
                    sp.dma_start(values[k, g].rearrange("(j r) n -> r j n", r=P)[:, p * TPC:(p + 1) * TPC],
                                 v[p][:, :, 4 * g:4 * g + 4].rearrange("r j h e -> r j (h e)")
                                 ).then_inc(stored[p], 16)

            pipelined(sp, NC, [(load, 0), (store, 1)])
            for p in range(2):
                sp.wait_ge(stored[p], 160 * NC // 2 + 16)

        @blk.tensor
        def _(pe):
            pe.sem_inc(x_free, 2)
            pe.wait_ge(w_in, 48)

            def project(t, k, p):
                pe.wait_ge(x_in[p], k * 16 + 16)
                for m in range(4):
                    pe.wait_ge(biased, t * 4 + m + 1)
                    for c in range(DC):
                        mm = pe.matmul(pqk[m][:], w[:, c, m * P:(m + 1) * P], x[p][:, c],
                                       start=(c == 0), stop=(c == DC - 1))
                    mm.then_inc(qk_mm, 1)
                for j in range(2):
                    pe.wait_ge(v_done, t * 2 + j + 1)
                    for h in range(2):
                        for c in range(DC):
                            mm = pe.matmul(pv[j][:, h], x[p][:, c, (2 * j + h) * P:(2 * j + h + 1) * P],
                                           w[:, c, 2 * D:], start=(c == 0), stop=(c == DC - 1))
                    mm.then_inc(v_mm, 1)
                pe.wait_ge(v_mm, t * 2 + 2)
                pe.sem_inc(x_free, 1)

            pipelined(pe, NC, [(project, 0)])

        @blk.scalar
        def _(act):
            act.sem_inc(biased, 4)
            act.wait_ge(w_in, 48)

            def bias(t, k, p):
                for m in range(4):
                    act.wait_ge(qk_mm, t * 4 + m + 1)
                    act.wait_ge(dve, t * 12 + m * 3 + 1)
                    act.wait_ge(part1, t * 4 + m + 1)
                    act.activation(full[:, m], pqk[m][:], ACT.Identity, bias=bcol[:, m:m + 1]).then_inc(biased, 1)

            pipelined(act, NC, [(bias, 0)])

        @blk.gpsimd
        def _(pool):
            for p in range(2):
                pool.memset(v[p][:, :, :, EA:], 1.0).then_inc(ones_set, 1)
            pool.sem_inc(part1, 4)
            for p in range(2):
                pool.sem_inc(stored[p], 16)

            def first(t, k, p):
                pool.wait_ge(stored[p], k * 160 + 16)
                for m in range(4):
                    pool.wait_ge(biased, t * 4 + m + 5)
                    pool.sem_inc(passed, 1)
                    pool.tensor_copy(split[p][:, 0, m], full[:, m]).then_inc(part1, 1)

            pipelined(pool, NC, [(first, 0)])

        @blk.vector
        def _(dve_):
            dve_.sem_inc(dve, 12)
            dve_.sem_inc(v_done, 2)
            dve_.wait_ge(ones_set, 2)
            dve_.wait_ge(w_in, 48)

            def rest_parts(t, k, p):
                dve_.wait_ge(stored[p], k * 160 + 16)
                for m in range(4):
                    dve_.wait_ge(part1, t * 4 + m + 5)
                    dve_.tensor_tensor(rest[:, m], full[:, m], split[p][:, 0, m], ALU.subtract).then_inc(dve, 1)
                    dve_.wait_ge(dve, t * 12 + m * 3 + 13)
                    dve_.tensor_copy(split[p][:, 1, m], rest[:, m]).then_inc(dve, 1)
                    dve_.wait_ge(dve, t * 12 + m * 3 + 14)
                    dve_.tensor_tensor(split[p][:, 2, m], rest[:, m], split[p][:, 1, m], ALU.subtract
                                       ).then_inc(dve, 1)

            def value(t, k, p):
                for j in range(2):
                    dve_.wait_ge(v_mm, t * 2 + j + 1)
                    dve_.tensor_tensor(
                        v[p][:, 2 * j:2 * j + 2, :, 0:EA],
                        pv[j][:].rearrange("r a (h e) -> r a h e", h=HA),
                        vb[:].rearrange("r (a h e) -> r a h e", a=1, h=HA).to_broadcast([P, 2, HA, EA]),
                        ALU.add).then_inc(v_done, 1)

            pipelined(dve_, NC, [(rest_parts, 0), (value, 0)])


def attn_core(nc, parts, values, ident, heads_out):
    UNITS = 4 * KT * 2
    STEPS = 2 * KT * 2
    TURNS = STEPS // 2
    HALF = UNITS // 2
    TURN_SHIFT_AT = 20
    COPY_AT = (2, 18)
    TURN_AT = (3, 22)
    V_CREDIT = 2 * TURNS + 4
    K2 = ROWS + SHIFT_ROWS

    def unit(t, k, p, n):
        if n < HALF:
            return (t + 1, k + p, 1 - p, HALF + n) if not (isinstance(t, int) and t + 1 >= NI) else None
        return (t + 2, k + 1, p, n - HALF) if not (isinstance(t, int) and t + 2 >= NI) else None

    with Stage(nc, "co") as st:
        q1 = [st.sb(f"q1_{i}", [P, 4, L], BF16) for i in range(2)]
        k1 = [st.sb(f"k1_{i}", [P, 4, L], BF16) for i in range(2)]
        q2 = [st.sb(f"q2_{i}", [P, 4, L], BF16) for i in range(2)]
        k2 = [st.sb(f"k2_{i}", [P, 4, L], BF16) for i in range(2)]
        v = [st.sb(f"v{i}", [P, KT, P]) for i in range(2)]
        probs = [st.sb(f"probs{i}", [P, 4, CH]) for i in range(4)]
        half_max = st.sb("half_max", [P, 4 * KT, 2])
        neg_max = st.sb("neg_max", [P, 4 * KT])
        left = st.sb("left", [P, 4 * KT])
        shift = st.sb("shift", [P, SHIFT_ROWS, 4 * KT], BF16)
        shift_t = [st.sb(f"shift_t{i}", [SHIFT_ROWS * 4 * KT, P], BF16) for i in range(2)]
        idb = st.sb("idb", [P, P], BF16)
        idf = st.sb("idf", [P, P])
        o_sb = [st.sb(f"o_sb{i}", [P, CH]) for i in range(2)]
        recip = [st.sb(f"recip{i}", [P, TPC * 4]) for i in range(2)]
        o_n = [st.sb(f"o_n{i}", [P, TPC, 4 * EA]) for i in range(2)]
        row_ps = [st.ps(f"row_ps{i}", [P, CH]) for i in range(2)]
        col_ps = [st.ps(f"col_ps{i}", [P, 2, CH]) for i in range(2)]
        o_ps = st.ps("o_ps", [P, CH])
        misc = st.ps("misc", [P, CH])
        misc_bf = misc[0:SHIFT_ROWS * 4 * KT, 0:P // 2].bitcast(BF16)

        const_in = st.sem("const_in")
        idb_done = st.sem("idb_done")
        ones_set = st.sem("ones_set")
        in1 = [st.sem(f"in1_{i}") for i in range(2)]
        in2 = [st.sem(f"in2_{i}") for i in range(2)]
        shift_in = [st.sem(f"shift_in{i}") for i in range(2)]
        row_mm = st.sem("row_mm")
        maxed = st.sem("maxed")
        dve = st.sem("dve")
        shift_mm = st.sem("shift_mm")
        shift_ev = st.sem("shift_ev")
        col_mm = st.sem("col_mm")
        exped = st.sem("exped")
        v_mm = st.sem("v_mm")
        o_read = st.sem("o_read")
        turned = st.sem("turned")
        recip_done = st.sem("recip_done")
        normed = st.sem("normed")
        stored = [st.sem(f"stored{i}") for i in range(2)]
        passed = st.sem("passed")
        blk = st.block()

        @blk.sync
        def _(sp):
            sp.dma_start(idf[:], ident).then_inc(const_in, 16)

            def load_stack(dst, which, part_of, t, sem):
                for g, part in enumerate(part_of):
                    src = parts[part, which].rearrange("b m r n -> (b m r) n")[bass.ds(t * 4 * EA, 4 * EA), :]
                    sp.dma_start(dst[EA * g:EA * (g + 1)], src.rearrange("(h e) n -> e h n", e=EA)).then_inc(sem, 16)

            def load1(t, k, p):
                sp.wait_ge(row_mm, t * UNITS + UNITS)
                sp.sem_inc(passed, 1)
                load_stack(q1[p], 0, Q_PART, t, in1[p])
                load_stack(k1[p], 1, K_PART, t, in1[p])

            def load2(t, k, p):
                sp.wait_ge(v_mm, t * TURNS + V_CREDIT - TURNS)
                sp.sem_inc(passed, 1)
                load_stack(q2[p], 0, Q_PART, t, in2[p])
                load_stack(k2[p], 1, K_PART, t, in2[p])
                sp.dma_start(v[p][:], values.rearrange("b g n c -> (b g n) c")[bass.ds(t * L, L), :].rearrange("(a r) n -> r a n", r=P)
                             ).then_inc(in2[p], 16)

            def shift_rows(t, k, p):
                sp.wait_ge(v_mm, t * TURNS + V_CREDIT - TURNS)
                sp.wait_ge(shift_ev, t + 1)
                for j in range(SHIFT_ROWS):
                    sp.dma_start(q2[p][ROWS + j:ROWS + j + 1].rearrange("j h (q c) -> j (h q) c", c=P),
                                 shift_t[p][4 * KT * j:4 * KT * (j + 1)]).then_inc(shift_in[p], 16)

            def store(t, k, qc):
                sp.wait_ge(normed, t * 2 + qc + 3)
                sp.sem_inc(passed, 1)
                dst = heads_out.rearrange("b g n c -> (b g n) c")[bass.ds(t * L + qc * CH, CH), :]
                sp.dma_start(dst.rearrange("(a r) c -> r a c", r=P), o_n[qc][:]).then_inc(stored[qc], 16)

            def body(t, k, p):
                static = isinstance(t, int)
                if not (static and t + 2 >= NI):
                    load1(t + 2, k + 1, p)
                if not (static and t + 1 >= NI):
                    load2(t + 1, k + p, 1 - p)
                if not (static and t == 0):
                    store(t - 1, k, 1)
                if not (static and t + 1 >= NI):
                    shift_rows(t + 1, k + p, 1 - p)
                store(t, k, 0)

            load1(0, 0, 0)
            load1(1, 0, 1)
            load2(0, 0, 0)
            shift_rows(0, 0, 0)
            pipelined(sp, NI, [(body, 1)], peel=2)
            store(NI - 1, 0, 1)
            for qc in range(2):
                sp.wait_ge(stored[qc], 16 * NI + 16)

        @blk.tensor
        def _(pe):
            pe.sem_inc(row_mm, 2 * UNITS)
            pe.sem_inc(v_mm, V_CREDIT)
            pe.sem_inc(turned, 2)
            pe.wait_ge(const_in, 16)
            pe.wait_ge(idb_done, 1)
            pe.wait_ge(ones_set, 2)

            def row_scores(t, k, p, u):
                h, qt, half = u // (2 * KT), u // 2 % KT, u % 2
                if u == 0:
                    pe.wait_ge(in1[p], k * 192 + 192)
                pe.wait_ge(maxed, t * UNITS + u + 1)
                pe.matmul(row_ps[u % 2][:], q1[p][0:ROWS, h, qt * P:(qt + 1) * P],
                          k1[p][0:ROWS, h, half * CH:(half + 1) * CH], start=True, stop=True).then_inc(row_mm, 1)

            def turn_shift(t, k, p):
                pe.wait_ge(dve, t * 6 + 6)
                if not (isinstance(t, int) and t == 0):
                    pe.wait_ge(normed, t * 2)
                pe.transpose(misc_bf, shift[:].rearrange("r j x -> r (j x)"), idb[:]).then_inc(shift_mm, 1)

            def col_scores(t, k, p, s, j):
                qc, kt, pair = s // (2 * KT), s // 2 % KT, s % 2
                if s == 0 and j == 0:
                    pe.wait_ge(in2[p], k * 208 + 208)
                    pe.wait_ge(shift_in[p], k * 48 + 48)
                if j == 0:
                    pe.wait_ge(exped, t * STEPS + s + 1)
                h = 2 * pair + j
                mm = pe.matmul(col_ps[s % 2][:, j], k2[p][0:K2, h, kt * P:(kt + 1) * P],
                               q2[p][0:K2, h, qc * CH:(qc + 1) * CH], start=True, stop=True)
                if j == 1:
                    mm.then_inc(col_mm, 1)

            def times_v(t, k, p, m, half):
                qc, kt = m // KT, m % KT
                if half == 0:
                    if kt == 0:
                        pe.wait_ge(o_read, t * 2 + qc + 1)
                    pe.wait_ge(exped, t * STEPS + 2 * m + 4)
                for h in range(2 * half, 2 * half + 2):
                    mm = pe.matmul(o_ps[32 * h:32 * h + 32, :], v[p][:, kt, 32 * h:32 * h + 32],
                                   probs[m % 4][:, h], start=(kt == 0), stop=(kt == KT - 1))
                if half == 1:
                    mm.then_inc(v_mm, 1)

            def v_step(t, k, p, s):
                m, half = (s - 3) // 2, (s + 1) % 2
                if m >= 0:
                    times_v(t, k, p, m, half)
                elif not (isinstance(t, int) and t == 0):
                    times_v(t - 1, k + p - 1, 1 - p, TURNS + m, half)

            def turn_back(t, qc):
                pe.wait_ge(o_read, t * 2 + qc + 2)
                pe.wait_ge(normed, t * 2 + qc + 2)
                if not (isinstance(t, int) and t == NI - 1):
                    pe.wait_ge(shift_ev, t + 2)
                for a in range(TPC):
                    mm = pe.transpose(misc[:, a * P:(a + 1) * P], o_sb[qc][:, a * P:(a + 1) * P], idf[:])
                mm.then_inc(turned, 1)

            def body(t, k, p):
                first = isinstance(t, int) and t == 0
                last = isinstance(t, int) and t == NI - 1
                for s in range(STEPS):
                    for j in range(2):
                        col_scores(t, k, p, s, j)
                    for j in range(2):
                        ahead = unit(t, k, p, 2 * s + j)
                        if ahead:
                            row_scores(*ahead)
                        if j == 0:
                            v_step(t, k, p, s)
                    if s == TURN_AT[0] and not first:
                        turn_back(t - 1, 1)
                    if s == TURN_AT[1]:
                        turn_back(t, 0)
                    if s == TURN_SHIFT_AT and not last:
                        turn_shift(t + 1, k + p, 1 - p)

            for u in range(UNITS):
                row_scores(0, 0, 0, u)
            turn_shift(0, 0, 0)
            for u in range(HALF):
                row_scores(1, 0, 1, u)
            pipelined(pe, NI, [(body, 1)], peel=2)
            for m, half in ((TURNS - 2, 1), (TURNS - 1, 0), (TURNS - 1, 1)):
                times_v(NI - 1, 0, (NI - 1) % 2, m, half)
            turn_back(NI - 1, 1)

        @blk.scalar
        def _(act):
            act.sem_inc(exped, 2)

            def copy_shift(t, k, p):
                act.wait_ge(shift_mm, t + 1)
                if not (isinstance(t, int) and t < 2):
                    act.wait_ge(shift_in[p], k * 48)
                act.copy(shift_t[p][:], misc_bf).then_inc(shift_ev, 1)

            def exp(t, k, p, s):
                act.wait_ge(col_mm, t * STEPS + s + 1)
                act.wait_ge(v_mm, t * TURNS + s // 2 - 3 + V_CREDIT)
                act.activation(probs[s // 2 % 4][:, 2 * (s % 2):2 * (s % 2) + 2], col_ps[s % 2][:], ACT.Exp,
                               scale=float(EA) ** -0.5).then_inc(exped, 1)

            def body(t, k, p):
                last = isinstance(t, int) and t == NI - 1
                for s in range(STEPS):
                    exp(t, k, p, s)
                    if s == TURN_SHIFT_AT and not last:
                        copy_shift(t + 1, k + p, 1 - p)

            copy_shift(0, 0, 0)
            pipelined(act, NI, [(body, 1)], peel=2)

        @blk.gpsimd
        def _(pool):
            for p in range(2):
                pool.memset(k2[p][ROWS:K2], 1.0).then_inc(ones_set, 1)
                pool.sem_inc(stored[p], 16)

        @blk.vector
        def _(ve):
            ve.sem_inc(maxed, 2)
            ve.sem_inc(normed, 2)
            ve.sem_inc(o_read, 1)
            ve.wait_ge(const_in, 16)
            ve.tensor_copy(idb[:], idf[:]).then_inc(idb_done, 1)

            def row_max(t, u):
                ve.wait_ge(row_mm, t * UNITS + u + 1 + 2 * UNITS)
                if u == 0 and not (isinstance(t, int) and t == 0):
                    ve.wait_ge(dve, t * 6 - 5)
                ve.tensor_reduce(half_max[:, u // 2, u % 2:u % 2 + 1], row_ps[u % 2][:], AXX, ALU.max
                                 ).then_inc(maxed, 1)

            def split_max(t, op):
                if op == 0:
                    ve.wait_ge(maxed, t * UNITS + UNITS + 2)
                    if not (isinstance(t, int) and t == 0):
                        ve.wait_ge(shift_mm, t)
                    ve.tensor_reduce(neg_max[:], half_max[:], AXX, ALU.max, negate=True).then_inc(dve, 1)
                else:
                    ve.wait_ge(dve, t * 6 + op)
                if op == 1:
                    ve.tensor_copy(shift[:, 0], neg_max[:]).then_inc(dve, 1)
                elif op == 2:
                    ve.tensor_tensor(left[:], neg_max[:], shift[:, 0], ALU.subtract).then_inc(dve, 1)
                elif op == 3:
                    ve.tensor_copy(shift[:, 1], left[:]).then_inc(dve, 1)
                elif op == 4:
                    ve.tensor_tensor(neg_max[:], left[:], shift[:, 1], ALU.subtract).then_inc(dve, 1)
                elif op == 5:
                    ve.tensor_copy(shift[:, 2], neg_max[:]).then_inc(dve, 1)

            def copy_o(t, qc):
                ve.wait_ge(v_mm, t * TURNS + (qc + 1) * KT + V_CREDIT)
                ve.wait_ge(turned, t * 2 + qc + 1)
                ve.tensor_copy(o_sb[qc][:], o_ps[:]).then_inc(o_read, 1)

            def norm(t, qc):
                heads = misc[:].rearrange("r (x e) -> r x e", e=2 * EA)
                ve.wait_ge(turned, t * 2 + qc + 3)
                ve.reciprocal(recip[qc][:], heads[:, :, EA]).then_inc(recip_done, 1)
                ve.wait_ge(recip_done, t * 2 + qc + 1)
                ve.wait_ge(stored[qc], t * 16 + 16)
                ve.tensor_tensor(o_n[qc][:].rearrange("r a (h e) -> r (a h) e", e=EA), heads[:, :, 0:EA],
                                 recip[qc][:].rearrange("r (x e) -> r x e", e=1).to_broadcast([P, TPC * 4, EA]),
                                 ALU.mult).then_inc(normed, 1)

            def body(t, k, p):
                first = isinstance(t, int) and t == 0
                last = isinstance(t, int) and t == NI - 1
                after = [2 * (s + 1) for s in TURN_AT]
                for n in range(UNITS):
                    if n == 2 * COPY_AT[0] + 1 and not first:
                        copy_o(t - 1, 1)
                    if n == 2 * COPY_AT[1] + 1:
                        copy_o(t, 0)
                    if n == after[0] and not first:
                        norm(t - 1, 1)
                    if n == after[1]:
                        norm(t, 0)
                    if HALF <= n < HALF + 6 and not last:
                        split_max(t + 1, n - HALF)
                    ahead = unit(t, k, p, n)
                    if ahead:
                        row_max(ahead[0], ahead[3])

            for u in range(UNITS):
                row_max(0, u)
            for op in range(6):
                split_max(0, op)
            for u in range(HALF):
                row_max(1, u)
            pipelined(ve, NI, [(body, 1)], peel=2)
            copy_o(NI - 1, 1)
            norm(NI - 1, 1)


EPS = 1e-5


def attn_close(nc, x, heads, proj_wT, proj_b_row, ident, x1):
    with Stage(nc, "cl") as st:
        w = st.sb("w", [P, DC, D])
        bias = st.sb("bias", [P, D])
        idf = st.sb("idf", [P, P])
        zero = st.sb("zero", [B, D])
        power = st.sb("power", [P, TPC])
        h = [st.sb(f"h{i}", [P, TPC, D]) for i in range(2)]
        xr = [st.sb(f"xr{i}", [P, TPC, D]) for i in range(2)]
        xb = [st.sb(f"xb{i}", [P, TPC, D]) for i in range(2)]
        hT = [st.sb(f"hT{i}", [P, DC, CH]) for i in range(2)]
        res = [st.sb(f"res{i}", [P, TPC, D]) for i in range(2)]
        out = [st.sb(f"out{i}", [P, TPC, D]) for i in range(2)]
        stats = st.sb("stats", [P, TPC, 6])
        mv = [st.sb(f"mv{i}", [P, TPC, 2]) for i in range(2)]
        var = [st.sb(f"var{i}", [P, TPC]) for i in range(2)]
        rstd = [st.sb(f"rstd{i}", [P, TPC]) for i in range(2)]
        turn_ps = [[st.ps(f"turn{i}{c}", [P, CH]) for c in range(DC)] for i in range(2)]
        y_ps = [[st.ps(f"y{i}{j}", [P, 2, D]) for j in range(2)] for i in range(2)]

        const_in = st.sem("const_in")
        set_ = st.sem("set")
        h_in = [st.sem(f"h_in{i}") for i in range(2)]
        x_in = [st.sem(f"x_in{i}") for i in range(2)]
        turned = st.sem("turned")
        hT_done = st.sem("hT_done")
        y_mm = st.sem("y_mm")
        xb_done = st.sem("xb_done")
        added = st.sem("added")
        dve = st.sem("dve")
        rstd_done = st.sem("rstd_done")
        normed = st.sem("normed")
        stored = [st.sem(f"stored{i}") for i in range(2)]
        zeros_out = st.sem("zeros_out")
        passed = st.sem("passed")
        blk = st.block()
        xc = x.rearrange("(t a r) c -> t r a c", a=TPC, r=P)

        @blk.sync
        def _(sp):
            sp.dma_start(w[:], proj_wT.rearrange("(c p) n -> p c n", p=P)).then_inc(const_in, 16)
            sp.dma_start(bias[:], proj_b_row.to_broadcast([P, D])).then_inc(const_in, 16)
            sp.dma_start(idf[:], ident).then_inc(const_in, 16)
            sp.wait_ge(set_, 2)
            sp.dma_start(x1[:, 0], zero[:]).then_inc(zeros_out, 16)

            def load(t, k, p):
                sp.wait_ge(turned, t * DC + DC)
                sp.sem_inc(passed, 1)
                for g in range(QUADS):
                    src = heads[k, g].rearrange("(t a r) c -> t r a c", a=TPC, r=P)[p]
                    sp.dma_start(h[p][:, :, 4 * EA * g:4 * EA * (g + 1)], src).then_inc(h_in[p], 16)
                sp.wait_ge(xb_done, t + 1)
                sp.sem_inc(passed, 1)
                sp.dma_start(xr[p][:], xc[t]).then_inc(x_in[p], 16)

            def store(t, k, p):
                sp.wait_ge(normed, t * TPC + 3 * TPC)
                sp.sem_inc(passed, 1)
                sp.dma_start(x1[k, 1 + p * CH:1 + (p + 1) * CH].rearrange("(a r) c -> r a c", r=P), out[p][:]
                             ).then_inc(stored[p], 16)

            pipelined(sp, NC, [(load, 0), (store, 3)])
            sp.wait_ge(zeros_out, 16)
            for p in range(2):
                sp.wait_ge(stored[p], 16 * NC // 2 + 16)

        @blk.tensor
        def _(pe):
            pe.sem_inc(turned, 2 * DC)
            pe.sem_inc(y_mm, 4)
            pe.wait_ge(const_in, 48)

            def turn(t, k, p):
                pe.wait_ge(h_in[p], k * 64 + 64)
                for c in range(DC):
                    pe.wait_ge(hT_done, t * DC + c + 1)
                    for a in range(TPC):
                        mm = pe.transpose(turn_ps[p][c][:, a * P:(a + 1) * P], h[p][:, a, c * P:(c + 1) * P], idf[:])
                    mm.then_inc(turned, 1)

            def project(t, k, p):
                pe.wait_ge(hT_done, t * DC + 3 * DC)
                for j in range(2):
                    pe.wait_ge(added, t * 2 + j + 1)
                    for a in range(2):
                        for c in range(DC):
                            mm = pe.matmul(y_ps[p][j][:, a], hT[p][:, c, (2 * j + a) * P:(2 * j + a + 1) * P],
                                           w[:, c], start=(c == 0), stop=(c == DC - 1))
                    mm.then_inc(y_mm, 1)

            pipelined(pe, NC, [(turn, 0), (project, 1)])

        @blk.scalar
        def _(act):
            act.sem_inc(hT_done, 2 * DC)

            def copy_h(t, k, p):
                for c in range(DC):
                    act.wait_ge(turned, t * DC + c + 1 + 2 * DC)
                    act.wait_ge(y_mm, t * 2 + 2)
                    act.copy(hT[p][:, c], turn_ps[p][c][:]).then_inc(hT_done, 1)

            pipelined(act, NC, [(copy_h, 0)])

        @blk.gpsimd
        def _(pool):
            pool.sem_inc(xb_done, 2)
            for p in range(2):
                pool.sem_inc(stored[p], 16)
            pool.memset(zero[:], 0.0).then_inc(set_, 1)
            pool.memset(power[:], -0.5).then_inc(set_, 1)
            pool.wait_ge(set_, 2)
            pool.wait_ge(const_in, 48)

            def add_bias(t, k, p):
                pool.wait_ge(x_in[p], k * 16 + 16)
                pool.wait_ge(added, t * 2 + 2)
                pool.tensor_tensor(xb[p][:], xr[p][:], bias[:].rearrange("r (a c) -> r a c", a=1
                                   ).to_broadcast([P, TPC, D]), ALU.add).then_inc(xb_done, 1)

            def root(t, k, p):
                pool.wait_ge(dve, t * (2 * TPC + 1) + 2 * TPC + 1)
                pool.tensor_tensor(rstd[p][:], var[p][:], power[:], ALU.pow).then_inc(rstd_done, 1)

            pipelined(pool, NC, [(add_bias, 0), (root, 1)])

        @blk.vector
        def _(ve):
            ve.sem_inc(added, 4)
            ve.sem_inc(normed, 2 * TPC)

            def add(t, k, p):
                ve.wait_ge(normed, t * TPC + TPC)
                for j in range(2):
                    ve.wait_ge(y_mm, t * 2 + j + 5)
                    ve.wait_ge(xb_done, t + 3)
                    ve.tensor_tensor(res[p][:, 2 * j:2 * j + 2], y_ps[p][j][:], xb[p][:, 2 * j:2 * j + 2], ALU.add
                                     ).then_inc(added, 1)

            def moments(t, k, p):
                n = t * (2 * TPC + 1)
                for a in range(TPC):
                    ve.wait_ge(added, t * 2 + a // 2 + 5)
                    ve.bn_stats(stats[:, a], res[p][:, a]).then_inc(dve, 1)
                ve.wait_ge(dve, n + TPC)
                ve.sem_inc(passed, 1)
                for a in range(TPC):
                    ve.bn_aggr(mv[p][:, a], stats[:, a]).then_inc(dve, 1)
                ve.wait_ge(dve, n + 2 * TPC)
                ve.tensor_scalar(var[p][:], mv[p][:, :, 1], EPS, None, ALU.add).then_inc(dve, 1)

            def norm(t, k, p):
                ve.wait_ge(rstd_done, t + 1)
                ve.wait_ge(stored[p], k * 16 + 16)
                for a in range(TPC):
                    ve.tensor_scalar(out[p][:, a], res[p][:, a], mv[p][:, a, 0:1], rstd[p][:, a:a + 1],
                                     ALU.subtract, ALU.mult).then_inc(normed, 1)

            pipelined(ve, NC, [(add, 0), (moments, 0), (norm, 1)])


HB, EB = 8, 64
INNER = HB * EB
WIN = P
NW = L // WIN
PAIRS = HB // 2
QK_SCALE = 8.0
MASKED = -1e37
ROWS_B = 1 + L
ORDER = (1, 2, 3, 0)


def window_attn(nc, name, src, dst, wqkv, wo, q_scale, k_scale, rope, masks, masks0, ident):
    src_rows, dst_rows = src.rearrange("b n c -> (b n) c"), dst.rearrange("b n c -> (b n) c")
    with Stage(nc, name) as st:
        w = st.sb("w", [P, DC, 3 * INNER])
        w_out = st.sb("w_out", [P, PAIRS, D])
        idf = st.sb("idf", [P, P])
        tab = st.sb("tab", [P, NW, 4, EB])
        scales = st.sb("scales", [P, 4, EB])
        mask = [st.sb(f"mask{i}", [P, 2 * WIN]) for i in range(2)]
        zero = st.sb("zero", [B, D])
        power = st.sb("power", [P, HB])
        xf = [st.sb(f"xf{i}", [P, P]) for i in range(2)]
        xs = [st.sb(f"xs{i}", [P, P]) for i in range(2)]
        xr = [st.sb(f"xr{i}", [P, D]) for i in range(2)]
        hT = st.sb("hT", [P, DC, P])
        sq = st.sb("sq", [P, 2, INNER])
        ssq = st.sb("ssq", [P, 2, HB])
        inv = st.sb("inv", [P, 2, HB])
        by_cos = st.sb("by_cos", [P, 2, INNER])
        by_sin = st.sb("by_sin", [P, 2, INNER])
        turned = st.sb("turned", [P, 2, INNER])
        unit = st.sb("unit", [P, INNER])
        qT = st.sb("qT", [P, HB, P])
        kT = [st.sb(f"kT{i}", [P, PAIRS, WIN]) for i in range(2)]
        v = [st.sb(f"v{i}", [P, INNER]) for i in range(2)]
        sim = st.sb("sim", [P, HB, 2 * WIN])
        top = st.sb("top", [P, HB])
        shift = st.sb("shift", [P, HB])
        probs = st.sb("probs", [P, HB, 2 * WIN])
        total = st.sb("total", [P, HB])
        recip = st.sb("recip", [P, HB])
        on = st.sb("on", [P, INNER])
        pT = st.sb("pT", [P, PAIRS, CH])
        oT = st.sb("oT", [P, PAIRS, P])
        out = [st.sb(f"out{i}", [P, D]) for i in range(2)]
        t_ps = st.ps("t_ps", [P, DC, P])
        y_ps = t_ps
        qkv_ps = [st.ps(f"qkv_ps{i}", [P, INNER]) for i in range(3)]
        s_ps = [st.ps(f"s_ps{g}", [P, CH]) for g in range(PAIRS)]
        o_ps = s_ps[0]

        const_in, set_, tab_done = st.sem("const_in"), st.sem("set"), st.sem("tab_done")
        a_in = [st.sem(f"a_in{i}") for i in range(2)]
        r_in = [st.sem(f"r_in{i}") for i in range(2)]
        m_in = st.sem("m_in")
        xT_mm = st.sem("xT_mm")
        hT_done = st.sem("hT_done")
        qkv_mm = st.sem("qkv_mm")
        squared = st.sem("squared")
        summed = st.sem("summed")
        bounded = st.sem("bounded")
        inv_done = st.sem("inv_done")
        rope_mul = st.sem("rope_mul")
        rope_add = st.sem("rope_add")
        unit_done = st.sem("unit_done")
        qkT_mm = st.sem("qkT_mm")
        qT_done = st.sem("qT_done")
        kT_done = st.sem("kT_done")
        v_done = st.sem("v_done")
        s_mm = st.sem("s_mm")
        top_done = st.sem("top_done")
        shift_done = st.sem("shift_done")
        exped = st.sem("exped")
        recip_done = st.sem("recip_done")
        pT_mm = st.sem("pT_mm")
        pT_done = st.sem("pT_done")
        o_mm = st.sem("o_mm")
        on_done = st.sem("on_done")
        oT_mm = st.sem("oT_mm")
        oT_done = st.sem("oT_done")
        y_mm = st.sem("y_mm")
        y_done = st.sem("y_done")
        stored = [st.sem(f"stored{i}") for i in range(2)]
        zeros_out = st.sem("zeros_out")
        passed = st.sem("passed")
        blk = st.block()

        def static(t):
            return isinstance(t, int)

        @blk.sync
        def _(sp):
            for c in range(DC):
                sp.dma_start(w[:, c], wqkv[c * P:(c + 1) * P]).then_inc(const_in, 16)
            sp.dma_start(w_out[:], wo.rearrange("(g p) n -> p g n", p=P)).then_inc(const_in, 16)
            sp.dma_start(idf[:], ident).then_inc(const_in, 16)
            for f in range(4):
                sp.dma_start(tab[:, :, f], rope[f].rearrange("(w r) e -> r w e", r=P)).then_inc(const_in, 16)
            sp.dma_start(mask[0][:, WIN:], masks[:, WIN:]).then_inc(const_in, 16)
            sp.dma_start(mask[1][:], masks).then_inc(const_in, 16)
            for f, scale in enumerate((q_scale, k_scale)):
                sp.dma_start(scales[:, 2 * f], scale.to_broadcast([P, EB])).then_inc(const_in, 16)
                for h in range(2):
                    sp.dma_start(scales[:, 2 * f + 1, h * EB // 2:(h + 1) * EB // 2],
                                 scale[:, (1 - h) * EB // 2:(2 - h) * EB // 2].to_broadcast([P, EB // 2])
                                 ).then_inc(const_in, 16)
            sp.wait_ge(set_, 5)
            sp.dma_start(dst[:, 0], zero[:]).then_inc(zeros_out, 16)

            def load(t, k, p):
                sp.wait_ge(xT_mm, t + 1)
                sp.sem_inc(passed, 1)
                sp.dma_start(xf[p][:], src_rows[bass.ds(t * P + k // 4 + 1, P), 0:P]).then_inc(a_in[p], 16)
                sp.dma_start(xs[p][:], src_rows[bass.ds(t * P + k // 4, P), P:D]).then_inc(a_in[p], 16)

            def load_rest(t, k, p):
                sp.wait_ge(y_done, t + 1)
                sp.sem_inc(passed, 1)
                sp.dma_start(xr[p][:], src_rows[bass.ds(t * P + k // 4 + 1, P), :]).then_inc(r_in[p], 16)

            def load_mask(t, k, p):
                if p == 0:
                    sp.wait_ge(top_done, t * HB + HB)
                    sp.sem_inc(passed, 1)
                    sp.dma_start(mask[0][:, 0:WIN], masks0[k % 4]).then_inc(m_in, 16)

            def store(t, k, p):
                sp.wait_ge(y_done, t + 3)
                sp.sem_inc(passed, 1)
                sp.dma_start(dst_rows[bass.ds(t * P + k // 4 + 1, P), :], out[p][:]).then_inc(stored[p], 16)

            pipelined(sp, NT, [(load, 0), (load_mask, 0), (load_rest, 1), (store, 3)])
            sp.wait_ge(zeros_out, 16)
            for p in range(2):
                sp.wait_ge(stored[p], 16 * NT // 2 + 16)

        @blk.tensor
        def _(pe):
            pe.sem_inc(xT_mm, 2)
            pe.wait_ge(const_in, 16 * 16)
            pe.wait_ge(set_, 5)

            def turn_x(t, k, p):
                pe.wait_ge(a_in[p], k * 32 + 32)
                if not (static(t) and t < 3):
                    pe.wait_ge(y_done, t)
                for c, x in enumerate((xf[p], xs[p])):
                    mm = pe.transpose(t_ps[:, c], x[:], idf[:])
                mm.then_inc(xT_mm, 1)

            def qkv(t, k, p):
                pe.wait_ge(hT_done, t + 1)
                for i in (1, 0, 2):
                    if not (static(t) and t == 0):
                        if i == 0:
                            pe.wait_ge(qT_done, t * 2)
                        elif i == 1:
                            pe.wait_ge(kT_done, t)
                        else:
                            pe.wait_ge(v_done, t)
                    for c in range(DC):
                        mm = pe.matmul(qkv_ps[i][:], hT[:, c], w[:, c, i * INNER:(i + 1) * INNER],
                                       start=(c == 0), stop=(c == DC - 1))
                    mm.then_inc(qkv_mm, 1)

            def turn_qk(t, k, p):
                pe.wait_ge(unit_done, t + 1)
                for g in range(PAIRS):
                    mm = pe.transpose(qkv_ps[1][:, g * P:(g + 1) * P], unit[:, g * P:(g + 1) * P], idf[:])
                mm.then_inc(qkT_mm, 1)
                pe.wait_ge(rope_add, t * 2 + 2)
                pe.wait_ge(squared, t * 2 + 2)
                for g in range(PAIRS):
                    mm = pe.transpose(qkv_ps[0][:, g * P:(g + 1) * P], turned[:, 0, g * P:(g + 1) * P], idf[:])
                mm.then_inc(qkT_mm, 1)

            def scores(places):
                def fn(t, k, p):
                    pe.wait_ge(qT_done, t * 2 + 2)
                    pe.wait_ge(kT_done, t + 1)
                    for i in places:
                        g = ORDER[i]
                        if not (static(t) and t == 0):
                            if g == 0:
                                pe.wait_ge(oT_done, t)
                            else:
                                pe.wait_ge(pT_done, t * PAIRS + i + 1 - PAIRS)
                        for j in range(2):
                            for c, keys in enumerate((kT[1 - p], kT[p])):
                                mm = pe.matmul(s_ps[g][:, (2 * j + c) * P:(2 * j + c + 1) * P], qT[:, 2 * g + j],
                                               keys[:, g], start=True, stop=True)
                        mm.then_inc(s_mm, 1)
                return fn

            def turn_p(t, k, p):
                for i, g in enumerate(ORDER):
                    pe.wait_ge(exped, t * HB + 2 * i + 2)
                    pe.wait_ge(top_done, t * HB + 2 * i + 2 + 2 * HB)
                    for j in range(2):
                        for c in range(2):
                            mm = pe.transpose(s_ps[g][:, (2 * j + c) * P:(2 * j + c + 1) * P],
                                              probs[:, 2 * g + j, c * WIN:(c + 1) * WIN], idf[:])
                    mm.then_inc(pT_mm, 1)

            def times_v(t, k, p):
                pe.wait_ge(pT_done, t * PAIRS + PAIRS)
                pe.wait_ge(v_done, t + 1)
                for h in range(HB):
                    for c, values in enumerate((v[1 - p], v[p])):
                        mm = pe.matmul(o_ps[:, h * EB:(h + 1) * EB],
                                       pT[:, h // 2, (2 * (h % 2) + c) * P:(2 * (h % 2) + c + 1) * P],
                                       values[:, h * EB:(h + 1) * EB], start=(c == 0), stop=(c == 1))
                mm.then_inc(o_mm, 1)

            def turn_o(t, k, p):
                pe.wait_ge(on_done, t + 1)
                for g in range(PAIRS):
                    mm = pe.transpose(o_ps[:, g * P:(g + 1) * P], on[:, g * P:(g + 1) * P], idf[:])
                mm.then_inc(oT_mm, 1)

            def out_proj(t, k, p):
                pe.wait_ge(oT_done, t + 1)
                if not (static(t) and t >= NT - 2):
                    pe.wait_ge(hT_done, t + 3)
                elif t == NT - 1:
                    pe.wait_ge(y_done, t + 2)
                for g in range(PAIRS):
                    mm = pe.matmul(y_ps[:].rearrange("r c n -> r (c n)"), oT[:, g], w_out[:, g],
                                   start=(g == 0), stop=(g == PAIRS - 1))
                mm.then_inc(y_mm, 1)

            pipelined(pe, NT, [(turn_x, 0), (scores(range(0, 1)), 1), (turn_o, 2), (scores(range(1, PAIRS)), 1),
                               (out_proj, 2), (qkv, 0), (turn_p, 1), (turn_qk, 0), (times_v, 1)])

        @blk.scalar
        def _(act):
            def copy_x(t, k, p):
                act.wait_ge(xT_mm, t + 3)
                if not (static(t) and t == 0):
                    act.wait_ge(qkv_mm, t * 3)
                act.copy(hT[:], t_ps[:]).then_inc(hT_done, 1)

            def exps(t, k, p):
                if not (static(t) and t == 0):
                    act.wait_ge(pT_mm, t * PAIRS)
                    act.wait_ge(recip_done, t)
                for i, g in enumerate(ORDER):
                    act.wait_ge(shift_done, t * PAIRS + i + 1)
                    for h in (2 * g, 2 * g + 1):
                        act.activation(probs[:, h], sim[:, h], ACT.Exp, bias=shift[:, h:h + 1],
                                       scale=inv[:, 0, h:h + 1], accum_out=total[:, h:h + 1]).then_inc(exped, 1)

            def squares(t, k, p):
                for n, i in enumerate((1, 0)):
                    act.wait_ge(qkv_mm, t * 3 + n + 1)
                    if not (static(t) and t == 0):
                        act.wait_ge(summed, t * 2 + n - 1)
                    act.activation(sq[:, i], qkv_ps[i][:], ACT.Square).then_inc(squared, 1)

            def copy_p(t, k, p):
                if not (static(t) and t == 0):
                    act.wait_ge(o_mm, t)
                for i, g in enumerate(ORDER):
                    act.wait_ge(pT_mm, t * PAIRS + i + 1)
                    act.copy(pT[:, g], s_ps[g][:]).then_inc(pT_done, 1)

            def copy_o(t, k, p):
                act.wait_ge(oT_mm, t + 1)
                if not (static(t) and t == 0):
                    act.wait_ge(y_mm, t)
                act.copy(oT[:].rearrange("r g n -> r (g n)"), o_ps[:]).then_inc(oT_done, 1)

            def copy_v(t, k, p):
                act.wait_ge(qkv_mm, t * 3 + 3)
                if not (static(t) and t == 0):
                    act.wait_ge(o_mm, t)
                act.copy(v[p][:], qkv_ps[2][:]).then_inc(v_done, 1)

            def copy_q(t, k, p):
                act.wait_ge(qkT_mm, t * 2 + 2)
                if not (static(t) and t == 0):
                    act.wait_ge(s_mm, t * PAIRS)
                for j in range(2):
                    rows = slice(EB * j, EB * (j + 1))
                    act.copy(qT[rows, j:HB:2], qkv_ps[0][rows, :].rearrange("r (g n) -> r g n", g=PAIRS)
                             ).then_inc(qT_done, 1)

            act.wait_ge(set_, 5)
            pipelined(act, NT, [(copy_x, 0), (copy_o, 2), (exps, 1), (squares, 0), (copy_p, 1), (copy_q, 0),
                                (copy_v, 0)])

        @blk.gpsimd
        def _(pool):
            pool.memset(zero[:], 0.0).then_inc(set_, 1)
            pool.memset(power[:], -0.5).then_inc(set_, 1)
            pool.memset(kT[1][:], 0.0).then_inc(set_, 1)
            pool.memset(v[1][:], 0.0).then_inc(set_, 1)
            pool.memset(qT[:], 0.0).then_inc(set_, 1)
            for p in range(2):
                pool.sem_inc(stored[p], 16)
            pool.wait_ge(set_, 5)

            def lengths(t, k, p):
                pool.wait_ge(bounded, t * 2 + 1)
                pool.tensor_tensor(inv[:, 1], ssq[:, 1], power[:], ALU.pow).then_inc(inv_done, 1)
                pool.wait_ge(inv_done, t * 2 + 1)
                pool.wait_ge(rope_add, t * 2 + 1)
                if not (static(t) and t == 0):
                    pool.wait_ge(qkT_mm, t * 2 - 1)
                pool.tensor_tensor(unit[:].rearrange("r (h e) -> r h e", h=HB),
                                   turned[:, 1].rearrange("r (h e) -> r h e", h=HB),
                                   inv[:, 1].rearrange("r (h e) -> r h e", e=1).to_broadcast([P, HB, EB]),
                                   ALU.mult).then_inc(unit_done, 1)
                pool.wait_ge(bounded, t * 2 + 2)
                if not (static(t) and t == 0):
                    pool.wait_ge(exped, t * HB)
                pool.tensor_tensor(inv[:, 0], ssq[:, 0], power[:], ALU.pow).then_inc(inv_done, 1)

            pipelined(pool, NT, [(lengths, 0)])

        @blk.vector
        def _(ve):
            ve.sem_inc(top_done, 2 * HB)
            ve.sem_inc(y_done, 2)
            ve.wait_ge(const_in, 16 * 16)
            for f in range(4):
                ve.tensor_tensor(tab[:, :, f], tab[:, :, f], scales[:, f].rearrange("r (w e) -> r w e", w=1
                                 ).to_broadcast([P, NW, EB]), ALU.mult).then_inc(tab_done, 1)
            ve.wait_ge(tab_done, 4)
            ve.tensor_scalar(tab[:, :, 0:2], tab[:, :, 0:2], QK_SCALE, None, ALU.mult).then_inc(tab_done, 1)
            ve.wait_ge(tab_done, 5)

            def soften(t, k, p):
                if p == 0:
                    ve.wait_ge(m_in, k * 16 + 16)
                ve.wait_ge(inv_done, t * 2 + 2)
                if not (static(t) and t == 0):
                    ve.wait_ge(exped, t * HB)
                for i, g in enumerate(ORDER):
                    ve.wait_ge(s_mm, t * PAIRS + i + 1)
                    ve.sem_inc(passed, 1)
                    for j in range(2):
                        h = 2 * g + j
                        ve.tensor_tensor_reduce(out=sim[:, h], in0=s_ps[g][:, j * 2 * WIN:(j + 1) * 2 * WIN],
                                                in1=mask[p][:], scale=1.0, scalar=-3e38, op0=ALU.add, op1=ALU.max,
                                                accum_out=top[:, h:h + 1]).then_inc(top_done, 1)
                    ve.wait_ge(top_done, t * HB + 2 * i + 2 + 2 * HB)
                    ve.sem_inc(passed, 1)
                    ve.scalar_tensor_tensor(out=shift[:, 2 * g:2 * g + 2], in0=top[:, 2 * g:2 * g + 2], scalar=-1.0,
                                            in1=inv[:, 0, 2 * g:2 * g + 2], op0=ALU.mult, op1=ALU.mult
                                            ).then_inc(shift_done, 1)

            def invert(t, k, p):
                ve.wait_ge(exped, t * HB + HB)
                if not (static(t) and t == 0):
                    ve.wait_ge(on_done, t)
                ve.reciprocal(recip[:], total[:]).then_inc(recip_done, 1)

            def times_tables(n, i):
                def fn(t, k, p):
                    w_ = k % 4 * 2 + p
                    ve.wait_ge(qkv_mm, t * 3 + n + 1)
                    ve.wait_ge(squared, t * 2 + n + 1)
                    halves = qkv_ps[i][:].rearrange("r (h a e) -> r h a e", h=HB, a=2)
                    if not (static(t) and t == 0):
                        ve.wait_ge(rope_add, t * 2 + n - 1)
                    for j, x, dst_ in ((0, halves, by_cos), (1, halves[:, :, ::-1, :], by_sin)):
                        table = tab[:, bass.ds(w_, 1), 2 * i + j].rearrange("r w (a e) -> r w a e", a=2)
                        ve.tensor_tensor(dst_[:, i].rearrange("r (h a e) -> r h a e", h=HB, a=2), x,
                                         table.to_broadcast([P, HB, 2, EB // 2]), ALU.mult).then_inc(rope_mul, 1)
                return fn

            def lengths(n, i):
                def fn(t, k, p):
                    ve.wait_ge(squared, t * 2 + n + 1)
                    if not (static(t) and t == 0):
                        ve.wait_ge(inv_done, t * 2 + n - 1)
                    ve.tensor_reduce(ssq[:, i], sq[:, i].rearrange("r (h e) -> r h e", h=HB), AXX, ALU.add
                                     ).then_inc(summed, 1)
                    ve.wait_ge(summed, t * 2 + n + 1)
                    ve.tensor_scalar(ssq[:, i], ssq[:, i], 1e-24, None, ALU.max).then_inc(bounded, 1)
                return fn

            def rotate(n, i):
                def fn(t, k, p):
                    ve.wait_ge(rope_mul, t * 4 + 2 * n + 2)
                    if not (static(t) and t == 0):
                        if i == 1:
                            ve.wait_ge(unit_done, t)
                        else:
                            ve.wait_ge(qkT_mm, t * 2)
                    ve.tensor_tensor(turned[:, i], by_cos[:, i], by_sin[:, i], ALU.add).then_inc(rope_add, 1)
                return fn

            def normalise(t, k, p):
                ve.wait_ge(o_mm, t + 1)
                ve.wait_ge(recip_done, t + 1)
                if not (static(t) and t == 0):
                    ve.wait_ge(oT_mm, t)
                ve.tensor_tensor(on[:].rearrange("r (h e) -> r h e", h=HB), o_ps[:].rearrange("r (h e) -> r h e", h=HB),
                                 recip[:].rearrange("r (h e) -> r h e", e=1).to_broadcast([P, HB, EB]), ALU.mult
                                 ).then_inc(on_done, 1)

            def copy_k(t, k, p):
                ve.wait_ge(qkT_mm, t * 2 + 1)
                if not (static(t) and t == 0):
                    ve.wait_ge(s_mm, t * PAIRS)
                ve.tensor_copy(kT[p][:].rearrange("r g n -> r (g n)"), qkv_ps[1][:]).then_inc(kT_done, 1)

            def add(t, k, p):
                ve.wait_ge(y_mm, t + 1)
                ve.wait_ge(r_in[p], k * 16 + 16)
                ve.wait_ge(stored[p], k * 16 + 16)
                ve.tensor_tensor(out[p][:], y_ps[:].rearrange("r c n -> r (c n)"), xr[p][:], ALU.add).then_inc(y_done, 1)

            pipelined(ve, NT, [(soften, 1), (lengths(0, 1), 0), (times_tables(0, 1), 0), (rotate(0, 1), 0),
                               (times_tables(1, 0), 0), (rotate(1, 0), 0), (copy_k, 0), (lengths(1, 0), 0),
                               (invert, 1), (add, 2), (normalise, 1)])


HID = int(D * 4 * 2 / 3)
MT = -(-HID // P)
M_ROWS = [min(P, HID - m * P) for m in range(MT)]
AG = 2 * MT


def gated_ffn(nc, name, src, dst, w1, b1_col, w2, b2_row, ln_g_col, ln_b_col, ident, base=None):
    with Stage(nc, name) as st:
        w = st.sb("w", [P, DC, 2 * HID])
        wg = st.sb("wg", [P, DC, 2 * HID])
        v = st.sb("v", [P, MT, D])
        b1 = st.sb("b1", [P, AG])
        bias = st.sb("bias", [P, AG])
        b2 = st.sb("b2", [P, D])
        lg = st.sb("lg", [P, DC])
        lb = st.sb("lb", [P, DC])
        lb_wide = st.sb("lb_wide", [P, DC, 64])
        idf = st.sb("idf", [P, P])
        zero = st.sb("zero", [B, D])
        power = st.sb("power", [P, TPC])
        x = [st.sb(f"x{i}", [P, TPC, D]) for i in range(2)]
        xr = [st.sb(f"xr{i}", [P, TPC, D]) for i in range(2)]
        xb = [st.sb(f"xb{i}", [P, TPC, D]) for i in range(2)]
        xn = [st.sb(f"xn{i}", [P, TPC, D]) for i in range(2)]
        hT = [st.sb(f"hT{i}", [P, DC, CH]) for i in range(2)]
        ge = [st.sb(f"ge{i}", [P, CH]) for i in range(2)]
        hg = st.sb("hg", [P, MT, CH])
        out = [st.sb(f"out{i}", [P, TPC, D]) for i in range(2)]
        stats = st.sb("stats", [P, TPC, 6])
        mv = st.sb("mv", [P, TPC, 2])
        var = st.sb("var", [P, TPC])
        rstd = st.sb("rstd", [P, TPC])
        if base is not None:
            xbase = [st.sb(f"xbase{i}", [P, TPC, D]) for i in range(2)]
            xsum = st.sb("xsum", [P, TPC, D])
            res = [st.sb(f"res{i}", [P, TPC, D]) for i in range(2)]
            stats2 = st.sb("stats2", [P, TPC, 6])
            mv2 = [st.sb(f"mv2{i}", [P, TPC, 2]) for i in range(2)]
            var2 = [st.sb(f"var2{i}", [P, TPC]) for i in range(2)]
            rstd2 = [st.sb(f"rstd2{i}", [P, TPC]) for i in range(2)]
        turn_ps = [st.ps(f"turn{c}", [P, CH]) for c in range(DC)]
        a_ps = [st.ps(f"a_ps{i}", [P, CH]) for i in range(2)]
        g_ps = [st.ps(f"g_ps{i}", [P, CH]) for i in range(2)]
        y_ps = [st.ps(f"y_ps{j}", [P, 2, D]) for j in range(2)]

        const_in, set_, wg_done, lb_done = (st.sem(s) for s in ("const_in", "set", "wg_done", "lb_done"))
        bias_mm, bias_done = st.sem("bias_mm"), st.sem("bias_done")
        h_in = [st.sem(f"h_in{i}") for i in range(2)]
        x_in = [st.sem(f"x_in{i}") for i in range(2)]
        moments = st.sem("moments")
        rstd_done = st.sem("rstd_done")
        xn_done = st.sem("xn_done")
        turned = st.sem("turned")
        hT_done = st.sem("hT_done")
        ag_mm = st.sem("ag_mm")
        gelu_done = st.sem("gelu_done")
        gated = st.sem("gated")
        y_mm = st.sem("y_mm")
        xb_done = st.sem("xb_done")
        summed = st.sem("summed")
        added = st.sem("added")
        moments2 = st.sem("moments2")
        rstd2_done = st.sem("rstd2_done")
        normed = st.sem("normed")
        stored = [st.sem(f"stored{i}") for i in range(2)]
        zeros_out = st.sem("zeros_out")
        passed = st.sem("passed")
        blk = st.block()
        X_LOADS = 1 if base is None else 2

        @blk.sync
        def _(sp):
            sp.dma_start(w[:], w1.rearrange("(c p) n -> p c n", p=P)).then_inc(const_in, 16)
            sp.dma_start(b1[:], b1_col).then_inc(const_in, 16)
            sp.dma_start(b2[:], b2_row.to_broadcast([P, D])).then_inc(const_in, 16)
            sp.dma_start(lg[:], ln_g_col).then_inc(const_in, 16)
            sp.dma_start(lb[:], ln_b_col).then_inc(const_in, 16)
            sp.dma_start(idf[:], ident).then_inc(const_in, 16)
            sp.wait_ge(set_, 4)
            sp.dma_start(v[:, 0:MT - 1], w2[0:(MT - 1) * P].rearrange("(m p) n -> p m n", p=P)).then_inc(const_in, 16)
            sp.dma_start(v[0:M_ROWS[-1], MT - 1], w2[(MT - 1) * P:HID]).then_inc(const_in, 16)
            if base is None:
                sp.dma_start(dst[:, 0], zero[:]).then_inc(zeros_out, 16)

            def load(t, k, p):
                sp.wait_ge(xn_done, t * TPC + TPC)
                sp.sem_inc(passed, 1)
                for half in range(DC):
                    lo = 1 - half + p * CH
                    sp.dma_start(x[p][:, :, half * P:(half + 1) * P],
                                 src[k, lo:lo + CH, half * P:(half + 1) * P].rearrange("(a r) c -> r a c", r=P)
                                 ).then_inc(h_in[p], 16)
                sp.wait_ge(xb_done, t + 1)
                sp.sem_inc(passed, 1)
                rows = slice(1 + p * CH, 1 + (p + 1) * CH)
                sp.dma_start(xr[p][:], src[k, rows].rearrange("(a r) c -> r a c", r=P)).then_inc(x_in[p], 16)
                if base is not None:
                    sp.dma_start(xbase[p][:], base[k, rows].rearrange("(a r) c -> r a c", r=P)).then_inc(x_in[p], 16)

            def store(t, k, p):
                if base is None:
                    sp.wait_ge(added, t * 2 + 6)
                    place = dst[k, 1 + p * CH:1 + (p + 1) * CH]
                else:
                    sp.wait_ge(normed, t * TPC + 3 * TPC)
                    place = dst[k, p * CH:(p + 1) * CH]
                sp.sem_inc(passed, 1)
                sp.dma_start(place.rearrange("(a r) c -> r a c", r=P), out[p][:]).then_inc(stored[p], 16)

            pipelined(sp, NC, [(load, 0), (store, 3)])
            if base is None:
                sp.wait_ge(zeros_out, 16)
            for p in range(2):
                sp.wait_ge(stored[p], 16 * NC // 2 + 16)

        @blk.tensor
        def _(pe):
            pe.sem_inc(turned, 2 * DC)
            pe.sem_inc(ag_mm, 2 * AG)
            pe.sem_inc(y_mm, 2)
            pe.wait_ge(const_in, 16 * 8)
            pe.wait_ge(lb_done, 1)
            for i in range(AG):
                m, lo = i % MT, i // MT * HID + i % MT * P
                bank = a_ps[i % 2]
                if i > 1:
                    pe.wait_ge(bias_done, i - 1)
                for c in range(DC):
                    mm = pe.matmul(bank[0:M_ROWS[m], 0:64], w[:, c, lo:lo + M_ROWS[m]], lb_wide[:, c],
                                   start=(c == 0), stop=(c == DC - 1))
                mm.then_inc(bias_mm, 1)
            pe.wait_ge(bias_done, AG)
            pe.wait_ge(wg_done, DC)

            def turn(t, k, p):
                pe.wait_ge(xn_done, t * TPC + 3 * TPC)
                for c in range(DC):
                    pe.wait_ge(hT_done, t * DC + c + 1)
                    for a in range(TPC):
                        mm = pe.transpose(turn_ps[c][:, a * P:(a + 1) * P], xn[p][:, a, c * P:(c + 1) * P], idf[:])
                    mm.then_inc(turned, 1)

            def hidden(t, k, p):
                pe.wait_ge(hT_done, t * DC + 2 * DC)
                for m in range(MT):
                    pe.wait_ge(gated, t * MT + m + 1)
                    for bank, lo in ((g_ps[m % 2], HID + m * P), (a_ps[m % 2], m * P)):
                        for c in range(DC):
                            mm = pe.matmul(bank[0:M_ROWS[m], :], wg[:, c, lo:lo + M_ROWS[m]], hT[p][:, c],
                                           start=(c == 0), stop=(c == DC - 1))
                        mm.then_inc(ag_mm, 1)

            def project(t, k, p):
                pe.wait_ge(gated, t * MT + MT + 2)
                for j in range(2):
                    pe.wait_ge(added, t * 2 + j + 3)
                    for a in range(2):
                        for m in range(MT):
                            lo = (2 * j + a) * P
                            mm = pe.matmul(y_ps[j][:, a], hg[:, m, lo:lo + P], v[:, m],
                                           start=(m == 0), stop=(m == MT - 1))
                    mm.then_inc(y_mm, 1)

            pipelined(pe, NC, [(hidden, 1), (turn, 0), (project, 1)])

        @blk.scalar
        def _(act):
            act.sem_inc(hT_done, DC)
            act.wait_ge(bias_done, AG)

            def gelus(t, k, p):
                for m in range(MT):
                    act.wait_ge(ag_mm, t * AG + 2 * AG + 2 * m + 1)
                    act.wait_ge(gated, t * MT + m + 1)
                    act.activation(ge[m % 2][0:M_ROWS[m], :], g_ps[m % 2][0:M_ROWS[m], :], ACT.Gelu,
                                   bias=bias[0:M_ROWS[m], MT + m:MT + m + 1]).then_inc(gelu_done, 1)

            def copy_h(t, k, p):
                for c in range(DC):
                    act.wait_ge(turned, t * DC + c + 1 + 2 * DC)
                    act.wait_ge(ag_mm, t * AG + AG)
                    act.copy(hT[p][:, c], turn_ps[c][:]).then_inc(hT_done, 1)

            pipelined(act, NC, [(gelus, 1), (copy_h, 0)])

        @blk.gpsimd
        def _(pool):
            pool.sem_inc(xb_done, 2)
            for p in range(2):
                pool.sem_inc(stored[p], 16)
            pool.memset(zero[:], 0.0).then_inc(set_, 1)
            pool.memset(power[:], -0.5).then_inc(set_, 1)
            pool.memset(v[:, MT - 1], 0.0).then_inc(set_, 1)
            pool.memset(hg[:, MT - 1], 0.0).then_inc(set_, 1)
            pool.wait_ge(set_, 4)
            pool.wait_ge(const_in, 16 * 8)
            wide_b2 = b2[:].rearrange("r (a c) -> r a c", a=1).to_broadcast([P, TPC, D])

            def root(t, k, p):
                pool.wait_ge(moments, t * (2 * TPC + 1) + 2 * TPC + 1)
                if not (isinstance(t, int) and t == 0):
                    pool.wait_ge(xn_done, t * TPC + 2 * TPC)
                pool.tensor_tensor(rstd[:], var[:], power[:], ALU.pow).then_inc(rstd_done, 1)

            def add_bias(t, k, p):
                pool.wait_ge(x_in[p], k * 16 * X_LOADS + 16 * X_LOADS)
                pool.wait_ge(added, t * 2 + 2)
                if base is None:
                    pool.tensor_tensor(xb[p][:], xr[p][:], wide_b2, ALU.add).then_inc(xb_done, 1)
                else:
                    if not (isinstance(t, int) and t == 0):
                        pool.wait_ge(xb_done, t + 2)
                    pool.tensor_tensor(xsum[:], xr[p][:], wide_b2, ALU.add).then_inc(summed, 1)
                    pool.wait_ge(summed, t + 1)
                    pool.tensor_tensor(xb[p][:], xsum[:], xbase[p][:], ALU.add).then_inc(xb_done, 1)

            def root2(t, k, p):
                pool.wait_ge(moments2, t * (2 * TPC + 1) + 2 * TPC + 1)
                pool.tensor_tensor(rstd2[p][:], var2[p][:], power[:], ALU.pow).then_inc(rstd2_done, 1)

            pipelined(pool, NC, [(root, 0), (add_bias, 0)] + ([] if base is None else [(root2, 1)]))

        @blk.vector
        def _(ve):
            ve.sem_inc(xn_done, 2 * TPC)
            ve.sem_inc(gated, 2)
            ve.sem_inc(added, 4)
            ve.sem_inc(normed, 2 * TPC)
            ve.wait_ge(set_, 4)
            ve.wait_ge(const_in, 16 * 8)
            ve.tensor_copy(lb_wide[:], lb[:].rearrange("r (c o) -> r c o", o=1).to_broadcast([P, DC, 64])
                           ).then_inc(lb_done, 1)
            for c in range(DC):
                ve.tensor_scalar(wg[:, c], w[:, c], lg[:, c:c + 1], None, ALU.mult).then_inc(wg_done, 1)
            for i in range(AG):
                rows = slice(0, M_ROWS[i % MT])
                ve.wait_ge(bias_mm, i + 1)
                ve.tensor_tensor(bias[rows, i:i + 1], a_ps[i % 2][rows, 0:1], b1[rows, i:i + 1], ALU.add
                                 ).then_inc(bias_done, 1)
            ve.wait_ge(bias_done, AG)

            def measure(t, k, p):
                n = t * (2 * TPC + 1)
                ve.wait_ge(h_in[p], k * 32 + 32)
                for a in range(TPC):
                    ve.bn_stats(stats[:, a], x[p][:, a]).then_inc(moments, 1)
                ve.wait_ge(moments, n + TPC)
                ve.wait_ge(xn_done, t * TPC + 2 * TPC)
                ve.sem_inc(passed, 1)
                for a in range(TPC):
                    ve.bn_aggr(mv[:, a], stats[:, a]).then_inc(moments, 1)
                ve.wait_ge(moments, n + 2 * TPC)
                ve.tensor_scalar(var[:], mv[:, :, 1], EPS, None, ALU.add).then_inc(moments, 1)

            def normalise(t, k, p):
                ve.wait_ge(rstd_done, t + 1)
                ve.wait_ge(turned, t * DC + DC)
                for a in range(TPC):
                    ve.tensor_scalar(xn[p][:, a], x[p][:, a], mv[:, a, 0:1], rstd[:, a:a + 1],
                                     ALU.subtract, ALU.mult).then_inc(xn_done, 1)

            def gate(tiles):
                def fn(t, k, p):
                    ve.wait_ge(y_mm, t * 2 + 2)
                    for m in tiles:
                        rows = slice(0, M_ROWS[m])
                        ve.wait_ge(ag_mm, t * AG + 2 * AG + 2 * m + 2)
                        ve.wait_ge(gelu_done, t * MT + m + 1)
                        ve.scalar_tensor_tensor(out=hg[rows, m], in0=a_ps[m % 2][rows, :], scalar=bias[rows, m:m + 1],
                                                in1=ge[m % 2][rows, :], op0=ALU.add, op1=ALU.mult).then_inc(gated, 1)
                return fn

            def add(t, k, p):
                if base is None:
                    ve.wait_ge(stored[p], k * 16 + 16)
                else:
                    ve.wait_ge(normed, t * TPC + TPC)
                place = out[p] if base is None else res[p]
                for j in range(2):
                    ve.wait_ge(y_mm, t * 2 + j + 3)
                    ve.wait_ge(xb_done, t + 3)
                    ve.tensor_tensor(place[:, 2 * j:2 * j + 2], y_ps[j][:], xb[p][:, 2 * j:2 * j + 2], ALU.add
                                     ).then_inc(added, 1)

            def measure2(t, k, p):
                n = t * (2 * TPC + 1)
                for a in range(TPC):
                    ve.wait_ge(added, t * 2 + a // 2 + 5)
                    ve.bn_stats(stats2[:, a], res[p][:, a]).then_inc(moments2, 1)
                ve.wait_ge(moments2, n + TPC)
                ve.sem_inc(passed, 1)
                for a in range(TPC):
                    ve.bn_aggr(mv2[p][:, a], stats2[:, a]).then_inc(moments2, 1)
                ve.wait_ge(moments2, n + 2 * TPC)
                ve.tensor_scalar(var2[p][:], mv2[p][:, :, 1], EPS, None, ALU.add).then_inc(moments2, 1)

            def norm(t, k, p):
                ve.wait_ge(rstd2_done, t + 1)
                ve.wait_ge(stored[p], k * 16 + 16)
                for a in range(TPC):
                    ve.tensor_scalar(out[p][:, a], res[p][:, a], mv2[p][:, a, 0:1], rstd2[p][:, a:a + 1],
                                     ALU.subtract, ALU.mult).then_inc(normed, 1)

            steps = [(measure, 0), (gate(range(0, 3)), 1), (normalise, 0), (gate(range(3, MT)), 1), (add, 1)]
            if base is not None:
                steps = [(norm, 2)] + steps + [(measure2, 1)]
            pipelined(ve, NC, steps)


HC, EC = 2, D // 2
TM = 16
NS = L // TM
SQ = B // 4
REC = D + HC + HC * P


def step_rows(x, n):
    return x.rearrange("b (n t) c -> n b t c", t=TM)[n]


def ttt_project(nc, xs, down_w, down_b_col, wq, wk, wv, gain_row, shift_row, lr_wT, lr_b_row, tok_idx_row,
                inv_pos_row, causal, ident, kq, rec, xk, xq):
    with Stage(nc, "tp") as st:
        wd = st.sb("wd", [P, DC, D])
        wkq = st.sb("wkq", [P, DC, 2 * D])
        wvs = st.sb("wvs", [P, DC, D])
        wu = st.sb("wu", [P, DC, D + HC])
        db = st.sb("db", [P, DC])
        gain = st.sb("gain", [P, D])
        shift = st.sb("shift", [P, D])
        bias = st.sb("bias", [P, D + HC])
        idx = st.sb("idx", [P, TM])
        inv_pos = st.sb("inv_pos", [P, TM])
        last = st.sb("last", [P, 1])
        mask = st.sb("mask", [P, P])
        coef = st.sb("coef", [P, HC * P])
        idf = st.sb("idf", [P, P])
        x = [st.sb(f"x{i}", [P, TPC, D]) for i in range(2)]
        xT = st.sb("xT", [P, DC, CH])
        sg = st.sb("sg", [P, DC, CH])
        hT = [st.sb(f"hT{i}", [P, DC, CH]) for i in range(2)]
        kqT = [st.sb(f"kqT{i}", [P, 2 * HC, CH]) for i in range(2)]
        recs = [st.sb(f"recs{i}", [P, TPC, REC]) for i in range(2)]
        tk = [st.sb(f"tk{i}", [P, TPC, D]) for i in range(2)]
        tq = [st.sb(f"tq{i}", [P, TPC, D]) for i in range(2)]
        lr_raw = st.sb("lr_raw", [P, TPC, HC])
        lr_sg = st.sb("lr_sg", [P, TPC, HC])
        x_ps = [st.ps(f"x_ps{c}", [P, CH]) for c in range(DC)]
        m_ps = [st.ps(f"m_ps{i}", [P, CH]) for i in range(4)]
        g_ps = [st.ps(f"g_ps{i}", [P, 2, HC, P]) for i in range(2)]

        const_in, prep, wu_done = st.sem("const_in"), st.sem("prep"), st.sem("wu_done")
        x_in = [st.sem(f"x_in{i}") for i in range(2)]
        turned = st.sem("turned")
        xT_done = st.sem("xT_done")
        down_mm = st.sem("down_mm")
        sg_done = st.sem("sg_done")
        h_done = st.sem("h_done")
        kq_mm = st.sem("kq_mm")
        kq_done = st.sem("kq_done")
        gram_mm = st.sem("gram_mm")
        ct_done = st.sem("ct_done")
        u_mm = st.sem("u_mm")
        u_done = st.sem("u_done")
        lr_done = st.sem("lr_done")
        lr_sig = st.sem("lr_sig")
        lr_out = st.sem("lr_out")
        tok_mm = st.sem("tok_mm")
        tk_done = st.sem("tk_done")
        tq_done = st.sem("tq_done")
        stored = [st.sem(f"stored{i}") for i in range(2)]
        passed = st.sem("passed")
        blk = st.block()
        STORES = 4

        @blk.sync
        def _(sp):
            def halves(dst, w):
                return sp.dma_start(dst, w.rearrange("(c p) n -> p c n", p=P)).then_inc(const_in, 16)
            halves(wd[:], down_w)
            halves(wkq[:, :, 0:D], wk)
            halves(wkq[:, :, D:], wq)
            halves(wvs[:], wv)
            halves(wu[:, :, D:], lr_wT)
            for dst, row in ((gain[:], gain_row), (shift[:], shift_row), (bias[:, D:], lr_b_row),
                             (idx[:], tok_idx_row), (inv_pos[:], inv_pos_row)):
                sp.dma_start(dst, row.to_broadcast([P, row.shape[1]])).then_inc(const_in, 16)
            for dst, table in ((db, down_b_col), (mask, causal), (idf, ident)):
                sp.dma_start(dst[:], table).then_inc(const_in, 16)

            def load(t, k, p):
                sp.wait_ge(turned, t * DC + DC)
                sp.sem_inc(passed, 1)
                for a in range(TPC):
                    sp.dma_start(x[p][:, a], step_rows(xs, t * TPC + a)).then_inc(x_in[p], 16)

            def store(t, k, p):
                for done, count in ((kq_done, t * 4 + 4), (u_done, t * 4 + 4), (ct_done, t * 2 + 4),
                                    (lr_out, t + 2), (tk_done, t * 2 + 4), (tq_done, t * 2 + 4)):
                    sp.wait_ge(done, count)
                    sp.sem_inc(passed, 1)
                sp.dma_start(kq[t], kqT[p][:]).then_inc(stored[p], 16)
                for place, src in ((rec, recs), (xk, tk), (xq, tq)):
                    sp.dma_start(place.rearrange("(t a) r c -> t r a c", a=TPC)[t], src[p][:]).then_inc(stored[p], 16)

            pipelined(sp, NC, [(load, 0), (store, 3)])
            for p in range(2):
                sp.wait_ge(stored[p], 16 * STORES * (NC // 2 + 1))

        @blk.tensor
        def _(pe):
            pe.sem_inc(turned, 2 * DC)
            pe.sem_inc(down_mm, DC)
            pe.sem_inc(u_mm, 8)
            pe.sem_inc(tok_mm, 8)
            pe.wait_ge(const_in, 16 * 13)
            pe.wait_ge(wu_done, 2 * DC)

            def turn(t, k, p):
                pe.wait_ge(x_in[p], k * 64 + 64)
                for c in range(DC):
                    pe.wait_ge(h_done, t * DC + c + 1)
                    for a in range(TPC):
                        mm = pe.transpose(x_ps[c][:, a * P:(a + 1) * P], x[p][:, a, c * P:(c + 1) * P], idf[:])
                    mm.then_inc(turned, 1)

            def down(t, k, p):
                pe.wait_ge(xT_done, t * DC + DC)
                for m in range(DC):
                    for c in range(DC):
                        mm = pe.matmul(x_ps[m][:], wd[:, c, m * P:(m + 1) * P], xT[:, c],
                                       start=(c == 0), stop=(c == DC - 1))
                    mm.then_inc(down_mm, 1)

            def keys_queries(t, k, p):
                pe.wait_ge(h_done, t * DC + 2 * DC)
                for i in range(4):
                    if i < 2:
                        pe.wait_ge(tk_done, t * 2 + i + 1)
                    else:
                        pe.wait_ge(tq_done, t * 2 + i - 1)
                    for c in range(DC):
                        mm = pe.matmul(m_ps[i][:], wkq[:, c, i * P:(i + 1) * P], hT[p][:, c],
                                       start=(c == 0), stop=(c == DC - 1))
                    mm.then_inc(kq_mm, 1)

            def token_rows(t, k, p):
                for a in range(TPC):
                    pe.wait_ge(kq_done, t * 4 + a + 1)
                    for c in range(DC):
                        mm = pe.matmul(m_ps[a][:, 0:D + HC], hT[p][:, c, a * P:(a + 1) * P], wu[:, c],
                                       start=(c == 0), stop=(c == DC - 1))
                    mm.then_inc(u_mm, 1)

            def grams(t, k, p):
                for i in range(2):
                    pe.wait_ge(ct_done, t * 2 + i + 1)
                    for j in range(2):
                        for h in range(HC):
                            lo = (2 * i + j) * P
                            mm = pe.matmul(g_ps[i][:, j, h], kqT[p][:, h, lo:lo + P], kqT[p][:, HC + h, lo:lo + P],
                                           start=True, stop=True)
                    mm.then_inc(gram_mm, 1)

            def turn_back(t, k, p):
                for i in range(4):
                    which = i // 2
                    pe.wait_ge(u_done, t * 4 + i + 1)
                    pe.wait_ge(lr_done, t * 4 + i + 1)
                    for j in range(2):
                        for h in range(HC):
                            lo = (2 * (i % 2) + j) * P
                            mm = pe.transpose(m_ps[i][:, j * D + h * P:j * D + (h + 1) * P],
                                              kqT[p][:, HC * which + h, lo:lo + P], idf[:])
                    mm.then_inc(tok_mm, 1)

            pipelined(pe, NC, [(turn, 0), (keys_queries, 1), (down, 0), (token_rows, 1), (grams, 1), (turn_back, 1)])

        @blk.scalar
        def _(act):
            act.wait_ge(const_in, 16 * 13)

            def copy_x(t, k, p):
                for c in range(DC):
                    act.wait_ge(turned, t * DC + c + 1 + 2 * DC)
                    act.wait_ge(down_mm, t * DC + DC)
                    act.copy(xT[:, c], x_ps[c][:]).then_inc(xT_done, 1)

            def sigmoid(t, k, p):
                for m in range(DC):
                    act.wait_ge(down_mm, t * DC + DC + m + 1)
                    act.wait_ge(h_done, t * DC + m + 1)
                    act.activation(sg[:, m], x_ps[m][:], ACT.Sigmoid, bias=db[:, m:m + 1]).then_inc(sg_done, 1)

            def copy_kq(t, k, p):
                act.wait_ge(stored[p], (k + 1) * 16 * STORES)
                act.wait_ge(tok_mm, t * 4 + 4)
                for i in range(4):
                    act.wait_ge(kq_mm, t * 4 + i + 1)
                    act.copy(kqT[p][:, i], m_ps[i][:]).then_inc(kq_done, 1)

            def rates(t, k, p):
                act.wait_ge(lr_done, t * 4 + 4)
                act.wait_ge(lr_out, t + 1)
                act.activation(lr_sg[:], lr_raw[:], ACT.Sigmoid).then_inc(lr_sig, 1)

            pipelined(act, NC, [(copy_x, 0), (copy_kq, 1), (sigmoid, 0), (rates, 1)])

        @blk.vector
        def _(ve):
            ve.sem_inc(h_done, DC)
            ve.sem_inc(ct_done, 2)
            ve.sem_inc(lr_out, 1)
            ve.sem_inc(tk_done, 2)
            ve.sem_inc(tq_done, 2)
            for p in range(2):
                ve.sem_inc(stored[p], 16 * STORES)
            ve.wait_ge(const_in, 16 * 13)
            for c in range(DC):
                ve.tensor_tensor(wvs[:, c], wkq[:, c, 0:D], wvs[:, c], ALU.subtract).then_inc(wu_done, 1)
            ve.wait_ge(wu_done, DC)
            for c in range(DC):
                ve.tensor_tensor(wu[:, c, 0:D], wvs[:, c], gain[:], ALU.mult).then_inc(wu_done, 1)
            ve.tensor_tensor(bias[:, 0:D], shift[:], gain[:], ALU.mult).then_inc(prep, 1)
            ve.tensor_tensor(idx[:], idx[:], inv_pos[:], ALU.add).then_inc(prep, 1)
            ve.wait_ge(prep, 2)
            ve.tensor_scalar(idx[:], idx[:], 0.0, -1.0, ALU.max, ALU.mult).then_inc(prep, 1)
            ve.wait_ge(prep, 3)
            for h in range(HC):
                ve.tensor_tensor(coef[:, h * P:(h + 1) * P].rearrange("r (b i) -> r b i", b=B),
                                 mask[:].rearrange("r (b i) -> r b i", b=B),
                                 idx[:].rearrange("r (b i) -> r b i", b=1).to_broadcast([P, B, TM]), ALU.mult
                                 ).then_inc(prep, 1)
            ve.tensor_copy(last[:], idx[:, TM - 1:TM]).then_inc(prep, 1)
            ve.wait_ge(prep, 4 + HC)
            wide_coef = coef[:].rearrange("r (a n) -> r a n", a=1).to_broadcast([P, 2, HC * P])

            def gate(t, k, p):
                ve.wait_ge(u_mm, t * 4 + 4)
                for m in range(DC):
                    ve.wait_ge(sg_done, t * DC + m + 1)
                    ve.scalar_tensor_tensor(out=hT[p][:, m], in0=x_ps[m][:], scalar=db[:, m:m + 1], in1=sg[:, m],
                                            op0=ALU.add, op1=ALU.mult).then_inc(h_done, 1)

            def copy_u(t, k, p):
                ve.wait_ge(stored[p], (k + 1) * 16 * STORES)
                ve.wait_ge(lr_out, t + 1)
                for a in range(TPC):
                    ve.wait_ge(u_mm, t * 4 + a + 9)
                    ve.tensor_tensor(recs[p][:, a, 0:D], m_ps[a][:, 0:D], bias[:, 0:D], ALU.add).then_inc(u_done, 1)
                    ve.tensor_tensor(lr_raw[:, a], m_ps[a][:, D:D + HC], bias[:, D:], ALU.add).then_inc(lr_done, 1)

            def coefs(t, k, p):
                for i in range(2):
                    ve.wait_ge(gram_mm, t * 2 + i + 1)
                    ve.scalar_tensor_tensor(
                        out=recs[p][:, 2 * i:2 * i + 2, D + HC:],
                        in0=g_ps[i][:].rearrange("r a h n -> r a (h n)"), scalar=1.0, in1=wide_coef,
                        op0=ALU.add, op1=ALU.mult).then_inc(ct_done, 1)

            def copy_k(t, k, p):
                ve.wait_ge(lr_sig, t + 1)
                ve.tensor_scalar(recs[p][:, :, D:D + HC], lr_sg[:], 1.0 / EC, None, ALU.mult).then_inc(lr_out, 1)
                for i in range(2):
                    ve.wait_ge(tok_mm, t * 4 + i + 9)
                    ve.sem_inc(passed, 1)
                    ve.tensor_scalar(tk[p][:, 2 * i:2 * i + 2].rearrange("r a c -> r (a c)"), m_ps[i][:],
                                     last[:], None, ALU.mult).then_inc(tk_done, 1)

            def copy_q(t, k, p):
                for i in range(2):
                    ve.wait_ge(tok_mm, t * 4 + i + 11)
                    ve.tensor_tensor(tq[p][:, 2 * i:2 * i + 2], m_ps[2 + i][:].rearrange("r (a c) -> r a c", a=2),
                                     shift[:].rearrange("r (a c) -> r a c", a=1).to_broadcast([P, 2, D]), ALU.add
                                     ).then_inc(tq_done, 1)

            pipelined(ve, NC, [(gate, 0), (copy_u, 1), (coefs, 1), (copy_k, 1), (copy_q, 1)])


TTT_EPS = 1e-6
OPS = 11


def ttt_scan(nc, kq, rec, xk, w_first, b_first_row, gain_row, tok_idx_row, inv_pos_row, same_seq, ident, z1):
    with Stage(nc, "ts") as st:
        gain2 = st.sb("gain2", [P, HC, P])
        idx = st.sb("idx", [P, TM])
        inv_pos = st.sb("inv_pos", [P, TM])
        spread = st.sb("spread", [P, P])
        idf = st.sb("idf", [P, P])
        power = st.sb("power", [P, 1])
        kqc = [st.sb(f"kqc{i}", [P, 2 * HC, P]) for i in range(2)]
        kqp = [st.sb(f"kqp{i}", [P, 2 * HC * 4, 2 * 32]) for i in range(2)]
        rc = [st.sb(f"rc{i}", [P, REC]) for i in range(2)]
        xkm = [st.sb(f"xkm{i}", [P, B, D]) for i in range(2)]
        ws = [st.sb(f"ws{h}", [P, B, P]) for h in range(HC)]
        bs = [[st.sb(f"bs{i}{h}", [P, P]) for h in range(HC)] for i in range(2)]
        z, zc, g2, gy, junk, gw, grad = ([st.sb(f"{s}{h}", [P, P]) for h in range(HC)]
                                         for s in ("z", "zc", "g2", "gy", "junk", "gw", "grad"))
        stats = [st.sb(f"stats{h}", [P, 6]) for h in range(HC)]
        mv = [st.sb(f"mv{h}", [P, 2]) for h in range(HC)]
        var, rstd, s1, s2, rr, rate, mean1, q2 = (
            [st.sb(f"{s}{h}", [P, 1]) for h in range(HC)]
            for s in ("var", "rstd", "s1", "s2", "rr", "rate", "mean1", "q2"))
        out = [st.sb(f"out{i}", [P, HC, P]) for i in range(2)]
        w_ps = [[st.ps(f"w_ps{h}{i}", [P, CH]) for i in range(2)] for h in range(HC)]
        k_ps = [st.ps(f"k_ps{h}", [P, P]) for h in range(HC)]
        q_ps = [st.ps(f"q_ps{h}", [P, 2, P]) for h in range(HC)]

        const_in, set_, prep = st.sem("const_in"), st.sem("set"), st.sem("prep")
        kq_in = [st.sem(f"kq_in{i}") for i in range(2)]
        rec_in = [st.sem(f"rec_in{i}") for i in range(2)]
        xk_in = [st.sem(f"xk_in{i}") for i in range(2)]
        kq_spread = st.sem("kq_spread")
        z_mm = [st.sem(f"z_mm{h}") for h in range(HC)]
        d = [st.sem(f"d{h}") for h in range(HC)]
        rstd_done = [st.sem(f"rstd_done{h}") for h in range(HC)]
        w_mm = [st.sem(f"w_mm{h}") for h in range(HC)]
        w_done = [st.sem(f"w_done{h}") for h in range(HC)]
        zc_done = [st.sem(f"zc_done{h}") for h in range(HC)]
        rates_done = [st.sem(f"rates_done{h}") for h in range(HC)]
        b_done = [st.sem(f"b_done{h}") for h in range(HC)]
        c_mm = [st.sem(f"c_mm{h}") for h in range(HC)]
        z1_done = [st.sem(f"z1_done{h}") for h in range(HC)]
        stored = [st.sem(f"stored{i}") for i in range(2)]
        passed = st.sem("passed")
        blk = st.block()
        CONSTS = 16 * (HC * B + 7)

        @blk.sync
        def _(sp):
            for h in range(HC):
                for s in range(B):
                    sp.dma_start(ws[h][:, s], w_first[h]).then_inc(const_in, 16)
            sp.dma_start(gain2[:].rearrange("r h g -> r (h g)"), gain_row.to_broadcast([P, D])).then_inc(const_in, 16)
            for h in range(HC):
                sp.dma_start(bs[0][h][:], b_first_row[:, h * P:(h + 1) * P].to_broadcast([P, P])
                             ).then_inc(const_in, 16)
            for dst, r in ((idx[:], tok_idx_row), (inv_pos[:], inv_pos_row)):
                sp.dma_start(dst, r.to_broadcast([P, TM])).then_inc(const_in, 16)
            for dst, table in ((spread, same_seq), (idf, ident)):
                sp.dma_start(dst[:], table).then_inc(const_in, 16)
            sp.wait_ge(set_, 5)

            def load_kq(t, k, p):
                sp.wait_ge(kq_spread, t + 1)
                sp.sem_inc(passed, 1)
                sp.dma_start(kqc[p][:], kq[k // 2][:, :, bass.ds((k % 2) * 2 * P + p * P, P)]).then_inc(kq_in[p], 16)

            def load_rest(t, k, p):
                for h in range(HC):
                    sp.wait_ge(c_mm[h], t + 1)
                    sp.sem_inc(passed, 1)
                sp.dma_start(rc[p][:], rec[t]).then_inc(rec_in[p], 16)
                for s in range(B):
                    rows = slice(s * TM, (s + 1) * TM)
                    sp.dma_start(xkm[p][rows, s], xk[t, rows]).then_inc(xk_in[p], 16)

            def store(t, k, p):
                for h in range(HC):
                    sp.wait_ge(z1_done[h], t + 2)
                    sp.sem_inc(passed, 1)
                sp.dma_start(z1[t], out[p][:].rearrange("r h g -> r (h g)")).then_inc(stored[p], 16)

            pipelined(sp, NS, [(load_kq, 0), (store, 3), (load_rest, 0)])
            for p in range(2):
                sp.wait_ge(stored[p], 16 * NS // 2 + 16)

        @blk.tensor
        def _(pe):
            for h in range(HC):
                pe.sem_inc(c_mm[h], 2)
            pe.wait_ge(const_in, CONSTS)
            pe.wait_ge(prep, 4)

            def products(h, which, z_out, p):
                for half in range(SQ):
                    for q in range(4):
                        mm = pe.matmul(z_out[32 * q:32 * q + 32, :],
                                       kqp[p][:, (which * HC + h) * 4 + q, half * 32:half * 32 + 32],
                                       ws[h][:, SQ * q + half],
                                       start=(half == 0), stop=(which == 0 and half == SQ - 1))
                return mm

            def key_products(h):
                def fn(t, k, p):
                    pe.wait_ge(kq_spread, t + 3)
                    if not (isinstance(t, int) and t == 0):
                        pe.wait_ge(w_done[h], t * 2)
                        pe.wait_ge(d[h], t * OPS)
                    products(h, 0, k_ps[h][:], p).then_inc(z_mm[h], 1)
                return fn

            def query_products(h):
                def fn(t, k, p):
                    pe.wait_ge(z1_done[h], t + 1)
                    if not (isinstance(t, int) and t == 0):
                        pe.wait_ge(b_done[h], t)
                    products(h, 1, q_ps[h][:, 0], p)
                return fn

            def updates(h):
                def fn(t, k, p):
                    pe.wait_ge(xk_in[p], k * 16 * B + 16 * B)
                    pe.wait_ge(d[h], t * OPS + OPS)
                    for i in range(2):
                        for s in range(4):
                            mm = pe.matmul(w_ps[h][i][:, s * P:(s + 1) * P], xkm[p][:, 4 * i + s, h * P:(h + 1) * P],
                                           grad[h][:], start=True, stop=True)
                        mm.then_inc(w_mm[h], 1)
                    pe.matmul(q_ps[h][:, 0], rc[p][:, D + HC + h * P:D + HC + (h + 1) * P], grad[h][:],
                              start=False, stop=False)
                    pe.matmul(q_ps[h][:, 0], idf[:], bs[p][h][:], start=False, stop=True)
                    pe.matmul(q_ps[h][:, 1], spread[:], grad[h][:], start=True, stop=True).then_inc(c_mm[h], 1)
                return fn

            pipelined(pe, NS, [(key_products(0), 1), (updates(1), 2), (query_products(0), 1),
                               (key_products(1), 1), (updates(0), 1), (query_products(1), 1)])

        @blk.scalar
        def _(act):
            act.sem_inc(kq_spread, 2)
            for h in range(HC):
                act.sem_inc(z1_done[h], 1)
            act.wait_ge(set_, 5)

            def spread_kq(t, k, p):
                act.wait_ge(kq_in[p], k * 16 + 16)
                for h in range(HC):
                    if not (isinstance(t, int) and t < 2):
                        act.wait_ge(c_mm[h], t + 1)
                src = kqc[p][:].rearrange("r w (q a t) -> r (w q) a t", q=4, a=SQ)
                for a in range(SQ):
                    inst = act.copy(kqp[p][:, :, a * 48:a * 48 + TM], src[:, :, a])
                inst.then_inc(kq_spread, 1)

            def centre(h):
                def fn(t, k, p):
                    act.wait_ge(d[h], t * OPS + 3)
                    act.activation(zc[h][:], z[h][:], ACT.Identity, bias=mv[h][:, 0:1], scale=-1.0
                                   ).then_inc(zc_done[h], 1)
                return fn

            def result(h):
                def fn(t, k, p):
                    act.wait_ge(stored[p], k * 16 + 16)
                    act.wait_ge(c_mm[h], t + 3)
                    act.wait_ge(b_done[h], t + 1)
                    act.copy(out[p][:, h], q_ps[h][:, 0]).then_inc(z1_done[h], 1)
                return fn

            pipelined(act, NS, [(centre(0), 1), (result(1), 2), (spread_kq, 0), (centre(1), 1), (result(0), 1)])

        @blk.gpsimd
        def _(pool):
            for p in range(2):
                pool.sem_inc(stored[p], 16)
            pool.memset(power[:], -0.5).then_inc(set_, 1)
            for p in range(2):
                pool.memset(kqp[p][:], 0.0).then_inc(set_, 1)
                pool.memset(xkm[p][:], 0.0).then_inc(set_, 1)
            pool.wait_ge(set_, 5)

            def root(h):
                def fn(t, k, p):
                    pool.wait_ge(d[h], t * OPS + 4)
                    pool.tensor_tensor(rstd[h][:], var[h][:], power[:], ALU.pow).then_inc(rstd_done[h], 1)
                    pool.wait_ge(rec_in[p], k * 16 + 16)
                    pool.wait_ge(rstd_done[h], t + 1)
                    pool.tensor_tensor(rate[h][:], rstd[h][:], rc[p][:, D + h:D + h + 1], ALU.mult
                                       ).then_inc(rates_done[h], 1)
                    pool.tensor_tensor(rr[h][:], rstd[h][:], rstd[h][:], ALU.mult).then_inc(rates_done[h], 1)
                return fn

            pipelined(pool, NS, [(root(0), 1), (root(1), 1)])

        @blk.vector
        def _(ve):
            ve.wait_ge(const_in, CONSTS)
            ve.tensor_tensor(gain2[:], gain2[:], gain2[:], ALU.mult).then_inc(prep, 1)
            ve.tensor_tensor(idx[:], idx[:], inv_pos[:], ALU.add).then_inc(prep, 1)
            ve.wait_ge(prep, 2)
            ve.tensor_scalar(idx[:], idx[:], 0.0, -1.0, ALU.max, ALU.mult).then_inc(prep, 1)
            ve.wait_ge(prep, 3)
            ve.tensor_scalar(spread[:], spread[:], idx[:, TM - 1:TM], None, ALU.mult).then_inc(prep, 1)


            def normalise(h):
                def fn(t, k, p):
                    ve.wait_ge(z_mm[h], t + 1)
                    if not (isinstance(t, int) and t == 0):
                        ve.wait_ge(b_done[h], t)
                        ve.wait_ge(d[h], t * OPS)
                    ve.tensor_tensor(z[h][:], k_ps[h][:], bs[p][h][:], ALU.add).then_inc(d[h], 1)
                    ve.wait_ge(d[h], t * OPS + 1)
                    ve.bn_stats(stats[h][:], z[h][:]).then_inc(d[h], 1)
                    ve.wait_ge(d[h], t * OPS + 2)
                    ve.sem_inc(passed, 1)
                    ve.bn_aggr(mv[h][:], stats[h][:]).then_inc(d[h], 1)
                    ve.wait_ge(d[h], t * OPS + 3)
                    ve.tensor_scalar(var[h][:], mv[h][:, 1:2], TTT_EPS, None, ALU.add).then_inc(d[h], 1)
                    ve.scalar_tensor_tensor(out=g2[h][:], in0=z[h][:], scalar=mv[h][:, 0:1], in1=gain2[:, h],
                                            op0=ALU.subtract, op1=ALU.mult).then_inc(d[h], 1)
                return fn

            def sums(h):
                def fn(t, k, p):
                    ve.wait_ge(rstd_done[h], t + 1)
                    ve.wait_ge(rec_in[p], k * 16 + 16)
                    ve.wait_ge(d[h], t * OPS + 5)
                    ve.sem_inc(passed, 1)
                    ve.scalar_tensor_tensor(out=gy[h][:], in0=g2[h][:], scalar=rstd[h][:],
                                            in1=rc[p][:, h * P:(h + 1) * P], op0=ALU.mult, op1=ALU.add,
                                            accum_out=s1[h][:]).then_inc(d[h], 1)
                    ve.wait_ge(zc_done[h], t + 1)
                    ve.wait_ge(d[h], t * OPS + 6)
                    ve.sem_inc(passed, 1)
                    ve.tensor_tensor_reduce(out=junk[h][:], in0=gy[h][:], in1=zc[h][:], scale=-1.0 / EC, scalar=0.0,
                                            op0=ALU.mult, op1=ALU.add, accum_out=s2[h][:]).then_inc(d[h], 1)
                    ve.tensor_scalar(mean1[h][:], s1[h][:], 1.0 / EC, None, ALU.mult).then_inc(d[h], 1)
                return fn

            def gradient(h):
                def fn(t, k, p):
                    ve.wait_ge(rates_done[h], t * 2 + 2)
                    ve.wait_ge(d[h], t * OPS + 7)
                    ve.tensor_tensor(q2[h][:], s2[h][:], rr[h][:], ALU.mult).then_inc(d[h], 1)
                    ve.wait_ge(d[h], t * OPS + 9)
                    ve.scalar_tensor_tensor(out=gw[h][:], in0=zc[h][:], scalar=q2[h][:], in1=gy[h][:], op0=ALU.mult,
                                            op1=ALU.add).then_inc(d[h], 1)
                    ve.wait_ge(d[h], t * OPS + 10)
                    ve.tensor_scalar(grad[h][:], gw[h][:], mean1[h][:], rate[h][:], ALU.subtract, ALU.mult
                                     ).then_inc(d[h], 1)
                return fn

            def next_w(h, i):
                def fn(t, k, p):
                    ve.wait_ge(w_mm[h], t * 2 + i + 1)
                    part = ws[h][:, 4 * i:4 * i + 4].rearrange("r s g -> r (s g)")
                    ve.tensor_tensor(part, w_ps[h][i][:], part, ALU.add).then_inc(w_done[h], 1)
                return fn

            def next_b(h):
                def fn(t, k, p):
                    ve.wait_ge(c_mm[h], t + 3)
                    ve.tensor_tensor(bs[1 - p][h][:], q_ps[h][:, 1], bs[p][h][:], ALU.add).then_inc(b_done[h], 1)
                return fn

            ve.wait_ge(prep, 4)
            pipelined(ve, NS, [(normalise(0), 1), (next_w(1, 0), 2), (sums(0), 1), (next_w(1, 1), 2), (gradient(0), 1),
                               (next_b(1), 2), (normalise(1), 1), (next_w(0, 0), 1), (sums(1), 1), (next_w(0, 1), 1),
                               (gradient(1), 1), (next_b(0), 1)])


RANK = 32
GROUPS = [HC, 1, 1, 1, 1]
NORM_EPS = [TTT_EPS, EPS, EPS, EPS, EPS]
PROJ = (3, 2, 1)
NORM_LAG = [0, 1, 3, 5, 7]
PROJ_LAG = [None, 2, 4, 6]


def ttt_close(nc, z1, xq, xs, gain_row, post_w_col, post_b_col, wo, ln_w_col, ln_b_col, up_w, up_b_row,
              w_lastT, b_last_row, v_rT, c_T, ident, y):
    with Stage(nc, "tc") as st:
        w = [None] + [st.sb(f"w{i}", [P, DC, D]) for i in (1, 2, 3)]
        raw = [st.sb(f"raw{i}", [P, DC, D]) for i in range(2)]
        col = st.sb("col", [P, 4, DC])
        wide = st.sb("wide", [P, 2, DC, P])
        bias = [st.sb(f"bias{i}", [P, D]) for i in range(3)]
        gain = st.sb("gain", [P, D])
        vt = st.sb("vt", [P, D])
        ct = st.sb("ct", [P, D])
        idf = st.sb("idf", [P, P])
        power = st.sb("power", [P, TPC * HC])
        z_in_sb = [st.sb(f"z{i}", [P, TPC, D]) for i in range(2)]
        q_sb = [st.sb(f"q{i}", [P, TPC, D]) for i in range(2)]
        x_sb = [st.sb(f"x{i}", [P, TPC, D]) for i in range(2)]
        xb = st.sb("xb", [P, TPC, D])
        yb = st.sb("yb", [P, TPC, D])
        scaled = st.sb("scaled", [P, TPC, D])
        r = [None] + [st.sb(f"r{i}", [P, TPC, D]) for i in range(1, 5)]
        n = [st.sb(f"n{i}", [P, TPC, D]) for i in range(4)]
        out = [st.sb(f"out{i}", [P, TPC, D]) for i in range(2)]
        xT = [None] + [st.sb(f"xT{i}", [P, DC, CH]) for i in (1, 2, 3)]
        stats = [st.sb(f"stats{i}", [P, TPC * g, 6]) for i, g in enumerate(GROUPS)]
        mv = [st.sb(f"mv{i}", [P, TPC * g, 2]) for i, g in enumerate(GROUPS)]
        var, rstd, nb = ([st.sb(f"{s}{i}", [P, TPC * g]) for i, g in enumerate(GROUPS)] for s in ("var", "rstd", "nb"))
        turn_ps = [st.ps(f"turn{c}", [P, CH]) for c in range(DC)]
        y_ps = [None] + [[st.ps(f"y{i}{j}", [P, 2, D]) for j in range(2)] for i in (1, 2, 3)]

        const_in, set_, prep, bias_mm, bias_done = (
            st.sem(s) for s in ("const_in", "set", "prep", "bias_mm", "bias_done"))
        z_in, q_in, x_in, stored = ([st.sem(f"{s}{i}") for i in range(2)] for s in ("z_in", "q_in", "x_in", "stored"))
        G = [TPC * g for g in GROUPS]
        measured = [st.sem(f"measured{i}") for i in range(5)]
        rooted = [st.sem(f"rooted{i}") for i in range(5)]
        nb_done = [st.sem(f"nb_done{i}") for i in range(5)]
        normed = [st.sem(f"normed{i}") for i in range(5)]
        scaled_done = st.sem("scaled_done")
        summed = [None] + [st.sem(f"summed{i}") for i in range(1, 5)]
        xb_done = st.sem("xb_done")
        yb_done = st.sem("yb_done")
        turned = [None] + [st.sem(f"turned{i}") for i in (1, 2, 3)]
        copied = [None] + [st.sem(f"copied{i}") for i in (1, 2, 3)]
        y_mm = [None] + [st.sem(f"y_mm{i}") for i in (1, 2, 3)]
        passed = st.sem("passed")
        blk = st.block()
        CONSTS = 16 * 13

        def groups(tile_, i):
            return tile_[:].rearrange("r a (h c) -> r (a h) c", h=GROUPS[i])

        @blk.sync
        def _(sp):
            for dst, m in ((raw[0], wo), (raw[1], up_w), (w[3], w_lastT)):
                sp.dma_start(dst[:], m.rearrange("(c p) n -> p c n", p=P)).then_inc(const_in, 16)
            for i, c in enumerate((post_w_col, post_b_col, ln_w_col, ln_b_col)):
                sp.dma_start(col[:, i], c).then_inc(const_in, 16)
            for dst, row in ((bias[1], up_b_row), (bias[2], b_last_row), (gain, gain_row)):
                sp.dma_start(dst[:], row.to_broadcast([P, D])).then_inc(const_in, 16)
            sp.dma_start(idf[:], ident).then_inc(const_in, 16)
            sp.wait_ge(set_, 3)
            sp.dma_start(vt[0:RANK, :], v_rT).then_inc(const_in, 16)
            sp.dma_start(ct[0:RANK, :], c_T).then_inc(const_in, 16)

            def load_z(t, k, p):
                sp.wait_ge(normed[0], t * G[0] + G[0])
                sp.sem_inc(passed, 1)
                sp.dma_start(z_in_sb[p][:], z1.rearrange("(t a) r c -> t r a c", a=TPC)[t]).then_inc(z_in[p], 16)
                sp.wait_ge(summed[1], t * 2 + 2)
                sp.sem_inc(passed, 1)
                sp.dma_start(q_sb[p][:], xq.rearrange("(t a) r c -> t r a c", a=TPC)[t]).then_inc(q_in[p], 16)

            def load_x(t, k, p):
                sp.wait_ge(xb_done, t + 1)
                sp.sem_inc(passed, 1)
                for a in range(TPC):
                    sp.dma_start(x_sb[p][:, a], step_rows(xs, t * TPC + a)).then_inc(x_in[p], 16)

            def store(t, k, p):
                sp.wait_ge(normed[4], t * G[4] + 3 * G[4])
                sp.sem_inc(passed, 1)
                for a in range(TPC):
                    sp.dma_start(step_rows(y, t * TPC + a), out[p][:, a]).then_inc(stored[p], 16)

            pipelined(sp, NC, [(load_z, 0), (load_x, NORM_LAG[3] - 1), (store, NORM_LAG[4] + 1)])
            for p in range(2):
                sp.wait_ge(stored[p], 64 * NC // 2 + 64)

        @blk.tensor
        def _(pe):
            for i in PROJ:
                pe.sem_inc(turned[i], DC)
                pe.sem_inc(y_mm[i], 2)
            pe.wait_ge(const_in, CONSTS)
            pe.wait_ge(prep, 5)
            for i in range(2):
                for c in range(DC):
                    mm = pe.matmul(y_ps[1 + i][0][:, 0], wide[:, i, c], raw[i][:, c], start=(c == 0), stop=(c == DC - 1))
                mm.then_inc(bias_mm, 1)
            for c in range(DC):
                pe.matmul(y_ps[3][c][:, 0], vt[:, c * P:(c + 1) * P], ct[:], start=True, stop=True).then_inc(bias_mm, 1)
            pe.wait_ge(bias_done, 4)

            def turn(i):
                def fn(t, k, p):
                    s = t + PROJ_LAG[i]
                    if isinstance(t, int):
                        for j in PROJ:
                            chunk = min(s - PROJ_LAG[j] - (0 if j > i else 1), NC - 1)
                            if chunk >= 0:
                                pe.wait_ge(copied[j], chunk * DC + DC)
                    else:
                        j = i + 1 if i < 3 else 1
                        behind = PROJ_LAG[j] - PROJ_LAG[i] + (0 if j > i else 1)
                        pe.wait_ge(copied[j], t * DC + (1 - behind) * DC)
                    pe.wait_ge(normed[i], t * G[i] + 3 * G[i])
                    for c in range(DC):
                        for a in range(TPC):
                            mm = pe.transpose(turn_ps[c][:, a * P:(a + 1) * P], n[i][:, a, c * P:(c + 1) * P], idf[:])
                        mm.then_inc(turned[i], 1)
                return fn

            def product(i):
                def fn(t, k, p):
                    pe.wait_ge(copied[i], t * DC + DC)
                    for j in range(2):
                        pe.wait_ge(summed[i + 1], t * 2 + j + 3)
                        for a in range(2):
                            for c in range(DC):
                                lo = (2 * j + a) * P
                                mm = pe.matmul(y_ps[i][j][:, a], xT[i][:, c, lo:lo + P], w[i][:, c],
                                               start=(c == 0), stop=(c == DC - 1))
                        mm.then_inc(y_mm[i], 1)
                return fn

            pipelined(pe, NC, [(f(i), PROJ_LAG[i]) for f in (turn, product) for i in PROJ])

        @blk.scalar
        def _(act):
            for i in range(5):
                act.sem_inc(normed[i], 2 * G[i])

            def apply(i):
                def fn(t, k, p):
                    act.wait_ge(nb_done[i], t + 2)
                    if i == 0:
                        act.wait_ge(scaled_done, t + 1)
                    elif i == 4:
                        act.wait_ge(stored[p], k * 64 + 64)
                    else:
                        act.wait_ge(turned[i], t * DC + DC)
                    if i == 3:
                        act.wait_ge(yb_done, t + 1)
                    src, dst = (z_in_sb[p] if i == 0 else r[i]), (out[p] if i == 4 else n[i])
                    for g in range(G[i]):
                        act.activation(groups(dst, i)[:, g], groups(src, i)[:, g], ACT.Identity,
                                       bias=nb[i][:, g:g + 1], scale=rstd[i][:, g:g + 1]).then_inc(normed[i], 1)
                return fn

            def copy(i):
                def fn(t, k, p):
                    act.wait_ge(y_mm[i], t * 2 + 2)
                    for c in range(DC):
                        act.wait_ge(turned[i], t * DC + c + 1 + DC)
                        act.copy(xT[i][:, c], turn_ps[c][:]).then_inc(copied[i], 1)
                return fn

            pipelined(act, NC, [(copy(i), PROJ_LAG[i]) for i in PROJ]
                      + [(apply(i), NORM_LAG[i]) for i in (0, 4, 3, 2, 1)])

        @blk.gpsimd
        def _(pool):
            pool.sem_inc(xb_done, 2)
            pool.sem_inc(yb_done, 1)
            for p in range(2):
                pool.sem_inc(stored[p], 64)
            pool.memset(power[:], -0.5).then_inc(set_, 1)
            pool.memset(vt[:], 0.0).then_inc(set_, 1)
            pool.memset(ct[:], 0.0).then_inc(set_, 1)
            pool.wait_ge(set_, 3)
            pool.wait_ge(const_in, CONSTS)
            pool.wait_ge(bias_done, 4)

            def wide_row(tile_):
                return tile_[:].rearrange("r (a c) -> r a c", a=1).to_broadcast([P, TPC, D])

            def root(i):
                def fn(t, k, p):
                    pool.wait_ge(measured[i], t * (2 * G[i] + 1) + 2 * G[i] + 1)
                    pool.wait_ge(normed[i], t * G[i] + 2 * G[i])
                    pool.tensor_tensor(rstd[i][:], var[i][:], power[:, 0:G[i]], ALU.pow).then_inc(rooted[i], 1)
                return fn

            def residual(t, k, p):
                pool.wait_ge(x_in[p], k * 64 + 64)
                pool.wait_ge(summed[3], t * 2 + 4)
                pool.tensor_tensor(xb[:], x_sb[p][:], wide_row(bias[1]), ALU.add).then_inc(xb_done, 1)

            def residual_last(t, k, p):
                pool.wait_ge(normed[3], t * G[3] + 3 * G[3])
                pool.wait_ge(summed[4], t * 2 + 4)
                pool.tensor_tensor(yb[:], n[3][:], wide_row(bias[2]), ALU.add).then_inc(yb_done, 1)

            pipelined(pool, NC, [(root(0), 0), (root(4), NORM_LAG[4]), (residual_last, NORM_LAG[4] - 1),
                                 (root(3), NORM_LAG[3]), (residual, NORM_LAG[3] - 1), (root(2), NORM_LAG[2]),
                                 (root(1), NORM_LAG[1])])

        @blk.vector
        def _(ve):
            for i in range(5):
                ve.sem_inc(nb_done[i], 1)
            for i in range(1, 5):
                ve.sem_inc(summed[i], 4)
            ve.sem_inc(scaled_done, 1)
            ve.wait_ge(const_in, CONSTS)
            for i in range(2):
                for c in range(DC):
                    ve.tensor_scalar(w[1 + i][:, c], raw[i][:, c], col[:, 2 * i, c:c + 1], None, ALU.mult
                                     ).then_inc(prep, 1)
            ve.tensor_copy(wide[:], col[:, 1:4:2].rearrange("r i (c o) -> r i c o", o=1).to_broadcast([P, 2, DC, P])
                           ).then_inc(prep, 1)
            ve.wait_ge(bias_mm, 4)
            ve.tensor_copy(bias[0][:], y_ps[1][0][:, 0]).then_inc(bias_done, 1)
            ve.tensor_tensor(bias[1][:], y_ps[2][0][:, 0], bias[1][:], ALU.add).then_inc(bias_done, 1)
            for c in range(DC):
                ve.tensor_tensor(w[3][:, c], y_ps[3][c][:, 0], w[3][:, c], ALU.add).then_inc(bias_done, 1)
            ve.wait_ge(bias_done, 4)
            wide_gain = gain[:].rearrange("r (a c) -> r a c", a=1).to_broadcast([P, TPC, D])
            wide_bias = bias[0][:].rearrange("r (a c) -> r a c", a=1).to_broadcast([P, 2, D])

            def measure(i):
                def fn(t, k, p):
                    base = t * (2 * G[i] + 1)
                    if i == 0:
                        ve.wait_ge(z_in[p], k * 16 + 16)
                    elif i == 1:
                        ve.wait_ge(normed[0], t * G[0] + 3 * G[0])
                        ve.wait_ge(summed[1], t * 2 + 4)
                        ve.tensor_tensor(scaled[:], n[0][:], wide_gain, ALU.mult).then_inc(scaled_done, 1)
                        ve.wait_ge(scaled_done, t + 2)
                        ve.wait_ge(q_in[p], k * 16 + 16)
                    if i > 0:
                        ve.wait_ge(normed[i], t * G[i] + 2 * G[i])
                    if i == 3:
                        ve.wait_ge(xb_done, t + 3)
                    if i == 4:
                        ve.wait_ge(yb_done, t + 2)
                    if i > 0:
                        for j in range(2):
                            part = slice(2 * j, 2 * j + 2)
                            if i > 1:
                                ve.wait_ge(y_mm[i - 1], t * 2 + j + 3)
                            a = scaled[:, part] if i == 1 else y_ps[i - 1][j][:]
                            b = (q_sb[p][:, part], wide_bias, xb[:, part], yb[:, part])[i - 1]
                            ve.tensor_tensor(r[i][:, part], a, b, ALU.add).then_inc(summed[i], 1)
                    ve.wait_ge(nb_done[i], t + 1)
                    src = groups(z_in_sb[p] if i == 0 else r[i], i)
                    for g in range(G[i]):
                        if i > 0 and g % 2 == 0:
                            ve.wait_ge(summed[i], t * 2 + g // 2 + 5)
                        ve.bn_stats(stats[i][:, g], src[:, g]).then_inc(measured[i], 1)
                    ve.wait_ge(measured[i], base + G[i])
                    ve.sem_inc(passed, 1)
                    for g in range(G[i]):
                        ve.bn_aggr(mv[i][:, g], stats[i][:, g]).then_inc(measured[i], 1)
                    ve.wait_ge(measured[i], base + 2 * G[i])
                    ve.tensor_scalar(var[i][:], mv[i][:, :, 1], NORM_EPS[i], None, ALU.add).then_inc(measured[i], 1)
                return fn

            def offset(i):
                def fn(t, k, p):
                    ve.wait_ge(rooted[i], t + 1)
                    ve.wait_ge(normed[i], t * G[i] + 2 * G[i])
                    ve.sem_inc(passed, 1)
                    ve.scalar_tensor_tensor(out=nb[i][:], in0=mv[i][:, :, 0], scalar=-1.0, in1=rstd[i][:],
                                            op0=ALU.mult, op1=ALU.mult).then_inc(nb_done[i], 1)
                return fn

            order = [(measure, 0), (measure, 4), (offset, 0), (measure, 3), (offset, 4), (measure, 2), (offset, 3),
                     (measure, 1), (offset, 2), (offset, 1)]
            pipelined(ve, NC, [(f(i), NORM_LAG[i]) for f, i in order])


def model(nc, d, y):
    def scratch(name, shape, dt=F32):
        return nc.dram_tensor(name, list(shape), dt).ap()

    parts = scratch("qk_parts", (3, 2, B, 2, P, L), BF16)
    values = scratch("values", (B, QUADS, L, P))
    heads = scratch("heads", (B, QUADS, L, 4 * EA))
    x = [scratch(f"x{i}", (B, ROWS_B, D)) for i in range(5)]
    xs = scratch("xs", (B, L, D))
    kq = scratch("kq", (NC, P, 2 * HC, CH))
    rec = scratch("rec", (NS, P, REC))
    xk, xq, z1 = (scratch(s, (NS, P, D)) for s in ("xk", "xq", "z1"))
    ident = d["ident"]

    attn_project(nc, d["xT"], d["qkv_wT"], d["qkv_b_col"], d["v_b_row"], parts, values)
    attn_core(nc, parts, values, ident, heads)
    attn_close(nc, d["x"], heads, d["proj_wT"], d["proj_b_row"], ident, x[0])

    for i in range(2):
        window_attn(nc, f"wa{i}", x[2 * i], x[2 * i + 1], d["wqkv"][i], d["wo"][i], d["q_scale"][i:i + 1],
                    d["k_scale"][i:i + 1], d["rope"], d["masks"], d["masks0"], ident)
        gated_ffn(nc, f"gf{i}", x[2 * i + 1], x[2 * i + 2] if i == 0 else xs, d["w1"][i], d["b1_col"][i],
                  d["w2"][i], d["b2"][i:i + 1], d["ln_g_col"][i], d["ln_b_col"][i], ident,
                  None if i == 0 else x[0])

    ttt_project(nc, xs, d["down_w"], d["down_b_col"], d["wq"], d["wk"], d["wv"], d["ttt_w_row"], d["ttt_b_row"],
                d["lr_wT"], d["lr_b_row"], d["tok_idx_row"], d["inv_pos"], d["causal"], ident, kq, rec, xk, xq)
    ttt_scan(nc, kq, rec, xk, d["w_first"], d["b_first_row"], d["ttt_w_row"], d["tok_idx_row"], d["inv_pos"],
             d["same_seq"], ident, z1)
    ttt_close(nc, z1, xq, xs, d["ttt_w_row"], d["post_w_col"], d["post_b_col"], d["ttt_wo"], d["ln_w_col"],
              d["ln_b_col2"], d["up_w"], d["up_b_row"], d["w_lastT"], d["b_last_row"], d["v_rT"], d["c_T"], ident, y)


def shape_constants():
    f = np.float32
    half = np.arange(0, EB, 2, dtype=f)
    freqs = np.arange(L, dtype=f)[:, None] * (1.0 / f(10000.0) ** (half / f(EB))).astype(f)[None, :]
    freqs = np.concatenate([freqs, freqs], -1)
    base = ((half + f(0.4 * EB)) / f(1.4 * EB)).astype(f)
    power = ((np.arange(L, dtype=f) - L // 2) / f(WIN // 2)).astype(f)
    scale = (base[None] ** power[:, None]).astype(f)
    scale = np.concatenate([scale, scale], -1)
    sign = np.concatenate([-np.ones(EB // 2), np.ones(EB // 2)]).astype(f)
    cos, sin = np.cos(freqs), np.sin(freqs)
    rope = np.stack([cos * scale, sin * scale * sign, cos / scale, sin / scale * sign]).astype(f)
    i, j = np.arange(WIN)[:, None], np.arange(WIN)[None]
    before = np.where(j >= i, 0, MASKED)
    masks = np.concatenate([before, np.where(j <= i, 0, MASKED)], 1).astype(f)
    masks0 = np.stack([np.full((WIN, WIN), MASKED)] + [before] * (NW // 2 - 1)).astype(f)
    r = np.arange(P)
    same = r[:, None] // TM == r[None] // TM
    return dict(rope=rope, masks=masks, masks0=masks0, ident=np.eye(P, dtype=f), same_seq=same.astype(f),
                causal=(same & (r[:, None] <= r[None])).astype(f),
                inv_pos=(1.0 / np.arange(1, TM + 1, dtype=f)).reshape(1, TM).astype(f))


def laid_out(a):
    def columns(v):
        n = -(-v.size // P)
        out = np.zeros(n * P, v.dtype)
        out[:v.size] = v
        return out.reshape(n, P).T

    t = "L1_attn_"
    qkv_b, b1 = a["L0_attn_qkv_b"], a["L0_ffn_b1"]
    return dict(
        x=a["L0_attn_x"].reshape(B * L, D), xT=a["L0_attn_x"].reshape(B * L, D).T, qkv_wT=a["L0_attn_qkv_w"].T,
        qkv_b_col=columns(qkv_b[:2 * D]), v_b_row=qkv_b[2 * D:].reshape(1, D), proj_wT=a["L0_attn_proj_w"].T,
        proj_b_row=a["L0_attn_proj_b"].reshape(1, D),
        wqkv=a["L0_ffn_wqkv"], wo=a["L0_ffn_wo"], q_scale=a["L0_ffn_q_scale"], k_scale=a["L0_ffn_k_scale"],
        w1=a["L0_ffn_w1"], w2=a["L0_ffn_w2"], b2=a["L0_ffn_b2"],
        b1_col=np.stack([np.concatenate([columns(b[:HID]), columns(b[HID:])], 1) for b in b1]),
        ln_g_col=np.stack([columns(v) for v in a["L0_ffn_ln_g"]]),
        ln_b_col=np.stack([columns(v) for v in a["L0_ffn_ln_b"]]),
        down_w=a[t + "down_w"], down_b_col=columns(a[t + "down_b"]), wq=a[t + "wq"], wk=a[t + "wk"], wv=a[t + "wv"],
        ttt_w_row=a[t + "ttt_ln_w"].reshape(1, D), ttt_b_row=a[t + "ttt_ln_b"].reshape(1, D),
        lr_wT=a[t + "lr_w"].reshape(HC, D).T, lr_b_row=a[t + "lr_b"].reshape(1, HC),
        tok_idx_row=a[t + "tok_idx"].reshape(1, TM), w_first=a[t + "W1"], b_first_row=a[t + "b1"].reshape(1, D),
        post_w_col=columns(a[t + "post_w"]), post_b_col=columns(a[t + "post_b"]), ttt_wo=a[t + "wo"],
        ln_w_col=columns(a[t + "ln_w"]), ln_b_col2=columns(a[t + "ln_b"]), up_w=a[t + "up_w"],
        up_b_row=a[t + "up_b"].reshape(1, D), w_lastT=a["L1_ffn_W"].T, b_last_row=a["L1_ffn_b"].reshape(1, D),
        v_rT=a["L1_ffn_V_r"].T, c_T=a["L1_ffn_C"].T)


def kernel(**inputs):
    import concourse.bacc as _bacc
    from concourse.bass_utils import run_bass_kernel_spmd as _run

    arrays = laid_out({name: np.asarray(a) for name, a in inputs.items()})
    arrays.update(shape_constants())
    arrays = {name: np.ascontiguousarray(a) for name, a in arrays.items()}

    nc = _bacc.Bacc("TRN2", target_bir_lowering=False, num_devices=1)
    dram = {name: nc.dram_tensor(name, a.shape, mybir.dt.from_np(a.dtype), kind="ExternalInput").ap()
            for name, a in arrays.items()}
    y = nc.dram_tensor("y", [B, L, D], F32, kind="ExternalOutput").ap()
    model(nc, dram, y)
    return _run(nc, [arrays], core_ids=[0]).results[0]["y"]
```
